# Optimizing a Trainium2 kernel written in Bass

```python
import numpy as np
import jax
import jax.numpy as jnp

def _softmax(x, axis=-1):
    return jax.nn.softmax(x, axis=axis)

def _gelu(x):
    return jax.nn.gelu(x, approximate=True)

def _silu(x):
    return jax.nn.silu(x)

def _sigmoid(x):
    return jax.nn.sigmoid(x)

def _layernorm(x, axis=-1, eps=1e-05):
    m = jnp.mean(x, axis=axis, keepdims=True)
    v = jnp.var(x, axis=axis, keepdims=True)
    return (x - m) / jnp.sqrt(v + eps)

def _scatter_add(tgt, idx, src, axis=0):
    return tgt.at[idx].add(src)

def _segment_sum(src, seg, n):
    return jax.ops.segment_sum(src, seg, n)
kernel_name = 'mk_sandwich_d1_jaxref_r4_3758f4'

def setup_inputs(seed: int=0):
    np.random.seed(seed)
    _w = jnp.asarray

    def _L0_attn_setup():
        import jax, jax.numpy as jnp
        import numpy as np
        H_HEADS = 16
        SEG = 64
        EPS = 1e-06
        key = jax.random.key(seed)
        ks = jax.random.split(key, 6)
        B, T, D = (2, 1024, 256)
        sc = 1.0 / np.sqrt(D)
        return {'x': jax.random.normal(ks[0], (B, T, D), jnp.float32), 'norm_w': jnp.ones((D,), jnp.float32), 'Wq': jax.random.normal(ks[1], (D, D), jnp.float32) * sc, 'Wk': jax.random.normal(ks[2], (D, D), jnp.float32) * sc, 'Wv': jax.random.normal(ks[3], (D, D), jnp.float32) * sc, 'Wo': jax.random.normal(ks[4], (D, D), jnp.float32) * sc, 'Wu': jax.random.normal(ks[5], (D, D), jnp.float32) * sc}
    _L0_attn_in = _L0_attn_setup()

    def _L0_ffn_setup():
        import jax, jax.numpy as jnp
        import numpy as np
        H = 256
        I = 256
        E = 16
        K = 4
        LIMIT = 7.0
        ALPHA = 1.702
        EPS = 1e-05
        key = jax.random.key(seed)
        ks = jax.random.split(key, 8)
        x = jax.random.normal(ks[0], (2, 128, H), dtype=jnp.float32)
        norm_scale = jnp.ones((H,), dtype=jnp.float32)
        wg = jax.random.normal(ks[1], (H, E), dtype=jnp.float32) * 0.02
        bg = jax.random.normal(ks[2], (E,), dtype=jnp.float32) * 0.02
        w1 = jax.random.normal(ks[3], (E, H, 2 * I), dtype=jnp.float32) * 0.02
        b1 = jax.random.normal(ks[4], (E, 2 * I), dtype=jnp.float32) * 0.02
        w2 = jax.random.normal(ks[5], (E, I, H), dtype=jnp.float32) * 0.02
        b2 = jax.random.normal(ks[6], (E, H), dtype=jnp.float32) * 0.02
        return {'x': x, 'norm_scale': norm_scale, 'wg': wg, 'bg': bg, 'w1': w1, 'b1': b1, 'w2': w2, 'b2': b2}
    _L0_ffn_in = _L0_ffn_setup()
    _d = {'L0_attn_x': _L0_attn_in['x'], 'L0_attn_norm_w': _L0_attn_in['norm_w'], 'L0_attn_Wq': _L0_attn_in['Wq'], 'L0_attn_Wk': _L0_attn_in['Wk'], 'L0_attn_Wv': _L0_attn_in['Wv'], 'L0_attn_Wo': _L0_attn_in['Wo'], 'L0_attn_Wu': _L0_attn_in['Wu'], 'L0_ffn_norm_scale': _L0_ffn_in['norm_scale'], 'L0_ffn_wg': _L0_ffn_in['wg'], 'L0_ffn_bg': _L0_ffn_in['bg'], 'L0_ffn_w1': _L0_ffn_in['w1'], 'L0_ffn_b1': _L0_ffn_in['b1'], 'L0_ffn_w2': _L0_ffn_in['w2'], 'L0_ffn_b2': _L0_ffn_in['b2']}
    _x0 = _d['L0_attn_x']
    _d['L0_attn_x'] = jax.random.normal(jax.random.fold_in(jax.random.key(seed), 1), (2, 2048, 256), dtype=_x0.dtype)
    del _x0
    return _d

def reference(L0_attn_x, L0_attn_norm_w, L0_attn_Wq, L0_attn_Wk, L0_attn_Wv, L0_attn_Wo, L0_attn_Wu, L0_ffn_norm_scale, L0_ffn_wg, L0_ffn_bg, L0_ffn_w1, L0_ffn_b1, L0_ffn_w2, L0_ffn_b2):

    def _L0_attn_ref(x, norm_w, Wq, Wk, Wv, Wo, Wu):
        import jax, jax.numpy as jnp
        import numpy as np
        H_HEADS = 16
        SEG = 64
        EPS = 1e-06
        B, T, D = x.shape
        H = H_HEADS
        dk = D // H
        N = T // SEG
        xn = x * jax.lax.rsqrt(jnp.mean(x * x, axis=-1, keepdims=True) + EPS) * norm_w

        def proj(W):
            return (xn @ W.T).reshape(B, T, H, dk)
        q, k, v = (proj(Wq), proj(Wk), proj(Wv))
        pq = jax.nn.elu(q) + 1.0
        pk = jax.nn.elu(k) + 1.0
        pqc = pq.reshape(B, N, SEG, H, dk)
        pkc = pk.reshape(B, N, SEG, H, dk)
        vc = v.reshape(B, N, SEG, H, dk)
        S_chunk = jnp.einsum('bnchk,bnchv->bnhkv', pkc, vc)
        S_cum = jnp.cumsum(S_chunk, axis=1)
        S_excl = S_cum - S_chunk
        boundary_states = S_cum
        inter = jnp.einsum('bnchk,bnhkv->bnchv', pqc, S_excl)
        tri = jnp.tril(jnp.ones((SEG, SEG), x.dtype))
        A = jnp.einsum('bnchk,bndhk->bnhcd', pqc, pkc) * tri
        intra = jnp.einsum('bnhcd,bndhv->bnchv', A, vc)
        zk = pkc.sum(axis=2)
        z_excl = jnp.cumsum(zk, axis=1) - zk
        z = z_excl[:, :, None] + jnp.cumsum(pkc, axis=2)
        denom = jnp.einsum('bnchk,bnchk->bnch', pqc, z) + EPS
        attn_out = ((inter + intra) / denom[..., None]).reshape(B, T, D) @ Wo.T
        x_out = x + attn_out
        xc = x.reshape(B, N, SEG, D)
        m_stack = xc.mean(axis=2)
        counts = jnp.arange(1, SEG + 1, dtype=x.dtype)[None, None, :, None]
        m_current = (jnp.cumsum(xc, axis=2) / counts).reshape(B, T, D)
        causal_mask = (jnp.arange(T) // SEG)[:, None] > jnp.arange(N)[None, :]
        u = x @ Wu.T
        scale = 1.0 / jnp.sqrt(jnp.asarray(D, x.dtype))
        sc_cached = jnp.einsum('btd,bnd->btn', u, m_stack) * scale
        sc_cached = jnp.where(causal_mask[None], sc_cached, -jnp.inf)
        sc_cur = jnp.sum(u * m_current, axis=-1, keepdims=True) * scale
        attn_w = jax.nn.softmax(jnp.concatenate([sc_cached, sc_cur], axis=-1), axis=-1)
        gates_cached = attn_w[..., :N]
        gate_current = attn_w[..., N:]
        h_retrieved = jnp.einsum('btn,bthk,bnhkv->bthv', gates_cached, pq, boundary_states).reshape(B, T, D)
        retrieval_scale = 1.0
        return gate_current * x_out + retrieval_scale * h_retrieved

    def _L0_ffn_ref(x, norm_scale, wg, bg, w1, b1, w2, b2):
        import jax, jax.numpy as jnp
        import numpy as np
        H = 256
        I = 256
        E = 16
        K = 4
        LIMIT = 7.0
        ALPHA = 1.702
        EPS = 1e-05
        shape = x.shape
        xf = x.reshape(-1, shape[-1])
        xn = xf * jax.lax.rsqrt(jnp.mean(xf * xf, axis=-1, keepdims=True) + EPS) * norm_scale
        logits = xn @ wg + bg
        vals, idx = jax.lax.top_k(logits, K)
        gates = jax.nn.softmax(vals, axis=-1)
        gate_full = jnp.einsum('tke,tk->te', jax.nn.one_hot(idx, E, dtype=gates.dtype), gates)
        h = jnp.einsum('th,ehd->etd', xn, w1) + b1[:, None, :]
        a = jnp.minimum(h[..., ::2], LIMIT)
        b = jnp.clip(h[..., 1::2], -LIMIT, LIMIT)
        s = a * jax.nn.sigmoid(ALPHA * a) * (b + 1.0)
        y = jnp.einsum('eti,eih->eth', s, w2) + b2[:, None, :]
        t = jnp.einsum('eth,te->th', y, gate_full)
        return x + t.reshape(shape)
    x = L0_attn_x
    x = x + _layernorm(_L0_attn_ref(_layernorm(x, axis=-1), L0_attn_norm_w, L0_attn_Wq, L0_attn_Wk, L0_attn_Wv, L0_attn_Wo, L0_attn_Wu), axis=-1)
    x = x + _layernorm(_L0_ffn_ref(_layernorm(x, axis=-1), L0_ffn_norm_scale, L0_ffn_wg, L0_ffn_bg, L0_ffn_w1, L0_ffn_b1, L0_ffn_w2, L0_ffn_b2), axis=-1)
    return x

_drawn_inputs = setup_inputs


def setup_inputs(seed=0):
    import zlib

    import numpy as np

    out = dict(_drawn_inputs(seed))
    spreads = {'L0_attn_norm_w': (1.0, 0.2), 'L0_ffn_norm_scale': (1.0, 0.6)}
    factors = {'L0_attn_Wu': 4.224,
     'L0_ffn_wg': 4.835,
     'L0_ffn_bg': 8.0,
     'L0_ffn_w1': 4.676,
     'L0_ffn_b1': 8.0,
     'L0_ffn_w2': 4.537,
     'L0_ffn_b2': 26.988}
    for name, (base, spread) in spreads.items():
        noise = np.random.default_rng([zlib.crc32(name.encode()), seed]).standard_normal(out[name].shape)
        drawn = base * np.exp(spread * noise) if base else spread * noise
        out[name] = jnp.asarray(drawn.astype(out[name].dtype))
    for name, factor in factors.items():
        out[name] = (out[name] * factor).astype(out[name].dtype)
    return out
```

```python
from contextlib import ExitStack

import numpy as np

import concourse.bass as bass
from concourse import mybir

P = 128
F32 = mybir.dt.float32
I32 = mybir.dt.int32
U32 = mybir.dt.uint32
BF16 = mybir.dt.bfloat16
ALU = mybir.AluOpType
ACT = mybir.ActivationFunctionType
AX_X = mybir.AxisListType.X
ds = bass.ds

B, T, D = 2, 2048, 256
H, DK, SEG = 16, 16, 64
NT = T // P
NTT = B * NT
NSEG = T // SEG
DC = D // P
G = 4
HV = DK + 1
HG = H // 2
SW = 2 * HG * HV
RING = 6
E, TOPK, INNER = 16, 4, 256
CAP = B * T + P
NBLK = B * T * TOPK // P + E
IDCOL = D + E
ROW = 276
PER_BATCH = 262
CREDIT = 2
LN_EPS, ATT_RMS_EPS, DEN_EPS, FFN_RMS_EPS = 1e-5, 1e-6, 1e-6, 1e-5
LIMIT, ALPHA = 7.0, 1.702

C_IDENT = 0
C_CAUSAL = C_IDENT + P
C_MEANS = C_CAUSAL + SEG
C_SEGMEAN = C_MEANS + P
C_HEADS = C_SEGMEAN + 2
C_SCORE = C_HEADS + HG * HV
C_BEFORE = C_SCORE + NT * (NSEG + 1)
C_IOTA = C_BEFORE + P
C_BASE = C_IOTA + E
C_TOK = C_BASE + E
C_BLK = C_TOK + NTT
C_ALL = C_BLK + NBLK


def constants():
    c = np.zeros((P, C_ALL), np.float32)
    p = np.arange(P)
    c[:, C_IDENT:C_IDENT + P] = np.eye(P)
    c[:, C_CAUSAL:C_CAUSAL + SEG] = np.arange(SEG)[None] >= (p % SEG)[:, None]
    same = (p[:, None] // SEG) == (p[None] // SEG)
    c[:, C_MEANS:C_MEANS + P] = same * (p[:, None] <= p[None]) / ((p % SEG)[None] + 1.0)
    c[:, C_SEGMEAN:C_SEGMEAN + 2] = (p[:, None] // SEG == np.arange(2)[None]) / float(SEG)
    c[:, C_HEADS:C_HEADS + HG * HV] = (p[:, None] // DK) == (np.arange(HG * HV)[None] // HV)
    score = np.zeros((P, NT, NSEG + 1), np.float32)
    for i in range(NT):
        seg = 2 * i + p // SEG
        score[:, i, :NSEG] = np.where(seg[:, None] > np.arange(NSEG)[None], 0.0, -1e30)
    c[:, C_SCORE:C_BEFORE] = score.reshape(P, -1)
    c[:, C_BEFORE:C_BEFORE + P] = p[:, None] < p[None]
    c[:, C_IOTA:C_IOTA + E] = np.arange(E)
    c[:, C_BASE:C_BASE + E] = np.arange(E) * CAP
    c[:, C_TOK:C_TOK + NTT] = np.arange(NTT)[None] * P + p[:, None]
    c[:, C_BLK:C_BLK + NBLK] = np.arange(NBLK) * P
    fill = np.zeros((P, ROW), np.int32)
    fill[:, IDCOL] = B * T + p
    return c, fill


def program(nc, x_in, norm_w, Wq, Wk, Wv, Wo, Wu, norm_scale, wg, bg, w1, b1, w2, b2,
            const_in, fill_in, out, lists, sums, parts_dram):
    with ExitStack() as ctx:
        def sb(name, shape, dt=F32):
            return ctx.enter_context(nc.sbuf_tensor(name, shape, dt))

        def sem(name):
            return ctx.enter_context(nc.semaphore(name))

        PS = ctx.enter_context(nc.psum_tensor("PS", [P, 8, 512], F32))
        const = sb("const", [P, C_ALL])
        fill = sb("fill", [P, ROW], I32)
        ident = const[:, C_IDENT:C_IDENT + P]
        X2 = sb("X2", [P, NTT, D])
        XO = sb("XO", [P, NT, D])
        arena = sb("arena", [P, 24576])
        PQT = arena[:, 0:4096].rearrange("p (i c t) -> p i c t", i=NT, c=2)
        SB = arena[:, 4096:4096 + NSEG * SW].rearrange("p (n c w) -> p n c w", n=NSEG, c=2)
        W1 = arena[:, 0:16384].rearrange("p (e c n) -> p e c n", e=E, c=DC)
        FS = arena[:, 0:NTT * D].rearrange("p (t d) -> p t d", t=NTT)
        W2 = arena[:, 16384:24576].rearrange("p (e c n) -> p e c n", e=E, c=DC)
        spare = [4096 + NSEG * SW]

        def early(shape):
            n = int(np.prod(shape))
            view = arena[:, spare[0]:spare[0] + n]
            spare[0] += n
            assert spare[0] <= 24576
            names = " ".join("abcd"[:len(shape)])
            return view.rearrange(f"p ({names}) -> p {names}", **dict(zip("abcd", shape)))

        WT = early([DC, 4 * D])
        WoT = early([DC, D])
        Wun = early([DC, D])
        wraw = arena[:, 0:2048].rearrange("p (k c d) -> p k c d", k=4, c=DC)
        nw = sb("nw", [P, DC])
        nsB = sb("nsB", [P, D])
        wgS = sb("wgS", [P, DC, E])
        bgB = sb("bgB", [P, E])
        zeros = early([SW])
        MV = sb("MV", [P, NTT, 2])
        RS = sb("RS", [P, NTT])
        RR = sb("RR", [P, NTT])
        tmpS = sb("tmpS", [P, NTT])
        sqS = sb("sqS", [P, NTT])
        XS = sb("XS", [P, 2, D])
        MT = early([DC, NSEG])
        VM = early([DC, NSEG])
        XT = sb("XT", [P, 2, DC, P])
        MC = sb("MC", [P, 2, D])
        EX = sb("EX", [P, 2, 2 * D])
        RL = sb("RL", [P, 2, 2 * D])
        PF = sb("PF", [P, 2, 2, H, 32])
        V1 = sb("V1", [P, 2, H, HV])
        QT = sb("QT", [P, 2, G, P])
        F2 = early([2, 2, D])
        Q2 = early([2, 2, P])
        KT = early([2, G, P])
        AM = early([2, G * G, SEG]).rearrange("p b (j g) c -> p b j g c", j=G)
        SX = early([4, 2, HG * HV])
        AN = sb("AN", [P, 2, D])
        rden = sb("rden", [P, 2, H])
        ANT = early([2, DC, P])
        SCS = early([2, NSEG + 1])
        SC = early([NT, NSEG + 1])
        red = sb("red", [P, NT])
        MV2 = sb("MV2", [P, NT, 2])
        RS2 = sb("RS2", [P, NT])
        RR2 = sb("RR2", [P, NT])
        NM = sb("NM", [P, NTT])
        LG = sb("LG", [P, 2, E])
        M8 = sb("M8", [P, 2, 8])
        I8 = sb("I8", [P, 2, 8], U32)
        TV = sb("TV", [P, NT, TOPK])
        TI = sb("TI", [P, NT, TOPK])
        OH = EX[:].rearrange("p b (i j e) -> p (b i) j e", j=TOPK, e=E)
        OT = RL[:].rearrange("p b (i j e) -> p (b i) j e", j=TOPK, e=E)
        ST = RL[:].rearrange("p b w -> p (b w)")[:, 0:6 * NTT].rearrange("p (t s) -> p t s", t=NTT)
        MK = sb("MK", [P, NT, E])
        MKb = sb("MKb", [P, NT, E], BF16)
        beforeB = sb("beforeB", [P, P], BF16)
        onesB = sb("onesB", [P, P], BF16)
        PR = sb("PR", [P, NT, E])
        CNT = sb("CNT", [P, E])
        POSF = sb("POSF", [P, NT, TOPK])
        POS = sb("POS", [P, NT, TOPK], I32)
        TOKI = sb("TOKI", [P, NTT], I32)
        RW = sb("RW", [P, NT, ROW])
        XR = RW[:, 0:RING]
        ti32 = sb("ti32", [P, E], I32)
        nb = sb("nb", [P, E])
        cum = sb("cum", [P, E])
        onesE = sb("onesE", [P, E])
        BPART = NBLK // 3
        cmp = OT[0:1].rearrange("p i j e -> p (i j e)")[:, 0:BPART * E].rearrange("p (k e) -> p k e", e=E)
        blkE = sb("blkE", [1, NBLK])
        blkC = sb("blkC", [1, NBLK])
        blkR = blkC
        tabE = sb("tabE", [1, NBLK], I32)
        tabR = sb("tabR", [1, NBLK], I32)
        padF = sb("padF", [1, E])
        padR = sb("padR", [1, E], I32)
        b1s = arena[0:E, 6144:6144 + 2 * INNER]
        b2s = arena[0:E, 7168:7168 + D]
        bh = arena[0:E, 2048:2048 + 1152].bitcast(BF16).rearrange("e (k n) -> e k n", k=3)
        bres = arena[0:E, 4096:4096 + 1536].rearrange("e (k n) -> e k n", k=2)
        b1h = XO[0:3].rearrange("k i d -> k (i d)").bitcast(BF16).rearrange("k (e n) -> k e n", e=E)
        b2h = PF[0:3].rearrange("k a b h w -> k (a b h w)").bitcast(BF16).rearrange("k (e n) -> k e n", e=E)
        XRT = QT[:].rearrange("p b g t -> p b (g t)")[:, :, 0:D].rearrange("p b (c t) -> p b c t", c=DC)
        sT = QT[:].rearrange("p b g t -> p b (g t)")[:, :, D:2 * D].rearrange("p b (c t) -> p b c t", c=DC)
        hA, hS = EX[:, :, 0:INNER], EX[:, :, INNER:2 * INNER]
        hB, sS = RL[:, :, 0:INNER], RL[:, :, INNER:2 * INNER]
        YS = AN

        (const_in_s, weights_in, x_in_s, bias_in, small_in) = map(
            sem, ("const_loaded", "weights_loaded", "x_loaded", "bias_loaded", "small_loaded"))
        wt_ready, wt_copied = sem("wt_ready"), sem("wt_copied")
        prep, sqrt_asked, sqrt_done = sem("prep_done"), sem("sqrt_asked"), sem("sqrt_done")
        dve = sem("dve_order")
        names = ("xs0_ready", "mean_ready", "mean_copied", "vm_ready", "vm_copied",
                 "xs_ready", "front_T_ready", "xT_copied", "mcur_copied", "proj_ready", "exp_done",
                 "relu_done", "v_copied", "score_taken", "feat_ready", "qkT_ready", "qT_copied",
                 "kT_copied", "q_stored", "state0_ready", "state0_kept", "scores_ready", "masked",
                 "raw_score_ready", "raw_score_read", "state1_ready", "state1_kept", "states_stored", "attn_ready", "attn_normed",
                 "attnT_ready", "attnT_copied", "wo_ready", "xo_done", "score_stored",
                 "gate_arg", "gate_exp", "gates_ready", "z_ready", "z_used", "combined",
                 "xn_ready", "xnT_ready", "xnT_copied", "sum_asked", "sum_normed", "q2_kept", "roots_ready", "rows_sent", "logit_ready", "logit_used",
                 "h_ready", "top_arg", "top_exp", "mask_ready", "rank_ready", "routed")
        S = {n: sem(n) for n in names}
        h_out = [sem("h_stored_even"), sem("h_stored_odd")]
        sc_out = sem("scattered")
        pad_out, table_ready = sem("fill_stored"), sem("table_ready")
        w_in = [sem("expert_weights_even"), sem("expert_weights_odd")]
        biasq = sem("bias_parts")
        biasd = sem("bias_moved")
        xr_in = [sem(f"rows_loaded_{k}") for k in range(RING)]
        enames = ("xrT_ready", "xrT_copied", "hid_ready", "lin_ready", "sig_ready", "gate_lin_ready",
                  "s_ready", "sT_ready", "sT_copied", "y_ready", "y_scaled", "sum_added", "result_ready")
        S.update({n: sem(n) for n in enames})
        added = sem("block_added")
        f_in = [sem(f"sums_loaded_{k}") for k in range(4)]
        fout = sem("out_stored")
        seeded = sem("seeded")
        ordD, ordB = sem("order_den"), sem("order_batch")
        ord3, ord4, ord5, ord6 = sem("order_stats"), sem("order_sum"), sem("order_top"), sem("order_top_kept")
        ordE, final_asked, final_normed = sem("order_expert"), sem("final_roots"), sem("final_normed")
        turns = sem("waits_met")

        def met(eng):
            eng.sem_inc(turns, 1)


        def done(eng, name, count):
            eng.wait_ge(S[name], count + CREDIT)

        def inc(ins, name):
            return ins.then_inc(S[name], 1)

        x_v = x_in.rearrange("b (i p) d -> p (b i) d", p=P)
        out_v = out.rearrange("b (i p) d -> (b i p) d", p=P)
        block = ctx.enter_context(nc.Block())

        def steps(eng, step):
            step(0, 0)
            step(1, 1)
            with eng.Fori(1, NT // 2) as m:
                for par in range(2):
                    step(2 * m + par, par, True)
            step(NT, 0)
            step(NT + 1, 1)

        def parts(s, inner):
            if inner:
                return True, True, True
            return s < NT, 1 <= s <= NT, 2 <= s

        @block.sync
        def _(sp):
            sp.dma_start(const[:], const_in).then_inc(const_in_s, 16)
            for b in range(B):
                if b:
                    sp.wait_ge(x_in_s, 16 * b)
                sp.dma_start(X2[:, NT * b:NT * (b + 1), :], x_v[:, NT * b:NT * (b + 1), :]).then_inc(x_in_s, 16)
                if b == 0:
                    for k, w in enumerate((Wq, Wk, Wv, Wo)):
                        sp.dma_start(wraw[:, k], w.rearrange("(c p) d -> p c d", p=P)).then_inc(weights_in, 16)
                    sp.dma_start(Wun[:], Wu.rearrange("(c p) d -> p c d", p=P)).then_inc(weights_in, 16)
                    with nc.allow_non_contiguous_dma(reason="256 numbers, once"):
                        sp.dma_start(nw[:], norm_w.rearrange("(c p) -> p c", p=P)).then_inc(weights_in, 16)
            sp.dma_start(nsB[:], norm_scale.partition_broadcast(P)).then_inc(small_in, 16)
            sp.dma_start(bgB[:], bg.partition_broadcast(P)).then_inc(small_in, 16)
            sp.dma_start(wgS[:], wg.rearrange("(c p) e -> p c e", p=P)).then_inc(small_in, 16)
            sp.dma_start(fill[:], fill_in).then_inc(small_in, 16)
            sp.dma_start(b1s[:], b1).then_inc(bias_in, 16)
            sp.dma_start(b2s[:], b2).then_inc(bias_in, 16)
            sp.wait_ge(biasq, 5)
            sp.dma_start(parts_dram.rearrange("k e n -> e k n"), bh).then_inc(biasd, 16)
            sp.wait_ge(biasd, 16)
            sp.dma_start(sums[B * T:B * T + P, :], nsB[:]).then_inc(pad_out, 16)
            with sp.Fori(0, B) as b:
                with sp.Fori(0, NT // 2) as m:
                    for par in range(2):
                        i = 2 * m + par
                        t = b * NT + i
                        done(sp, "h_ready", t + 1)
                        sp.dma_start(sums[ds(t * P, P), :], XS[:, par]).then_inc(h_out[par], 16)
            done(sp, "combined", B)
            for e in range(E):
                if e >= 2:
                    sp.wait_ge(w_in[e % 2], 32 * (e // 2))
                sp.dma_start(W1[:, e], w1[e].rearrange("(c p) n -> p c n", p=P)).then_inc(w_in[e % 2], 16)
                sp.dma_start(W2[:, e], w2[e].rearrange("(c p) n -> p c n", p=P)).then_inc(w_in[e % 2], 16)
            done(sp, "xnT_copied", B * NT)
            sp.dma_start(b1h, parts_dram[:, :, 0:2 * INNER]).then_inc(biasd, 16)
            sp.dma_start(b2h, parts_dram[:, :, 2 * INNER:3 * INNER]).then_inc(biasd, 16)
            sp.wait_ge(table_ready, 1)
            sp.wait_ge(small_in, 64)
            sp.dma_start(lists[E * CAP:E * CAP + P, :], fill[:].bitcast(F32)).then_inc(pad_out, 16)
            with sp.Fori(0, E) as e:
                row = sp.value_load(padR[0:1, ds(e, 1)], min_val=0, max_val=E * CAP - P)
                sp.dma_start(lists[ds(row, P), :], fill[:].bitcast(F32)).then_inc(pad_out, 16)
            sp.wait_ge(pad_out, 16 * (E + 2))
            sp.wait_ge(sc_out, 16 * TOPK * NTT)

            def load_rows(k, slot):
                row = sp.value_load(tabR[0:1, ds(k, 1)], min_val=0, max_val=E * CAP)
                sp.dma_start(XR[:, slot], lists[ds(row, P), :]).then_inc(xr_in[slot], 16)

            for k in range(RING):
                load_rows(k, k)
            with sp.Fori(1, NBLK // RING) as m:
                for slot in range(RING):
                    done(sp, "sum_added", RING * m + slot - RING + 1)
                    load_rows(RING * m + slot, slot)
            done(sp, "sum_added", NBLK)
            for k in range(4):
                sp.dma_start(FS[:, 8 * k:8 * k + 8, :], sums[8 * k * P:8 * (k + 1) * P, :].rearrange(
                    "(t p) d -> p t d", p=P)).then_inc(f_in[k], 16)
            with sp.Fori(0, NTT // 4) as m:
                done(sp, "result_ready", 4 * m + 4)
                sp.dma_start(out_v[ds(m * (4 * P), 4 * P), :].rearrange("(t p) d -> p t d", p=P),
                             arena[:, ds(m * (4 * D), 4 * D)].rearrange("p (t d) -> p t d", t=4)).then_inc(fout, 16)
            sp.wait_ge(fout, 16 * (NTT // 4))

        @block.tensor
        def _(pe):
            for n in ("mean_ready", "vm_ready", "front_T_ready", "proj_ready", "qkT_ready", "state0_ready",
                      "state1_ready", "raw_score_ready", "scores_ready", "attn_ready", "attnT_ready", "wo_ready", "z_ready",
                      "xnT_ready", "logit_ready", "rank_ready", "xrT_ready", "hid_ready", "sT_ready", "y_ready"):
                pe.sem_inc(S[n], CREDIT)
            pe.sem_inc(seeded, 1)
            pe.wait_ge(seeded, 5)
            pe.wait_ge(const_in_s, 16)
            pe.wait_ge(weights_in, 96)
            for k in range(5):
                for oc in range(DC):
                    for c in range(DC):
                        w = Wun[:, oc, c * P:(c + 1) * P] if k == 4 else wraw[:, k, oc, c * P:(c + 1) * P]
                        last = pe.transpose(PS[:, k, c * D + oc * P:c * D + (oc + 1) * P], w, ident)
                last.then_inc(wt_ready, 1)
            pe.wait_ge(wt_copied, 5 * DC)

            def pass0(b):
                with pe.Fori(0, NT // 2) as m:
                    for par in range(2):
                        i = 2 * m + par
                        done(pe, "xs0_ready", b * NT + i + 1)
                        for c in range(DC):
                            last = pe.matmul(PS[:, c, ds(2 * i, 2)], lhsT=XS[:, par, c * P:(c + 1) * P],
                                             rhs=const[:, C_SEGMEAN:C_SEGMEAN + 2], start=True, stop=True)
                        inc(last, "mean_ready")
                done(pe, "mean_copied", b + 1)
                for c in range(DC):
                    for oc in range(DC):
                        last = pe.matmul(PS[:, 2, c * NSEG:(c + 1) * NSEG], lhsT=Wun[:, oc, c * P:(c + 1) * P],
                                         rhs=MT[:, oc, :], start=(oc == 0), stop=(oc == DC - 1))
                inc(last, "vm_ready")
                done(pe, "vm_copied", b + 1)
                pe.matmul(PS[:, 7, 0:SW], lhsT=zeros[:, 0:P], rhs=zeros[:], start=True, stop=False,
                          skip_group_check=True)

            def front_T(b, s, p):
                done(pe, "xs_ready", b * NT + s + 1)
                done(pe, "masked", b * NT + s - 1)
                done(pe, "q2_kept", b * NT + s)
                for c in range(DC):
                    pe.transpose(PS[:, 2, c * P:(c + 1) * P], XS[:, p, c * P:(c + 1) * P], ident)
                inc(pe.matmul(PS[:, 2, D:2 * D], lhsT=const[:, C_MEANS:C_MEANS + P], rhs=XS[:, p],
                              start=True, stop=True), "front_T_ready")

            def project(b, s, p):
                t = b * NT + s
                done(pe, "xT_copied", t + 1)
                done(pe, "exp_done", t)
                done(pe, "relu_done", t)
                done(pe, "xo_done", t - 1)
                done(pe, "v_copied", t)
                done(pe, "score_taken", t)
                done(pe, "attn_normed", t - 1)
                for c in range(DC):
                    last = pe.matmul(PS[:, 6, 272:272 + NSEG], lhsT=XT[:, p, c, :], rhs=VM[:, c, :],
                                     start=(c == 0), stop=(c == DC - 1))
                inc(last, "raw_score_ready")
                for half in range(2):
                    for c in range(DC):
                        last = pe.matmul(PS[:, 4 + half, :], lhsT=XT[:, p, c, :], rhs=WT[:, c, half * 512:half * 512 + 512],
                                  start=(c == 0), stop=(c == DC - 1))
                inc(last, "proj_ready")

            def features_T(b, s, p):
                t = b * NT + s
                done(pe, "feat_ready", t + 1)
                done(pe, "masked", t)
                for k in range(2):
                    for g in range(G):
                        pe.transpose(PS[:, k, g * P:(g + 1) * P],
                                     PF[:, p, k, 4 * g:4 * g + 4, :].rearrange("p h k -> p (h k)"), ident)
                for c in range(2):
                    last = pe.transpose(PS[:, 2, c * P:(c + 1) * P], F2[:, p, 0, c * P:(c + 1) * P], ident)
                inc(last, "qkT_ready")

            def state(b, s, p, seg):
                rows = slice(SEG * seg, SEG * seg + SEG)
                for c in range(2):
                    last = pe.matmul(PS[:, 7, c * HG * HV:(c + 1) * HG * HV],
                                     lhsT=F2[rows, p, 1, c * P:(c + 1) * P],
                                     rhs=V1[rows, p, HG * c:HG * (c + 1), :].rearrange("p h k -> p (h k)"),
                                     start=False, stop=False, skip_group_check=True)
                inc(last, f"state{seg}_ready")

            def scores(b, s, p):
                t = b * NT + s
                done(pe, "v_copied", t + 1)
                done(pe, "state1_kept", t)
                state(b, s, p, 0)
                done(pe, "qT_copied", t + 1)
                done(pe, "kT_copied", t + 1)
                done(pe, "attnT_copied", t)
                for g in range(G):
                    for seg in range(2):
                        for j in range(G):
                            rows = slice(32 * j, 32 * j + 32)
                            toks = slice(SEG * seg, SEG * seg + SEG)
                            last = pe.matmul(PS[toks, j, g * SEG:(g + 1) * SEG], lhsT=KT[rows, p, g, toks],
                                             rhs=QT[rows, p, g, toks], start=True, stop=True,
                                             skip_group_check=True)
                inc(last, "scores_ready")
                done(pe, "state0_kept", t + 1)
                state(b, s, p, 1)

            def attend(b, s, p, front):
                t = b * NT + s
                done(pe, "attn_normed", t)
                done(pe, "masked", t + 1)
                done(pe, "raw_score_read", t + 2 if front else t + 1)
                for seg in range(2):
                    toks = slice(SEG * seg, SEG * seg + SEG)
                    slot = (2 * p + seg - 1) % 4
                    for c in range(2):
                        pe.matmul(PS[toks, 6, c * HG * HV:(c + 1) * HG * HV], lhsT=Q2[:, p, c, toks],
                                  rhs=SX[:, slot, c, :], start=(c == 0), stop=False, skip_group_check=True)
                    for h in range(H):
                        last = pe.matmul(PS[toks, 6, h * HV:(h + 1) * HV], lhsT=AM[toks, p, h % G, h // G, :],
                                         rhs=V1[toks, p, h, :], start=False, stop=True, skip_group_check=True)
                inc(last, "attn_ready")

            def attended_T(b, s, p):
                done(pe, "attn_normed", b * NT + s + 1)
                for c in range(DC):
                    last = pe.transpose(PS[:, 3, c * P:(c + 1) * P], AN[:, p, c * P:(c + 1) * P], ident)
                inc(last, "attnT_ready")

            def out_proj(b, s, p):
                done(pe, "attnT_copied", b * NT + s + 1)
                for c in range(DC):
                    last = pe.matmul(PS[:, 4, 0:D], lhsT=ANT[:, p, c, :], rhs=WoT[:, c, :],
                                     start=(c == 0), stop=(c == DC - 1))
                inc(last, "wo_ready")

            with pe.Fori(0, B) as b:
                pass0(b)

                def step(s, par, inner=False):
                    f, k, w = parts(s, inner)
                    if f:
                        front_T(b, s, par)
                    if w:
                        out_proj(b, s - 2, par)
                    if k:
                        if f:
                            done(pe, "xT_copied", b * NT + s + 1)
                            done(pe, "mcur_copied", b * NT + s + 1)
                        else:
                            done(pe, "q2_kept", b * NT + s)
                        scores(b, s - 1, 1 - par)
                    if f:
                        project(b, s, par)
                    if k:
                        attend(b, s - 1, 1 - par, f)
                    if f:
                        features_T(b, s, par)
                    if k:
                        attended_T(b, s - 1, 1 - par)

                steps(pe, step)
                done(pe, "gates_ready", b + 1)
                done(pe, "q_stored", (b + 1) * NT)
                done(pe, "states_stored", (b + 1) * NT)
                done(pe, "xo_done", (b + 1) * NT)
                turn = 0
                for i in range(NT):
                    for grp in range(2 * i // 8 + 1):
                        done(pe, "z_used", b * 40 + turn - 1)
                        for c in range(2):
                            for half in range(2):
                                first = 8 * grp + 4 * half
                                last = pe.matmul(PS[:, 4 * (turn % 2) + 2 * c + half, :], lhsT=PQT[:, i, c, :],
                                                 rhs=SB[:, first:first + 4, c, :].rearrange(
                                                     "p n (h v) -> p n h v", h=HG)[:, :, :, 0:DK],
                                                 start=True, stop=True)
                        inc(last, "z_ready")
                        turn += 1
                done(pe, "z_used", b * 40 + 40)
                met(pe)
                with pe.Fori(0, NT // 2) as m:
                    for par in range(2):
                        t = b * NT + 2 * m + par
                        done(pe, "xn_ready", t + 1)
                        done(pe, "xnT_copied", t - 1)
                        for c in range(DC):
                            last = pe.transpose(PS[:, par, c * P:(c + 1) * P], MC[:, par, c * P:(c + 1) * P], ident)
                        inc(last, "xnT_ready")
                        done(pe, "xnT_copied", t + 1)
                        done(pe, "logit_used", t - 1)
                        for c in range(DC):
                            last = pe.matmul(PS[:, 2 + par, 0:E], lhsT=XT[:, par, c, :], rhs=wgS[:, c, :],
                                             start=(c == 0), stop=(c == DC - 1))
                        inc(last, "logit_ready")
                done(pe, "mask_ready", b + 1)
                pe.matmul(PS[:, 4, 0:NT * E], lhsT=beforeB[:], rhs=MKb[:].rearrange("p i e -> p (i e)"),
                          start=True, stop=False, skip_group_check=True)
                for i in range(NT - 1):
                    pe.matmul(PS[:, 4, (i + 1) * E:NT * E].rearrange("p (i e) -> p i e", e=E), lhsT=onesB[:],
                              rhs=MKb[:, i:i + 1, :].broadcast_to([P, NT - 1 - i, E]),
                              start=False, stop=False, skip_group_check=True)
                for i in range(NT):
                    last = pe.matmul(PS[:, 5, 0:E], lhsT=onesB[:], rhs=MKb[:, i, :], start=(i == 0),
                                     stop=(i == NT - 1))
                inc(last, "rank_ready")
                done(pe, "routed", b + 1)

            pe.wait_ge(biasd, 48)
            pe.wait_ge(table_ready, 1)

            def turn_rows(k, m, slot):
                par = slot % 2
                pe.wait_ge(xr_in[slot], 16 * m + 16)
                done(pe, "xrT_copied", k - 1)
                for c in range(DC):
                    last = pe.transpose(PS[:, par, c * P:(c + 1) * P], XR[:, slot, c * P:(c + 1) * P], ident)
                inc(last, "xrT_ready")

            def hidden(k, par):
                e = pe.value_load(tabE[0:1, ds(k, 1)], min_val=0, max_val=E - 1)
                done(pe, "xrT_copied", k + 1)
                done(pe, "gate_lin_ready", k - 1)
                done(pe, "lin_ready", k - 1)
                w = arena[:, ds(e * 1024, 1024)].rearrange("p (c f two) -> p c two f", c=DC, two=2)
                for c in range(DC):
                    pe.matmul(PS[:, 2 + par, :], lhsT=XRT[:, par, c, :], rhs=w[:, c], start=(c == 0), stop=False)
                bias = b1h.rearrange("k e n -> k (e n)")[:, ds(e * 512, 512)].rearrange("k (f two) -> k two f", two=2)
                inc(pe.matmul(PS[:, 2 + par, :], lhsT=onesB[0:3, :], rhs=bias, start=False, stop=True), "hid_ready")

            def turn_s(k, par):
                done(pe, "s_ready", k + 1)
                done(pe, "sT_copied", k - 1)
                for c in range(2):
                    last = pe.transpose(PS[:, 4 + par, c * P:(c + 1) * P], sS[:, par, c * P:(c + 1) * P], ident)
                inc(last, "sT_ready")

            def expert_out(k, par):
                e = pe.value_load(tabE[0:1, ds(k, 1)], min_val=0, max_val=E - 1)
                done(pe, "sT_copied", k + 1)
                done(pe, "y_scaled", k - 1)
                for c in range(2):
                    pe.matmul(PS[:, 6 + par, 0:D], lhsT=sT[:, par, c, :],
                              rhs=arena[:, ds(e * 512 + (16384 + c * D), D)], start=(c == 0), stop=False)
                inc(pe.matmul(PS[:, 6 + par, 0:D], lhsT=onesB[0:3, :],
                              rhs=b2h.rearrange("k e n -> k (e n)")[:, ds(e * D, D)], start=False, stop=True),
                    "y_ready")

            for par in range(2):
                pe.wait_ge(w_in[par], 16 * E)
            def block_step(k, m, j, inner=False):
                if inner or k + 1 < NBLK:
                    hidden(k + 1, (j + 1) % 2)
                turn_s(k, j % 2)
                if inner or k + 2 < NBLK:
                    turn_rows(k + 2, m + (j + 2) // RING, (j + 2) % RING)
                if inner or k >= 1:
                    expert_out(k - 1, (j + 1) % 2)

            turn_rows(0, 0, 0)
            turn_rows(1, 0, 1)
            hidden(0, 0)
            for j in range(RING):
                block_step(j, 0, j)
            with pe.Fori(1, NBLK // RING - 1) as m:
                for j in range(RING):
                    block_step(RING * m + j, m, j, True)
            for j in range(RING):
                block_step(NBLK - RING + j, NBLK // RING - 1, j)
            expert_out(NBLK - 1, 1)

        @block.scalar
        def _(act):
            for n in ("xT_copied", "mcur_copied", "exp_done", "relu_done", "v_copied", "kT_copied", "attnT_copied",
                      "gate_exp", "xnT_copied", "h_ready", "sum_normed", "q2_kept", "states_stored", "q_stored", "top_exp", "xrT_copied", "sig_ready", "y_scaled"):
                act.sem_inc(S[n], CREDIT)
            act.sem_inc(seeded, 1)
            act.wait_ge(seeded, 5)

            def root(asked, n):
                act.wait_ge(sqrt_asked, asked)
                nc.scalar.activation(sqS[:, 0:n], tmpS[:, 0:n], ACT.Sqrt).then_inc(sqrt_done, 1)

            root(1, NTT)
            root(2, NTT)

            with act.Fori(0, B) as b:
                def step(s, par, inner=False):
                    f, k, w = parts(s, inner)
                    t = b * NT + s
                    if f:
                        done(act, "front_T_ready", t + 1)
                        done(act, "proj_ready", t - 1)
                        inc(nc.scalar.copy(XT[:, par], PS[:, 2, 0:D].rearrange("p (c t) -> p c t", c=DC)), "xT_copied")
                        done(act, "score_taken", t - 1)
                        inc(nc.scalar.copy(MC[:, par], PS[:, 2, D:2 * D]), "mcur_copied")
                        done(act, "proj_ready", t + 1)
                        done(act, "feat_ready", t - 1)
                        met(act)
                        r = RR[:, ds(t, 1)]
                        inc(nc.scalar.activation(EX[:, par], PS[:, 4, :], ACT.Exp, scale=r), "exp_done")
                        inc(nc.scalar.activation(RL[:, par], PS[:, 4, :], ACT.Relu, scale=r), "relu_done")
                        done(act, "score_taken", t + 1)
                        done(act, "attn_ready", t - 1)
                        met(act)
                        inc(nc.scalar.activation(V1[:, par, :, 0:DK], PS[:, 5, 0:D].rearrange("p (h v) -> p h v", h=H),
                                                 ACT.Copy, scale=r), "v_copied")
                        done(act, "qkT_ready", t + 1)
                        done(act, "scores_ready", t - 1)
                        done(act, "attn_ready", t - 1)
                        inc(nc.scalar.copy(KT[:, par], PS[:, 1, :].rearrange("p (g t) -> p g t", g=G)), "kT_copied")
                        inc(nc.scalar.copy(Q2[:, par], PS[:, 2, 0:D].rearrange("p (c t) -> p c t", c=2)), "q2_kept")
                    if k:
                        done(act, "attnT_ready", t)
                        done(act, "state1_kept", t)
                        done(act, "wo_ready", t - 2)
                        inc(nc.scalar.copy(ANT[:, 1 - par], PS[:, 3, 0:D].rearrange("p (c t) -> p c t", c=DC)),
                            "attnT_copied")
                        met(act)
                        inc(nc.scalar.copy(arena[:, ds((s - 1) * (2 * SW) + 4096, 2 * SW)],
                                           SX[:, 2 - 2 * par:4 - 2 * par].rearrange("p s c w -> p (s c w)")),
                            "states_stored")
                    if f:
                        done(act, "q2_kept", t + 1)
                        met(act)
                        inc(nc.scalar.copy(arena[:, ds(s * D, D)], Q2[:, par].rearrange("p c t -> p (c t)")),
                            "q_stored")

                act.wait_ge(biasd, 16)
                steps(act, step)
                done(act, "gate_arg", b + 1)
                inc(nc.scalar.activation(SC[:], SC[:], ACT.Exp), "gate_exp")
                root(3 * b + 3, NT)

                def scaled(i, dst, src, name, asked):
                    done(act, name, asked)
                    met(act)
                    return nc.scalar.activation(dst, src, ACT.Identity, scale=RS2[:, ds(i, 1)], bias=NM[:, ds(i, 1)])

                with act.Fori(0, NT) as i:
                    xo = XO[:, ds(i, 1), :].rearrange("p o d -> p (o d)")
                    inc(scaled(i, xo, xo, "sum_asked", b + 1), "sum_normed")
                root(3 * b + 4, NT)
                root(3 * b + 5, NT)
                with act.Fori(0, NT // 2) as m:
                    for par in range(2):
                        i = 2 * m + par
                        t = b * NT + i
                        act.wait_ge(h_out[par], 16 * (b * (NT // 2) + m) + 16)
                        done(act, "xn_ready", t - 1)
                        inc(scaled(i, XS[:, par], X2[:, ds(t, 1), :].rearrange("p o d -> p (o d)"),
                                   "roots_ready", b + 1), "h_ready")
                    for par in range(2):
                        t = b * NT + 2 * m + par
                        done(act, "xnT_ready", t + 1)
                        done(act, "logit_ready", t - 1)
                        inc(nc.scalar.copy(XT[:, par], PS[:, par, 0:D].rearrange("p (c t) -> p c t", c=DC)), "xnT_copied")
                done(act, "top_arg", b + 1)
                inc(nc.scalar.activation(TV[:], TV[:], ACT.Exp), "top_exp")

            act.wait_ge(table_ready, 1)

            def copy_rows(k, par):
                done(act, "xrT_ready", k + 1)
                done(act, "hid_ready", k - 1)
                inc(nc.scalar.copy(XRT[:, par], PS[:, par, 0:D].rearrange("p (c t) -> p c t", c=DC)), "xrT_copied")

            def sigmoid(k, par):
                done(act, "lin_ready", k + 1)
                done(act, "s_ready", k - 1)
                inc(nc.scalar.activation(hS[:, par], hA[:, par], ACT.Sigmoid, scale=ALPHA), "sig_ready")

            def scale_out(k, slot):
                par = slot % 2
                e = act.value_load(tabE[0:1, ds(k, 1)], min_val=0, max_val=E - 1)
                done(act, "y_ready", k + 1)
                done(act, "sum_added", k - 1)
                met(act)
                inc(nc.scalar.activation(YS[:, par], PS[:, 6 + par, 0:D], ACT.Copy,
                                         scale=XR[:, slot, ds(e + D, 1)]), "y_scaled")

            def block_step(k, j, inner=False):
                if inner or k + 1 < NBLK:
                    sigmoid(k + 1, (j + 1) % 2)
                if inner or k + 2 < NBLK:
                    copy_rows(k + 2, j % 2)
                if inner or k >= 1:
                    scale_out(k - 1, (j - 1) % RING)

            copy_rows(0, 0)
            copy_rows(1, 1)
            sigmoid(0, 0)
            for j in range(RING):
                block_step(j, j)
            with act.Fori(1, NBLK // RING - 1) as m:
                for j in range(RING):
                    block_step(RING * m + j, j, True)
            for j in range(RING):
                block_step(NBLK - RING + j, j)
            scale_out(NBLK - 1, RING - 1)
            root(9, NTT)
            act.wait_ge(final_asked, 1)
            with act.Fori(0, NTT) as t:
                fs = arena[:, ds(t * D, D)]
                nc.scalar.activation(fs, fs, ACT.Identity, scale=RS[:, ds(t, 1)],
                                     bias=NM[:, ds(t, 1)]).then_inc(final_normed, 1)

        @block.vector
        def _(v):
            order = [0]

            def own(ins):
                order[0] += 1
                ins.then_inc(dve, 1)
                v.wait_ge(dve, order[0])

            for n in ("raw_score_read", "xs0_ready", "mean_copied", "vm_copied", "xs_ready", "score_taken", "feat_ready", "qT_copied",
                      "state0_kept", "state1_kept", "masked", "attn_normed", "xo_done", "gate_arg", "gates_ready",
                      "z_used", "combined", "xn_ready", "sum_asked", "roots_ready", "logit_used", "top_arg", "mask_ready", "routed",
                      "lin_ready", "gate_lin_ready", "s_ready", "sT_copied", "result_ready", "score_stored"):
                v.sem_inc(S[n], CREDIT)
            for q in h_out:
                v.sem_inc(q, 16)
            v.sem_inc(seeded, 1)
            v.memset(zeros[:], 0.0).then_inc(prep, 1)
            v.memset(PF[:], 0.0).then_inc(prep, 1)
            v.memset(V1[:], 1.0).then_inc(prep, 1)
            v.memset(CNT[:], 0.0).then_inc(prep, 1)
            v.memset(onesB[:], 1.0).then_inc(prep, 1)
            v.memset(onesE[:], 1.0).then_inc(prep, 1)
            v.memset(RW[:], 0.0).then_inc(prep, 1)
            v.wait_ge(prep, 7)
            v.sem_inc(seeded, 1)
            v.wait_ge(seeded, 5)
            v.wait_ge(const_in_s, 16)
            v.tensor_copy(beforeB[:], const[:, C_BEFORE:C_BEFORE + P]).then_inc(prep, 1)
            v.tensor_copy(TOKI[:], const[:, C_TOK:C_TOK + NTT]).then_inc(prep, 1)
            v.wait_ge(weights_in, 96)
            for k in range(5):
                v.wait_ge(wt_ready, k + 1)
                for c in range(DC):
                    src = PS[:, k, c * D:(c + 1) * D]
                    if k < 3:
                        ins = v.tensor_scalar(WT[:, c, k * D:(k + 1) * D], src, nw[:, c:c + 1], None, ALU.mult)
                    elif k == 3:
                        ins = v.tensor_copy(WoT[:, c, :], src)
                    else:
                        ins = v.tensor_copy(WT[:, c, 3 * D:4 * D], src)
                    ins.then_inc(wt_copied, 1)
            v.wait_ge(bias_in, 32)
            b12 = [(b1s[:], slice(0, 2 * INNER)), (b2s[:], slice(2 * INNER, 3 * INNER))]
            for src, cols in b12:
                own(v.tensor_copy(bh[:, 0, cols], src))
                own(v.tensor_tensor(bres[:, 0, cols], src, bh[:, 0, cols], ALU.subtract))
                own(v.tensor_copy(bh[:, 1, cols], bres[:, 0, cols]))
                own(v.tensor_tensor(bres[:, 1, cols], bres[:, 0, cols], bh[:, 1, cols], ALU.subtract))
                own(v.tensor_copy(bh[:, 2, cols], bres[:, 1, cols]))
            v.sem_inc(biasq, 5)
            v.wait_ge(x_in_s, 16 * B)

            def aggregate(dst, n, q, count):
                v.wait_ge(q, count)
                met(v)
                for i in range(n):
                    last = v.bn_aggr(dst[:, i, :], ST[:, i, :])
                return last

            def tile(x, i):
                return x[:, ds(i, 1), :].rearrange("p o d -> p (o d)")

            with v.Fori(0, NTT) as t:
                v.bn_stats(tile(ST, t), tile(X2, t)).then_inc(ord3, 1)
            own(aggregate(MV, NTT, ord3, NTT))

            asked = [0]

            def inverse_root(dst, n, arg, base=None):
                asked[0] += 1
                at = asked[0] if base is None else base
                arg.then_inc(sqrt_asked, 1)
                v.wait_ge(sqrt_done, at)
                own(v.reciprocal(dst, sqS[:, 0:n]))

            inverse_root(RS[:], NTT, v.tensor_scalar(tmpS[:], MV[:, :, 1], LN_EPS, None, ALU.add))
            own(v.tensor_tensor(tmpS[:], RS[:], RS[:], ALU.mult))
            own(v.tensor_tensor(tmpS[:], tmpS[:], MV[:, :, 1], ALU.mult))
            inverse_root(RR[:], NTT, v.tensor_scalar(tmpS[:], tmpS[:], ATT_RMS_EPS, None, ALU.add))
            with v.Fori(0, B) as b:
                local = [0]

                def own_b(ins, last=None):
                    local[0] += 1
                    ins.then_inc(ordB, 1)
                    v.wait_ge(ordB, b * PER_BATCH + local[0])

                def root_b(dst, n, arg, k):
                    arg.then_inc(sqrt_asked, 1)
                    v.wait_ge(sqrt_done, 3 * b + 3 + k)
                    own_b(v.reciprocal(dst, sqS[:, 0:n]))

                with v.Fori(0, NT // 2) as m:
                    for par in range(2):
                        i = 2 * m + par
                        t = b * NT + i
                        done(v, "mean_ready", t - 1)
                        v.wait_ge(h_out[par], 16 * (b * (NT // 2)) + 16)
                        for dst in (tile(XO, i), XS[:, par]):
                            ins = v.tensor_scalar(dst, tile(X2, t), MV[:, ds(t, 1), 0:1].rearrange("p o d -> p (o d)"),
                                                  RS[:, ds(t, 1)], ALU.subtract, ALU.mult)
                        inc(ins, "xs0_ready")
                done(v, "mean_ready", (b + 1) * NT)
                inc(v.tensor_copy(MT[:], PS[:, 0:DC, 0:NSEG]), "mean_copied")
                done(v, "vm_ready", b + 1)
                inc(v.tensor_copy(VM[:], PS[:, 2, 0:DC * NSEG].rearrange("p (c n) -> p c n", c=DC)), "vm_copied")
                done(v, "attn_ready", b * NT)
                done(v, "states_stored", b * NT)
                own_b(v.memset(SX[:, 3], 0.0))

                def step(s, par, inner=False):
                    f, k, w = parts(s, inner)
                    t = b * NT + s
                    q = 1 - par
                    if f:
                        done(v, "front_T_ready", t - 1)
                        inc(v.tensor_copy(XS[:, par], tile(XO, s)), "xs_ready")
                    if w:
                        done(v, "wo_ready", t - 1)
                        xo = tile(XO, s - 2)
                        inc(v.tensor_tensor(xo, PS[:, 4, 0:D], xo, ALU.add), "xo_done")
                    if k:
                        heads = const[:, C_HEADS:C_HEADS + HG * HV].unsqueeze(1).broadcast_to([P, 2, HG * HV])
                        state = PS[:, 7, 0:SW].rearrange("p (c w) -> p c w", c=2)
                        done(v, "state0_ready", t)
                        done(v, "states_stored", t - 2)
                        done(v, "attn_ready", t - 1)
                        inc(v.tensor_tensor(SX[:, 2 * q], state, heads, ALU.mult), "state0_kept")
                        done(v, "scores_ready", t)
                        causal = const[:, C_CAUSAL:C_CAUSAL + SEG].unsqueeze(1).broadcast_to([P, G * G, SEG])
                        inc(v.tensor_tensor(AM[:, q], PS[:, 0:G, 0:G * SEG].rearrange("p j (g c) -> p j g c", g=G),
                                            causal.rearrange("p (j g) c -> p j g c", j=G), ALU.mult), "masked")
                        done(v, "state1_ready", t)
                        inc(v.tensor_tensor(SX[:, 2 * q + 1], state, heads, ALU.mult), "state1_kept")
                    if f:
                        done(v, "raw_score_ready", t + 1)
                        inc(v.tensor_copy(SCS[:, par, 0:NSEG], PS[:, 6, 272:272 + NSEG]), "raw_score_read")
                        done(v, "proj_ready", t + 1)
                        done(v, "mcur_copied", t + 1)
                        inc(v.tensor_tensor_reduce(MC[:, par], PS[:, 5, D:2 * D], MC[:, par], 1.0, 0.0, ALU.mult,
                                                   ALU.add, SCS[:, par, NSEG:NSEG + 1]), "score_taken")
                        done(v, "relu_done", t + 1)
                        done(v, "qkT_ready", t - 1)
                        done(v, "state1_ready", t - 1)
                        ex, rl = (x[:, par].rearrange("p (h w) -> p h w", w=DK) for x in (EX, RL))
                        v.scalar_tensor_tensor(F2[:, par].rearrange("p k w -> p (k w)"), EX[:, par], 1.0, RL[:, par],
                                               ALU.min, ALU.add)
                        inc(v.scalar_tensor_tensor(PF[:, par].rearrange("p k h w -> p (k h) w")[:, :, 0:DK], ex, 1.0,
                                                   rl, ALU.min, ALU.add), "feat_ready")
                    if k:
                        done(v, "attn_ready", t)
                        o = PS[:, 6, 0:H * HV].rearrange("p (h c) -> p h c", h=H)
                        v.tensor_scalar(rden[:, q], o[:, :, DK], DEN_EPS, None, ALU.add).then_inc(ordD, 1)
                        v.wait_ge(ordD, 2 * t - 1)
                        v.reciprocal(rden[:, q], rden[:, q]).then_inc(ordD, 1)
                        v.wait_ge(ordD, 2 * t)
                        done(v, "attnT_ready", t - 2)
                        inc(v.tensor_tensor(AN[:, q].rearrange("p (h v) -> p h v", h=H), o[:, :, 0:DK],
                                            rden[:, q].unsqueeze(2).broadcast_to([P, H, DK]), ALU.mult), "attn_normed")
                    if f:
                        done(v, "qkT_ready", t + 1)
                        inc(v.tensor_copy(QT[:, par], PS[:, 0, :].rearrange("p (g t) -> p g t", g=G)), "qT_copied")
                        done(v, "score_taken", t + 1)
                        inc(v.tensor_scalar(tile(SC, s), SCS[:, par], 1.0, None, ALU.mult), "score_stored")

                steps(v, step)

                done(v, "score_stored", (b + 1) * NT)
                flat = SC[:].rearrange("p i n -> p (i n)")
                own_b(v.scalar_tensor_tensor(flat, flat, 1.0 / 16.0, const[:, C_SCORE:C_BEFORE], ALU.mult, ALU.add))
                own_b(v.tensor_reduce(red[:], SC[:], AX_X, ALU.max))
                inc(v.tensor_tensor(SC[:], SC[:], red[:].unsqueeze(2).broadcast_to([P, NT, NSEG + 1]),
                                    ALU.subtract), "gate_arg")
                done(v, "gate_exp", b + 1)
                own_b(v.tensor_reduce(red[:], SC[:], AX_X, ALU.add))
                own_b(v.reciprocal(red[:], red[:]))
                inc(v.tensor_tensor(SC[:], SC[:], red[:].unsqueeze(2).broadcast_to([P, NT, NSEG + 1]),
                                    ALU.mult), "gates_ready")
                done(v, "gates_ready", b + 1)
                done(v, "xo_done", (b + 1) * NT)

                Z = PS[:].rearrange("p (z c half) w -> p z c half w", z=2, c=2)
                turn = 0
                for i in range(NT):
                    acc = XO[:, i, :]
                    own_b(v.tensor_scalar(acc, acc, SC[:, i, NSEG:NSEG + 1], None, ALU.mult))
                    for grp in range(2 * i // 8 + 1):
                        done(v, "z_ready", b * 40 + turn + 1)
                        for n in range(8 * grp, min(8 * grp + 8, 2 * i + 1)):
                            ins = v.scalar_tensor_tensor(
                                acc.rearrange("p (c w) -> p c w", c=2),
                                Z[:, turn % 2, :, n // 4 % 2, (n % 4) * P:(n % 4 + 1) * P],
                                SC[:, i, n:n + 1], acc.rearrange("p (c w) -> p c w", c=2), ALU.mult, ALU.add)
                            if n < min(8 * grp + 7, 2 * i):
                                own_b(ins)
                        inc(ins, "z_used")
                        turn += 1
                        done(v, "z_used", b * 40 + turn)
                v.sem_inc(S["combined"], 1)

                met(v)
                with v.Fori(0, NT) as i:
                    v.bn_stats(tile(ST, i), tile(XO, i)).then_inc(ord3, 1)
                own_b(aggregate(MV2, NT, ord3, NTT + (2 * b + 1) * NT))
                root_b(RS2[:], NT, v.tensor_scalar(tmpS[:, 0:NT], MV2[:, :, 1], LN_EPS, None, ALU.add), 0)
                minus_mean = (NM[:, 0:NT], MV2[:, :, 0], -1.0, RS2[:], ALU.mult, ALU.mult)
                inc(v.scalar_tensor_tensor(*minus_mean), "sum_asked")
                met(v)
                with v.Fori(0, NT) as i:
                    t = b * NT + i
                    done(v, "sum_normed", t + 1)
                    v.tensor_tensor(tile(X2, t), tile(X2, t), tile(XO, i), ALU.add).then_inc(ord4, 1)
                    v.wait_ge(ord4, t + 1)
                    met(v)
                    v.bn_stats(tile(ST, i), tile(X2, t)).then_inc(ord3, 1)
                own_b(aggregate(MV2, NT, ord3, NTT + (2 * b + 2) * NT))
                root_b(RS2[:], NT, v.tensor_scalar(tmpS[:, 0:NT], MV2[:, :, 1], LN_EPS, None, ALU.add), 1)
                own_b(v.scalar_tensor_tensor(*minus_mean))
                own_b(v.tensor_tensor(tmpS[:, 0:NT], RS2[:], RS2[:], ALU.mult))
                own_b(v.tensor_tensor(tmpS[:, 0:NT], tmpS[:, 0:NT], MV2[:, :, 1], ALU.mult))
                root_b(RR2[:], NT, v.tensor_scalar(tmpS[:, 0:NT], tmpS[:, 0:NT], FFN_RMS_EPS, None, ALU.add), 2)
                v.sem_inc(S["roots_ready"], 1)
                v.wait_ge(small_in, 64)
                done(v, "rows_sent", b)
                met(v)

                def normed(i, par):
                    t = b * NT + i
                    done(v, "h_ready", t + 1)
                    done(v, "xnT_ready", t - 1)
                    inc(v.scalar_tensor_tensor(MC[:, par], XS[:, par], RR2[:, ds(i, 1)], nsB[:], ALU.mult, ALU.mult),
                        "xn_ready")

                def top(m):
                    ts = [(2 * m + par, b * NT + 2 * m + par, par) for par in range(2)]
                    for i, t, par in ts:
                        done(v, "logit_ready", t + 1)
                        inc(v.tensor_tensor(LG[:, par], PS[:, 2 + par, 0:E], bgB[:], ALU.add), "logit_used")
                    for i, t, par in ts:
                        v.tensor_scalar(arow(i, 0, D), MC[:, par], 1.0, None, ALU.mult).then_inc(ord6, 1)
                    done(v, "logit_used", b * NT + 2 * m + 2)
                    met(v)
                    for i, t, par in ts:
                        v.max(M8[:, par], LG[:, par]).then_inc(ord5, 1)
                    v.wait_ge(ord5, 2 * (b * NT + 2 * m) + 2)
                    met(v)
                    for i, t, par in ts:
                        v.max_index(I8[:, par], M8[:, par], LG[:, par]).then_inc(ord5, 1)
                    v.wait_ge(ord5, 2 * (b * NT + 2 * m) + 4)
                    for i, t, par in ts:
                        v.tensor_scalar(tile(TV, i), M8[:, par, 0:TOPK], 1.0, None, ALU.mult).then_inc(ord6, 1)
                        v.tensor_scalar(tile(TI, i), I8[:, par, 0:TOPK], 1.0, None, ALU.mult).then_inc(ord6, 1)

                def arow(i, at, n):
                    return RW[:].rearrange("p i w -> p (i w)")[:, ds(i * ROW + at, n)]

                with v.Fori(0, NT // 2) as m:
                    for par in range(2):
                        normed(2 * m + par, par)
                    top(m)
                v.wait_ge(ord6, 3 * NT * (b + 1))

                iota = const[:, C_IOTA:C_IOTA + E].unsqueeze(1).broadcast_to([P, NT * TOPK, E])
                own_b(v.tensor_tensor(OH.rearrange("p i j e -> p (i j) e"),
                                      TI[:].rearrange("p i j -> p (i j)").unsqueeze(2).broadcast_to([P, NT * TOPK, E]),
                                      iota, ALU.is_equal))
                own_b(v.tensor_reduce(MK[:], OH.rearrange("p i j e -> p i e j"), AX_X, ALU.add))
                inc(v.tensor_copy(MKb[:], MK[:]), "mask_ready")
                own_b(v.tensor_copy(red[:], TV[:, :, 0]))
                inc(v.tensor_tensor(TV[:], TV[:], red[:].unsqueeze(2).broadcast_to([P, NT, TOPK]),
                                    ALU.subtract), "top_arg")
                done(v, "top_exp", b + 1)
                own_b(v.tensor_reduce(red[:], TV[:], AX_X, ALU.add))
                own_b(v.reciprocal(red[:], red[:]))
                own_b(v.tensor_tensor(TV[:], TV[:], red[:].unsqueeze(2).broadcast_to([P, NT, TOPK]), ALU.mult))
                tv = TV[:].rearrange("p i j -> p (i j)").unsqueeze(2).broadcast_to([P, NT * TOPK, E])
                own_b(v.tensor_tensor(OT.rearrange("p i j e -> p (i j) e"), OH.rearrange("p i j e -> p (i j) e"),
                                      tv, ALU.mult))
                own_b(v.tensor_reduce(RW[:, :, D:D + E], OT.rearrange("p i j e -> p i e j"), AX_X, ALU.add))
                own_b(v.tensor_scalar(RW[:, :, IDCOL].bitcast(I32), TOKI[:, ds(b * NT, NT)], 1.0, None, ALU.mult))
                done(v, "rank_ready", b + 1)
                own_b(v.tensor_tensor(PR[:], PS[:, 4, 0:NT * E].rearrange("p (i e) -> p i e", e=E),
                                      CNT[:].unsqueeze(1).broadcast_to([P, NT, E]), ALU.add))
                own_b(v.tensor_tensor(PR[:], PR[:], const[:, C_BASE:C_BASE + E].unsqueeze(1).broadcast_to([P, NT, E]),
                                      ALU.add))
                own_b(v.tensor_tensor(CNT[:], CNT[:], PS[:, 5, 0:E], ALU.add))
                for j in range(TOPK):
                    own_b(v.tensor_tensor(OT[:, :, j, :], OH[:, :, j, :], PR[:], ALU.mult))
                own_b(v.tensor_reduce(POSF[:], OT, AX_X, ALU.add))
                inc(v.tensor_copy(POS[:], POSF[:]), "routed")
                assert local[0] == PER_BATCH, local[0]

            own(v.tensor_copy(ti32[:], CNT[:]))
            own(v.tensor_scalar(ti32[:], CNT[:], float(P - 1), None, ALU.add))
            own(v.tensor_scalar(ti32[:], ti32[:], 7, None, ALU.arith_shift_right))
            own(v.tensor_copy(nb[:], ti32[:]))
            own(v.tensor_tensor_scan(cum[:], onesE[:], nb[:], 0.0, ALU.mult, ALU.add))
            own(v.tensor_scalar(cum[:], cum[:], float(P), None, ALU.mult))
            blk = const[0:1, C_BLK:C_BLK + NBLK].unsqueeze(2).broadcast_to([1, NBLK, E])
            cumB = cum[0:1, :].unsqueeze(1).broadcast_to([1, BPART, E])
            for part in range(3):
                ks = slice(part * BPART, (part + 1) * BPART)
                own(v.tensor_tensor(cmp, cumB, blk[:, ks], ALU.is_le))
                own(v.tensor_reduce(blkE[:, ks], cmp, AX_X, ALU.add))
                own(v.tensor_tensor(cmp, cmp, cumB, ALU.mult))
                own(v.tensor_reduce(blkC[:, ks], cmp, AX_X, ALU.max))
            own(v.scalar_tensor_tensor(blkR[:], blkE[:], float(CAP), blkC[:], ALU.mult, ALU.subtract))
            own(v.tensor_tensor(blkR[:], blkR[:], const[0:1, C_BLK:C_BLK + NBLK], ALU.add))
            own(v.tensor_scalar(tabR[:], blkR[:], float(E * CAP), None, ALU.min))
            own(v.tensor_scalar(tabE[:], blkE[:], float(E - 1), None, ALU.min))
            own(v.tensor_tensor(padF[:], CNT[0:1, :], const[0:1, C_BASE:C_BASE + E], ALU.add))
            own(v.tensor_copy(padR[:], padF[:]))
            v.sem_inc(table_ready, 1)

            def clip(k, par):
                done(v, "hid_ready", k + 1)
                done(v, "s_ready", k - 1)
                inc(v.tensor_scalar(hA[:, par], PS[:, 2 + par, 0:INNER], LIMIT, None, ALU.min), "lin_ready")
                inc(v.tensor_scalar(hB[:, par], PS[:, 2 + par, INNER:2 * INNER], LIMIT, -LIMIT, ALU.min, ALU.max),
                    "gate_lin_ready")

            def activate(k, par):
                done(v, "sT_ready", k - 1)
                done(v, "gate_lin_ready", k + 1)
                v.scalar_tensor_tensor(hB[:, par], hB[:, par], 1.0, hA[:, par], ALU.add, ALU.mult).then_inc(ordE, 1)
                v.wait_ge(ordE, k + 1)
                done(v, "sig_ready", k + 1)
                inc(v.tensor_tensor(sS[:, par], hB[:, par], hS[:, par], ALU.mult), "s_ready")

            def copy_s(k, par):
                done(v, "sT_ready", k + 1)
                done(v, "y_ready", k - 1)
                inc(v.tensor_copy(sT[:, par], PS[:, 4 + par, 0:D].rearrange("p (c t) -> p c t", c=2)), "sT_copied")

            clip(0, 0)
            activate(0, 0)

            def block_step(k, par):
                clip(k + 1, 1 - par)
                copy_s(k, par)
                activate(k + 1, 1 - par)

            with v.Fori(0, NBLK // 2 - 1) as m:
                block_step(2 * m, 0)
                block_step(2 * m + 1, 1)
            block_step(NBLK - 2, 0)
            copy_s(NBLK - 1, 1)

            for k in range(4):
                v.wait_ge(f_in[k], 16)
                with v.Fori(8 * k, 8 * k + 8) as t:
                    v.bn_stats(tile(ST, t), tile(FS, t)).then_inc(ord3, 1)
            own(aggregate(MV, NTT, ord3, NTT + 2 * B * NT + NTT))
            inverse_root(RS[:], NTT, v.tensor_scalar(tmpS[:], MV[:, :, 1], LN_EPS, None, ALU.add), 9)
            v.scalar_tensor_tensor(NM[:], MV[:, :, 0], -1.0, RS[:], ALU.mult, ALU.mult).then_inc(final_asked, 1)
            with v.Fori(0, NTT) as t:
                v.wait_ge(final_normed, t + 1)
                inc(v.tensor_tensor(tile(FS, t), tile(FS, t), tile(X2, t), ALU.add), "result_ready")

        @block.gpsimd
        def _(pool):
            for n in ("rows_sent", "sum_added"):
                pool.sem_inc(S[n], CREDIT)
            pool.sem_inc(seeded, 1)
            pool.wait_ge(seeded, 5)
            pool.wait_ge(prep, 9)
            with pool.Fori(0, B) as b:
                done(pool, "routed", b + 1)
                met(pool)
                for i in range(NT):
                    for j in range(TOPK):
                        pool.indirect_dma_start(
                            out=lists, out_offset=bass.IndirectOffsetOnAxis(ap=POS[:, i, j:j + 1], axis=0),
                            in_=RW[:, i], in_offset=None).then_inc(sc_out, 16)
                pool.wait_ge(sc_out, 16 * TOPK * NT * (b + 1))
                pool.sem_inc(S["rows_sent"], 1)
            for par in range(2):
                pool.wait_ge(h_out[par], 16 * (NTT // 2 + 1))
            pool.wait_ge(pad_out, 16 * (E + 2))
            with pool.Fori(0, NBLK // RING) as m:
                for slot in range(RING):
                    k = RING * m + slot
                    done(pool, "y_scaled", k + 1)
                    met(pool)
                    pool.indirect_dma_start(
                        out=sums,
                        out_offset=bass.IndirectOffsetOnAxis(ap=XR[:, slot, IDCOL:IDCOL + 1].bitcast(I32), axis=0),
                        in_=YS[:, slot % 2], in_offset=None, compute_op=ALU.add).then_inc(added, 16)
                    pool.wait_ge(added, 16 * k + 16)
                    pool.sem_inc(S["sum_added"], 1)


def kernel(**inputs):
    import concourse.bacc as _bacc
    from concourse.bass_utils import run_bass_kernel_spmd as _run

    nc = _bacc.Bacc("TRN2", target_bir_lowering=False, num_devices=1)
    order = ["L0_attn_x", "L0_attn_norm_w", "L0_attn_Wq", "L0_attn_Wk", "L0_attn_Wv", "L0_attn_Wo", "L0_attn_Wu",
             "L0_ffn_norm_scale", "L0_ffn_wg", "L0_ffn_bg", "L0_ffn_w1", "L0_ffn_b1", "L0_ffn_w2", "L0_ffn_b2"]
    arrays, args = {}, []
    c, fill = constants()
    for name, a in [(n, inputs[n]) for n in order] + [("consts", c), ("fill_rows", fill)]:
        a = np.ascontiguousarray(a)
        arrays[f"in_{name}"] = a
        args.append(nc.dram_tensor(f"in_{name}", a.shape, mybir.dt.from_np(a.dtype), kind="ExternalInput").ap())
    out = nc.dram_tensor("out", (B, T, D), F32, kind="ExternalOutput").ap()
    lists = nc.dram_tensor("lists", (E * CAP + P, ROW), F32, kind="Internal").ap()
    sums = nc.dram_tensor("sums", (B * T + P, D), F32, kind="Internal").ap()
    parts = nc.dram_tensor("bias_parts", (3, E, 3 * INNER), BF16, kind="Internal").ap()
    program(nc, *args, out, lists, sums, parts)
    return _run(nc, [arrays], core_ids=[0]).results[0]["out"]
```

```python
from contextlib import ExitStack

import numpy as np

import concourse.bass as bass
from concourse import mybir

P = 128
F32 = mybir.dt.float32
I32 = mybir.dt.int32
U32 = mybir.dt.uint32
BF16 = mybir.dt.bfloat16
ALU = mybir.AluOpType
ACT = mybir.ActivationFunctionType
AX_X = mybir.AxisListType.X
ds = bass.ds

B, T, D = 2, 2048, 256
H, DK, SEG = 16, 16, 64
NT = T // P
NTT = B * NT
NSEG = T // SEG
DC = D // P
G = 4
HV = DK + 1
HG = H // 2
SW = 2 * HG * HV
RING = 6
E, TOPK, INNER = 16, 4, 256
CAP = B * T + P
NBLK = B * T * TOPK // P + E
IDCOL = D + E
ROW = 276
QT4 = 4
NQ = NT // QT4
SEGT = 4
TURNS = [-(-(2 * i + 1) // SEGT) for i in range(NT)]
NTURN = sum(TURNS)
PER_BATCH = 325
CREDIT = 2
LN_EPS, ATT_RMS_EPS, DEN_EPS, FFN_RMS_EPS = 1e-5, 1e-6, 1e-6, 1e-5
LIMIT, ALPHA = 7.0, 1.702

C_IDENT = 0
C_CAUSAL = C_IDENT + P
C_MEANS = C_CAUSAL + SEG
C_SEGMEAN = C_MEANS + P
C_HEADS = C_SEGMEAN + 2
C_SCORE = C_HEADS + HG * HV
C_BEFORE = C_SCORE + NT * (NSEG + 1)
C_IOTA = C_BEFORE + P
C_BASE = C_IOTA + E
C_TOK = C_BASE + E
C_BLK = C_TOK + NTT
C_ALL = C_BLK + 2


def constants():
    c = np.zeros((P, C_ALL), np.float32)
    p = np.arange(P)
    c[:, C_IDENT:C_IDENT + P] = np.eye(P)
    c[:, C_CAUSAL:C_CAUSAL + SEG] = np.arange(SEG)[None] >= (p % SEG)[:, None]
    same = (p[:, None] // SEG) == (p[None] // SEG)
    c[:, C_MEANS:C_MEANS + P] = same * (p[:, None] <= p[None]) / ((p % SEG)[None] + 1.0)
    c[:, C_SEGMEAN:C_SEGMEAN + 2] = (p[:, None] // SEG == np.arange(2)[None]) / float(SEG)
    c[:, C_HEADS:C_HEADS + HG * HV] = (p[:, None] // DK) == (np.arange(HG * HV)[None] // HV)
    score = np.zeros((P, NT, NSEG + 1), np.float32)
    for i in range(NT):
        seg = 2 * i + p // SEG
        score[:, i, :NSEG] = np.where(seg[:, None] > np.arange(NSEG)[None], 0.0, -1e30)
    c[:, C_SCORE:C_BEFORE] = score.reshape(P, -1)
    c[:, C_BEFORE:C_BEFORE + P] = p[:, None] < p[None]
    c[:, C_IOTA:C_IOTA + E] = np.arange(E)
    c[:, C_BASE:C_BASE + E] = np.arange(E) * CAP
    c[:, C_TOK:C_TOK + NTT] = np.arange(NTT)[None] * P + p[:, None]
    c[:, C_BLK:C_BLK + 2] = (np.arange(2)[None] * P + p[:, None]) * P
    fill = np.zeros((P, ROW), np.int32)
    fill[:, IDCOL] = B * T + p
    return c, fill


def program(nc, x_in, norm_w, Wq, Wk, Wv, Wo, Wu, norm_scale, wg, bg, w1, b1, w2, b2,
            const_in, fill_in, out, lists, sums, parts_dram):
    with ExitStack() as ctx:
        def sb(name, shape, dt=F32):
            return ctx.enter_context(nc.sbuf_tensor(name, shape, dt))

        def sem(name):
            return ctx.enter_context(nc.semaphore(name))

        PS = ctx.enter_context(nc.psum_tensor("PS", [P, 8, 512], F32))
        const = sb("const", [P, C_ALL])
        fill = sb("fill", [P, ROW], I32)
        ident = const[:, C_IDENT:C_IDENT + P]
        X2 = sb("X2", [P, NTT, D])
        XO = sb("XO", [P, NT, D])
        arena = sb("arena", [P, 24576])
        PQT = arena[:, 0:4096].rearrange("p (i c t) -> p i c t", i=NT, c=2)
        SB = arena[:, 4096:4096 + NSEG * SW].rearrange("p (n c w) -> p n c w", n=NSEG, c=2)
        W1 = arena[:, 0:16384].rearrange("p (e c n) -> p e c n", e=E, c=DC)
        FS = arena[:, 0:NTT * D].rearrange("p (t d) -> p t d", t=NTT)
        W2 = arena[:, 16384:24576].rearrange("p (e c n) -> p e c n", e=E, c=DC)
        spare = [4096 + NSEG * SW]

        def early(shape):
            n = int(np.prod(shape))
            view = arena[:, spare[0]:spare[0] + n]
            spare[0] += n
            assert spare[0] <= 24576
            names = " ".join("abcd"[:len(shape)])
            return view.rearrange(f"p ({names}) -> p {names}", **dict(zip("abcd", shape)))

        SC = early([NT, NSEG + 1])
        WT = early([DC, 4 * D])
        WoT = early([DC, D])
        Wun = early([DC, D])
        wraw = arena[:, 0:2048].rearrange("p (k c d) -> p k c d", k=4, c=DC)
        nw = sb("nw", [P, DC])
        nsB = sb("nsB", [P, D])
        wgS = sb("wgS", [P, DC, E])
        bgB = sb("bgB", [P, E])
        zeros = early([SW])
        MV = sb("MV", [P, NTT, 2])
        RS = sb("RS", [P, NTT])
        RR = sb("RR", [P, NTT])
        tmpS = sb("tmpS", [P, NTT])
        sqS = sb("sqS", [P, NTT])
        XS = sb("XS", [P, 2, D])
        MT = early([DC, NSEG])
        VM = early([DC, NSEG])
        XT = sb("XT", [P, 2, DC, P])
        MC = sb("MC", [P, 2, D])
        EX = sb("EX", [P, 2, 2 * D])
        RL = sb("RL", [P, 2, 2 * D])
        PF = sb("PF", [P, 2, 2, H, 32])
        V1 = sb("V1", [P, 2, H, HV])
        QT = sb("QT", [P, 2, G, P])
        F2 = early([2, 2, D])
        Q2 = early([2, 2, P])
        KT = early([2, G, P])
        AM = early([2, G * G, SEG]).rearrange("p b (j g) c -> p b j g c", j=G)
        SX = early([4, 2, HG * HV])
        AN = sb("AN", [P, 2, D])
        rden = sb("rden", [P, 2, H])
        ANT = early([2, DC, P])
        SCS = early([2, NSEG + 1])
        red = sb("red", [P, NT])
        MV2 = sb("MV2", [P, NT, 2])
        RS2 = sb("RS2", [P, NT])
        RR2 = sb("RR2", [P, NT])
        NM = sb("NM", [P, NTT])
        LG = sb("LG", [P, QT4, E])
        M8 = sb("M8", [P, QT4, 8])
        I8 = sb("I8", [P, QT4, 8], U32)
        TV = sb("TV", [P, QT4, TOPK])
        TI = sb("TI", [P, QT4, TOPK])
        HN = EX[:].rearrange("p b (k d) -> p (b k) d", d=D)
        XNT = QT[:].rearrange("p b g t -> p (b g t)").rearrange("p (i c t) -> p i c t", i=QT4, c=DC)
        RLf = RL[:].rearrange("p b w -> p (b w)")
        OH = RLf[:, 0:QT4 * TOPK * E].rearrange("p (i j e) -> p i j e", j=TOPK, e=E)
        OT = RLf[:, 256:256 + QT4 * TOPK * E].rearrange("p (i j e) -> p i j e", j=TOPK, e=E)
        ST = RLf[:, 512:512 + 6 * NTT].rearrange("p (t s) -> p t s", t=NTT)
        MK = sb("MK", [P, QT4, E])
        MKb = sb("MKb", [P, QT4, E], BF16)
        beforeB = sb("beforeB", [P, P], BF16)
        onesB = sb("onesB", [P, P], BF16)
        PR = sb("PR", [P, QT4, E])
        CNT = sb("CNT", [P, E])
        POSF = sb("POSF", [P, QT4, TOPK])
        POS = sb("POS", [P, NT, TOPK], I32)
        TOKI = sb("TOKI", [P, NTT], I32)
        RW = sb("RW", [P, NT, ROW])
        XR = RW[:, 0:RING]
        ti32 = sb("ti32", [P, E], I32)
        nb = sb("nb", [P, E])
        cum = sb("cum", [P, E])
        onesE = sb("onesE", [P, E])
        cmp = sb("cmp", [P, 2, E])
        cmq = sb("cmq", [P, 2, E])
        blkE, blkC, blkR = sb("blkE", [P, 2]), sb("blkC", [P, 2]), sb("blkR", [P, 2])
        early_W1 = -(-(4096 + NSEG * SW + NT * (NSEG + 1)) // (DC * 2 * INNER))
        tabE = sb("tabE", [1, NBLK], I32)
        tabR = sb("tabR", [1, NBLK], I32)
        padF = sb("padF", [1, E])
        padR = sb("padR", [1, E], I32)
        b1s = arena[0:E, 6144:6144 + 2 * INNER]
        b2s = arena[0:E, 7168:7168 + D]
        bh = arena[0:E, 2048:2048 + 1152].bitcast(BF16).rearrange("e (k n) -> e k n", k=3)
        bres = arena[0:E, 4096:4096 + 1536].rearrange("e (k n) -> e k n", k=2)
        b1h = XO[0:3].rearrange("k i d -> k (i d)").bitcast(BF16).rearrange("k (e n) -> k e n", e=E)
        b2h = PF[0:3].rearrange("k a b h w -> k (a b h w)").bitcast(BF16).rearrange("k (e n) -> k e n", e=E)
        XRT = QT[:].rearrange("p b g t -> p b (g t)")[:, :, 0:D].rearrange("p b (c t) -> p b c t", c=DC)
        sT = QT[:].rearrange("p b g t -> p b (g t)")[:, :, D:2 * D].rearrange("p b (c t) -> p b c t", c=DC)
        hA, hS = EX[:, :, 0:INNER], EX[:, :, INNER:2 * INNER]
        hB, sS = RL[:, :, 0:INNER], RL[:, :, INNER:2 * INNER]
        YS = AN

        (const_in_s, weights_in, x_in_s, bias_in, small_in) = map(
            sem, ("const_loaded", "weights_loaded", "x_loaded", "bias_loaded", "small_loaded"))
        wt_ready, wt_copied = sem("wt_ready"), sem("wt_copied")
        prep, sqrt_asked, sqrt_done = sem("prep_done"), sem("sqrt_asked"), sem("sqrt_done")
        dve = sem("dve_order")
        names = ("xs0_ready", "mean_ready", "mean_copied", "vm_ready", "vm_copied",
                 "xs_ready", "front_T_ready", "xT_copied", "mcur_copied", "proj_ready", "exp_done",
                 "relu_done", "v_copied", "score_taken", "feat_ready", "qkT_ready", "qT_copied",
                 "kT_copied", "q_stored", "state0_ready", "state0_kept", "scores_ready", "masked",
                 "raw_score_ready", "raw_score_read", "state1_ready", "state1_kept", "states_stored", "attn_ready", "attn_normed",
                 "attnT_ready", "attnT_copied", "wo_ready", "xo_done", "score_stored",
                 "gate_arg", "gate_exp", "gates_ready", "z_ready", "z_used", "combined",
                 "xn_ready", "xnT_ready", "xnT_copied", "sum_asked", "sum_normed", "q2_kept", "roots_ready", "rows_sent", "logit_ready", "logit_used",
                 "h_ready", "top_arg", "top_exp", "mask_ready", "rank_ready", "routed")
        S = {n: sem(n) for n in names}
        h_out = sem("h_stored")
        sc_out = sem("scattered")
        pad_out, table_ready = sem("fill_stored"), sem("table_ready")
        blocks_ready, blocks_T_ready = sem("blocks_ready"), sem("blocks_T_ready")
        w_in = [sem("expert_weights_even"), sem("expert_weights_odd")]
        biasq = sem("bias_parts")
        biasd = sem("bias_moved")
        xr_in = [sem(f"rows_loaded_{k}") for k in range(RING)]
        enames = ("xrT_ready", "xrT_copied", "hid_ready", "lin_ready", "sig_ready", "gate_lin_ready",
                  "s_ready", "sT_ready", "sT_copied", "y_ready", "y_scaled", "sum_added", "result_ready")
        S.update({n: sem(n) for n in enames})
        added = sem("block_added")
        f_in = [sem(f"sums_loaded_{k}") for k in range(4)]
        fout = sem("out_stored")
        seeded = sem("seeded")
        ordD, ordB = sem("order_den"), sem("order_batch")
        ord3, ord4, ord5 = sem("order_stats"), sem("order_sum"), sem("order_top")
        ordE, final_asked, final_normed = sem("order_expert"), sem("final_roots"), sem("final_normed")
        turns = sem("waits_met")

        def met(eng):
            eng.sem_inc(turns, 1)


        def done(eng, name, count):
            eng.wait_ge(S[name], count + CREDIT)

        def inc(ins, name):
            return ins.then_inc(S[name], 1)

        x_v = x_in.rearrange("b (i p) d -> p (b i) d", p=P)
        out_v = out.rearrange("b (i p) d -> (b i p) d", p=P)
        block = ctx.enter_context(nc.Block())

        def steps(eng, step):
            step(0, 0)
            step(1, 1)
            with eng.Fori(1, NT // 2 - 1) as m:
                for par in range(2):
                    step(2 * m + par, par, True)
            for s in range(NT - 2, NT + 2):
                step(s, s % 2)

        def parts(s, inner):
            if inner:
                return True, True, True, True
            return s + 1 < NT, s < NT, 1 <= s <= NT, 2 <= s

        def store_fill(eng, first, last):
            with eng.Fori(first // 4, last // 4) as m:
                for k in range(4):
                    row = eng.value_load(padR[0:1, ds(4 * m + k, 1)], min_val=0, max_val=E * CAP - P)
                    eng.dma_start(lists[ds(row, P), :], fill[:].bitcast(F32)).then_inc(pad_out, 16)

        @block.sync
        def _(sp):
            sp.dma_start(const[:], const_in).then_inc(const_in_s, 16)
            for b in range(B):
                if b:
                    sp.wait_ge(x_in_s, 16 * b)
                sp.dma_start(X2[:, NT * b:NT * (b + 1), :], x_v[:, NT * b:NT * (b + 1), :]).then_inc(x_in_s, 16)
                if b == 0:
                    for k, w in enumerate((Wq, Wk, Wv, Wo)):
                        sp.dma_start(wraw[:, k], w.rearrange("(c p) d -> p c d", p=P)).then_inc(weights_in, 16)
                    sp.dma_start(Wun[:], Wu.rearrange("(c p) d -> p c d", p=P)).then_inc(weights_in, 16)
                    with nc.allow_non_contiguous_dma(reason="256 numbers, once"):
                        sp.dma_start(nw[:], norm_w.rearrange("(c p) -> p c", p=P)).then_inc(weights_in, 16)
            sp.dma_start(nsB[:], norm_scale.partition_broadcast(P)).then_inc(small_in, 16)
            sp.dma_start(bgB[:], bg.partition_broadcast(P)).then_inc(small_in, 16)
            sp.dma_start(wgS[:], wg.rearrange("(c p) e -> p c e", p=P)).then_inc(small_in, 16)
            sp.dma_start(fill[:], fill_in).then_inc(small_in, 16)
            sp.dma_start(b1s[:], b1).then_inc(bias_in, 16)
            sp.dma_start(b2s[:], b2).then_inc(bias_in, 16)
            sp.wait_ge(biasq, 5)
            sp.dma_start(parts_dram.rearrange("k e n -> e k n"), bh).then_inc(biasd, 16)
            sp.wait_ge(biasd, 16)
            sp.dma_start(sums[B * T:B * T + P, :], nsB[:]).then_inc(pad_out, 16)
            def store_normed(n):
                t = n * QT4
                done(sp, "h_ready", t + QT4)
                sp.dma_start(sums[ds(t * P, QT4 * P), :].rearrange("(t p) d -> p t d", p=P), HN).then_inc(h_out, 16)

            with sp.Fori(0, (B - 1) * NQ) as n:
                store_normed(n)
            def load_weights(n, dst, src):
                if n >= 2:
                    sp.wait_ge(w_in[n % 2], 16 * (n // 2))
                sp.dma_start(dst, src.rearrange("(c p) n -> p c n", p=P)).then_inc(w_in[n % 2], 16)

            done(sp, "gates_ready", B)
            done(sp, "xo_done", B * NT)
            done(sp, "states_stored", B * NT)
            done(sp, "q_stored", B * NT)
            for e in range(E):
                load_weights(e, W2[:, e], w2[e])
            for n, e in enumerate(range(early_W1, E)):
                load_weights(E + n, W1[:, e], w1[e])
            with sp.Fori((B - 1) * NQ, B * NQ - 1) as n:
                store_normed(n)
            done(sp, "combined", B)
            for e in range(early_W1):
                load_weights(2 * E - early_W1 + e, W1[:, e], w1[e])
            store_normed(B * NQ - 1)
            done(sp, "xnT_copied", B * NT // 2)
            sp.dma_start(b1h, parts_dram[:, :, 0:2 * INNER]).then_inc(biasd, 16)
            sp.dma_start(b2h, parts_dram[:, :, 2 * INNER:3 * INNER]).then_inc(biasd, 16)
            sp.wait_ge(table_ready, 1)
            sp.wait_ge(small_in, 64)
            sp.dma_start(lists[E * CAP:E * CAP + P, :], fill[:].bitcast(F32)).then_inc(pad_out, 16)
            store_fill(sp, 0, E // 2)
            sp.wait_ge(pad_out, 16 * (E + 2))
            sp.wait_ge(sc_out, 16 * TOPK * NTT)

            def load_rows(k, slot):
                row = sp.value_load(tabR[0:1, ds(k, 1)], min_val=0, max_val=E * CAP)
                sp.dma_start(XR[:, slot], lists[ds(row, P), :]).then_inc(xr_in[slot], 16)

            for k in range(RING):
                load_rows(k, k)
            with sp.Fori(1, NBLK // RING) as m:
                for slot in range(RING):
                    done(sp, "sum_added", RING * m + slot - RING + 1)
                    load_rows(RING * m + slot, slot)
            done(sp, "sum_added", NBLK)
            for k in range(4):
                sp.dma_start(FS[:, 8 * k:8 * k + 8, :], sums[8 * k * P:8 * (k + 1) * P, :].rearrange(
                    "(t p) d -> p t d", p=P)).then_inc(f_in[k], 16)
            for m in range(NTT // 4):
                done(sp, "result_ready", 4 * m + 4)
                sp.dma_start(out_v[4 * m * P:4 * (m + 1) * P, :].rearrange("(t p) d -> p t d", p=P),
                             FS[:, 4 * m:4 * m + 4]).then_inc(fout, 16)
            sp.wait_ge(fout, 16 * (NTT // 4))

        @block.tensor
        def _(pe):
            for n in ("mean_ready", "vm_ready", "front_T_ready", "proj_ready", "qkT_ready", "state0_ready",
                      "state1_ready", "raw_score_ready", "scores_ready", "attn_ready", "attnT_ready", "wo_ready", "z_ready",
                      "xnT_ready", "logit_ready", "rank_ready", "xrT_ready", "hid_ready", "sT_ready", "y_ready"):
                pe.sem_inc(S[n], CREDIT)
            pe.sem_inc(seeded, 1)
            pe.wait_ge(seeded, 5)
            pe.wait_ge(const_in_s, 16)
            pe.wait_ge(weights_in, 96)
            for k in range(5):
                for oc in range(DC):
                    for c in range(DC):
                        w = Wun[:, oc, c * P:(c + 1) * P] if k == 4 else wraw[:, k, oc, c * P:(c + 1) * P]
                        last = pe.transpose(PS[:, k, c * D + oc * P:c * D + (oc + 1) * P], w, ident)
                last.then_inc(wt_ready, 1)
            pe.wait_ge(wt_copied, 5 * DC)

            def pass0(b):
                for i in range(NT):
                    done(pe, "xs0_ready", b * NT + i + 1)
                    for c in range(DC):
                        last = pe.matmul(PS[:, c, 2 * i:2 * i + 2], lhsT=XO[:, i, c * P:(c + 1) * P],
                                         rhs=const[:, C_SEGMEAN:C_SEGMEAN + 2], start=True, stop=True)
                inc(last, "mean_ready")
                done(pe, "mean_copied", b + 1)
                for c in range(DC):
                    for oc in range(DC):
                        last = pe.matmul(PS[:, 2, c * NSEG:(c + 1) * NSEG], lhsT=Wun[:, oc, c * P:(c + 1) * P],
                                         rhs=MT[:, oc, :], start=(oc == 0), stop=(oc == DC - 1))
                inc(last, "vm_ready")
                done(pe, "vm_copied", b + 1)
                pe.matmul(PS[:, 7, 0:SW], lhsT=zeros[:, 0:P], rhs=zeros[:], start=True, stop=False,
                          skip_group_check=True)

            def front_T(b, s, p):
                done(pe, "xs_ready", b * NT + s + 1)
                done(pe, "masked", b * NT + s - 1)
                for c in range(DC):
                    pe.transpose(PS[:, 2, c * P:(c + 1) * P], XS[:, p, c * P:(c + 1) * P], ident)
                inc(pe.matmul(PS[:, 2, D:2 * D], lhsT=const[:, C_MEANS:C_MEANS + P], rhs=XS[:, p],
                              start=True, stop=True), "front_T_ready")

            def project(b, s, p):
                t = b * NT + s
                done(pe, "xT_copied", t + 1)
                done(pe, "exp_done", t)
                done(pe, "relu_done", t)
                if not isinstance(s, int) or s >= 3:
                    done(pe, "xo_done", t - 2)
                done(pe, "v_copied", t)
                done(pe, "score_taken", t)
                done(pe, "attn_normed", t - 1)
                for c in range(DC):
                    last = pe.matmul(PS[:, 6, 272:272 + NSEG], lhsT=XT[:, p, c, :], rhs=VM[:, c, :],
                                     start=(c == 0), stop=(c == DC - 1))
                inc(last, "raw_score_ready")
                for half in range(2):
                    for c in range(DC):
                        last = pe.matmul(PS[:, 4 + half, :], lhsT=XT[:, p, c, :], rhs=WT[:, c, half * 512:half * 512 + 512],
                                  start=(c == 0), stop=(c == DC - 1))
                inc(last, "proj_ready")

            def features_T(b, s, p):
                t = b * NT + s
                done(pe, "feat_ready", t + 1)
                done(pe, "masked", t)
                for k in range(2):
                    for g in range(G):
                        pe.transpose(PS[:, k, g * P:(g + 1) * P],
                                     PF[:, p, k, 4 * g:4 * g + 4, :].rearrange("p h k -> p (h k)"), ident)
                for c in range(2):
                    last = pe.transpose(PS[:, 3, D + c * P:D + (c + 1) * P], F2[:, p, 0, c * P:(c + 1) * P], ident)
                inc(last, "qkT_ready")

            def state(b, s, p, seg):
                rows = slice(SEG * seg, SEG * seg + SEG)
                for c in range(2):
                    last = pe.matmul(PS[:, 7, c * HG * HV:(c + 1) * HG * HV],
                                     lhsT=F2[rows, p, 1, c * P:(c + 1) * P],
                                     rhs=V1[rows, p, HG * c:HG * (c + 1), :].rearrange("p h k -> p (h k)"),
                                     start=False, stop=False, skip_group_check=True)
                inc(last, f"state{seg}_ready")

            def scores(b, s, p):
                t = b * NT + s
                done(pe, "v_copied", t + 1)
                done(pe, "state1_kept", t)
                state(b, s, p, 0)
                done(pe, "qT_copied", t + 1)
                done(pe, "kT_copied", t + 1)
                done(pe, "q2_kept", t + 1)
                done(pe, "attnT_copied", t)
                for g in range(G):
                    for seg in range(2):
                        for j in range(G):
                            rows = slice(32 * j, 32 * j + 32)
                            toks = slice(SEG * seg, SEG * seg + SEG)
                            last = pe.matmul(PS[toks, j, g * SEG:(g + 1) * SEG], lhsT=KT[rows, p, g, toks],
                                             rhs=QT[rows, p, g, toks], start=True, stop=True,
                                             skip_group_check=True)
                inc(last, "scores_ready")
                done(pe, "state0_kept", t + 1)
                state(b, s, p, 1)

            def attend(b, s, p, front):
                t = b * NT + s
                done(pe, "attn_normed", t)
                done(pe, "masked", t + 1)
                done(pe, "raw_score_read", t + 2 if front else t + 1)
                for seg in range(2):
                    toks = slice(SEG * seg, SEG * seg + SEG)
                    slot = (2 * p + seg - 1) % 4
                    for c in range(2):
                        pe.matmul(PS[toks, 6, c * HG * HV:(c + 1) * HG * HV], lhsT=Q2[:, p, c, toks],
                                  rhs=SX[:, slot, c, :], start=(c == 0), stop=False, skip_group_check=True)
                    for h in range(H):
                        last = pe.matmul(PS[toks, 6, h * HV:(h + 1) * HV], lhsT=AM[toks, p, h % G, h // G, :],
                                         rhs=V1[toks, p, h, :], start=False, stop=True, skip_group_check=True)
                inc(last, "attn_ready")

            def attended_T(b, s, p):
                done(pe, "attn_normed", b * NT + s + 1)
                for c in range(DC):
                    last = pe.transpose(PS[:, 3, c * P:(c + 1) * P], AN[:, p, c * P:(c + 1) * P], ident)
                inc(last, "attnT_ready")

            def out_proj(b, s, p):
                done(pe, "attnT_copied", b * NT + s + 1)
                for c in range(DC):
                    last = pe.matmul(PS[:, 4, 0:D], lhsT=ANT[:, p, c, :], rhs=WoT[:, c, :],
                                     start=(c == 0), stop=(c == DC - 1))
                inc(last, "wo_ready")

            def normed_T(b, q):
                done(pe, "routed", b * NQ + q)
                for pair in range(2):
                    i = QT4 * q + 2 * pair
                    done(pe, "xn_ready", b * NT + i + 2)
                    for k in range(2):
                        for c in range(DC):
                            last = pe.transpose(PS[:, 6 + pair, k * D + c * P:k * D + (c + 1) * P],
                                                RW[:, i + k, c * P:(c + 1) * P], ident)
                    inc(last, "xnT_ready")

            def logits(b, q):
                for pair in range(2):
                    done(pe, "xnT_copied", (b * NQ + q) * 2 + pair + 1)
                    for k in range(2):
                        for c in range(DC):
                            last = pe.matmul(PS[:, 6 + pair, k * E:(k + 1) * E], lhsT=XNT[:, 2 * pair + k, c, :],
                                             rhs=wgS[:, c, :], start=(c == 0), stop=(c == DC - 1))
                    inc(last, "logit_ready")

            def ranks(b, q):
                done(pe, "mask_ready", b * NQ + q + 1)
                pe.matmul(PS[:, 6, 0:QT4 * E], lhsT=beforeB[:], rhs=MKb[:].rearrange("p i e -> p (i e)"),
                          start=True, stop=False, skip_group_check=True)
                for i in range(QT4 - 1):
                    pe.matmul(PS[:, 6, (i + 1) * E:QT4 * E].rearrange("p (i e) -> p i e", e=E), lhsT=onesB[:],
                              rhs=MKb[:, i:i + 1, :].broadcast_to([P, QT4 - 1 - i, E]),
                              start=False, stop=False, skip_group_check=True)
                for i in range(QT4):
                    last = pe.matmul(PS[:, 7, 0:E], lhsT=onesB[:], rhs=MKb[:, i, :], start=(i == 0),
                                     stop=(i == QT4 - 1))
                inc(last, "rank_ready")

            with pe.Fori(0, B) as b:
                pass0(b)

                def step(s, par, inner=False):
                    n, f, k, w = parts(s, inner)
                    if f:
                        project(b, s, par)
                    if k:
                        if f:
                            done(pe, "xT_copied", b * NT + s + 1)
                            done(pe, "mcur_copied", b * NT + s + 1)
                        scores(b, s - 1, 1 - par)
                    if w:
                        if f:
                            done(pe, "exp_done", b * NT + s + 1)
                            done(pe, "relu_done", b * NT + s + 1)
                        out_proj(b, s - 2, par)
                    if n:
                        front_T(b, s + 1, 1 - par)
                    if k:
                        attend(b, s - 1, 1 - par, f)
                    if f:
                        features_T(b, s, par)
                    if k:
                        attended_T(b, s - 1, 1 - par)

                front_T(b, 0, 0)
                steps(pe, step)
                done(pe, "gates_ready", b + 1)
                done(pe, "q_stored", (b + 1) * NT)
                done(pe, "states_stored", (b + 1) * NT)
                done(pe, "xo_done", (b + 1) * NT)
                turn = 0
                for i in range(NT):
                    q = i // QT4 - 1
                    routing = q >= 0 and i % QT4 == QT4 - 1
                    for k in range(TURNS[i]):
                        if turn >= 3:
                            done(pe, "z_used", b * NTURN + turn - 2)
                        for c in range(2):
                            last = pe.matmul(PS[:, 2 * (turn % 3) + c, :], lhsT=PQT[:, i, c, :],
                                             rhs=SB[:, SEGT * k:SEGT * (k + 1), c, :].rearrange(
                                                 "p n (h v) -> p n h v", h=HG)[:, :, :, 0:DK],
                                             start=True, stop=True)
                        inc(last, "z_ready")
                        turn += 1
                        if routing and k == 0:
                            normed_T(b, q)
                        if routing and k == 1:
                            logits(b, q)
                    if routing:
                        ranks(b, q)
                normed_T(b, NQ - 1)
                logits(b, NQ - 1)
                ranks(b, NQ - 1)
                done(pe, "z_used", (b + 1) * NTURN)
                done(pe, "routed", (b + 1) * NQ)

            pe.wait_ge(blocks_ready, 1)
            for k, column in enumerate((blkR[:, 0:1], blkR[:, 1:2], blkE[:, 0:1], blkE[:, 1:2])):
                last = pe.transpose(PS[0:1, 0, k * P:(k + 1) * P], column, ident)
            last.then_inc(blocks_T_ready, 1)

            pe.wait_ge(biasd, 48)
            pe.wait_ge(table_ready, 1)

            def turn_rows(k, m, slot):
                par = slot % 2
                pe.wait_ge(xr_in[slot], 16 * m + 16)
                done(pe, "xrT_copied", k - 1)
                for c in range(DC):
                    last = pe.transpose(PS[:, par, c * P:(c + 1) * P], XR[:, slot, c * P:(c + 1) * P], ident)
                inc(last, "xrT_ready")

            def hidden(k, par):
                e = pe.value_load(tabE[0:1, ds(k, 1)], min_val=0, max_val=E - 1)
                done(pe, "xrT_copied", k + 1)
                done(pe, "gate_lin_ready", k - 1)
                done(pe, "lin_ready", k - 1)
                w = arena[:, ds(e * 1024, 1024)].rearrange("p (c f two) -> p c two f", c=DC, two=2)
                for c in range(DC):
                    pe.matmul(PS[:, 2 + par, :], lhsT=XRT[:, par, c, :], rhs=w[:, c], start=(c == 0), stop=False)
                bias = b1h.rearrange("k e n -> k (e n)")[:, ds(e * 512, 512)].rearrange("k (f two) -> k two f", two=2)
                inc(pe.matmul(PS[:, 2 + par, :], lhsT=onesB[0:3, :], rhs=bias, start=False, stop=True), "hid_ready")

            def turn_s(k, par):
                done(pe, "s_ready", k + 1)
                done(pe, "sT_copied", k - 1)
                for c in range(2):
                    last = pe.transpose(PS[:, 4 + par, c * P:(c + 1) * P], sS[:, par, c * P:(c + 1) * P], ident)
                inc(last, "sT_ready")

            def expert_out(k, par):
                e = pe.value_load(tabE[0:1, ds(k, 1)], min_val=0, max_val=E - 1)
                done(pe, "sT_copied", k + 1)
                done(pe, "y_scaled", k - 1)
                for c in range(2):
                    pe.matmul(PS[:, 6 + par, 0:D], lhsT=sT[:, par, c, :],
                              rhs=arena[:, ds(e * 512 + (16384 + c * D), D)], start=(c == 0), stop=False)
                inc(pe.matmul(PS[:, 6 + par, 0:D], lhsT=onesB[0:3, :],
                              rhs=b2h.rearrange("k e n -> k (e n)")[:, ds(e * D, D)], start=False, stop=True),
                    "y_ready")

            for par in range(2):
                pe.wait_ge(w_in[par], 16 * E)
            def block_step(k, m, j, inner=False):
                if inner or k + 1 < NBLK:
                    hidden(k + 1, (j + 1) % 2)
                turn_s(k, j % 2)
                if inner or k + 2 < NBLK:
                    turn_rows(k + 2, m + (j + 2) // RING, (j + 2) % RING)
                if inner or k >= 1:
                    expert_out(k - 1, (j + 1) % 2)

            turn_rows(0, 0, 0)
            turn_rows(1, 0, 1)
            hidden(0, 0)
            for j in range(RING):
                block_step(j, 0, j)
            with pe.Fori(1, NBLK // RING - 1) as m:
                for j in range(RING):
                    block_step(RING * m + j, m, j, True)
            for j in range(RING):
                block_step(NBLK - RING + j, NBLK // RING - 1, j)
            expert_out(NBLK - 1, 1)

        @block.scalar
        def _(act):
            for n in ("xT_copied", "mcur_copied", "exp_done", "relu_done", "v_copied", "kT_copied", "attnT_copied",
                      "gate_exp", "xnT_copied", "h_ready", "sum_normed", "q2_kept", "states_stored", "q_stored", "top_exp", "xrT_copied", "sig_ready", "y_scaled"):
                act.sem_inc(S[n], CREDIT)
            act.sem_inc(seeded, 1)
            act.wait_ge(seeded, 5)

            def root(asked, n):
                act.wait_ge(sqrt_asked, asked)
                nc.scalar.activation(sqS[:, 0:n], tmpS[:, 0:n], ACT.Sqrt).then_inc(sqrt_done, 1)

            root(1, NTT)
            root(2, NTT)

            with act.Fori(0, B) as b:
                def enter(s, par):
                    t = b * NT + s
                    done(act, "front_T_ready", t + 1)
                    done(act, "proj_ready", t - 1)
                    inc(nc.scalar.copy(XT[:, par], PS[:, 2, 0:D].rearrange("p (c t) -> p c t", c=DC)), "xT_copied")
                    done(act, "score_taken", t - 1)
                    inc(nc.scalar.copy(MC[:, par], PS[:, 2, D:2 * D]), "mcur_copied")

                def step(s, par, inner=False):
                    n, f, k, w = parts(s, inner)
                    t = b * NT + s
                    if f:
                        done(act, "proj_ready", t + 1)
                        done(act, "feat_ready", t - 1)
                        met(act)
                        r = RR[:, ds(t, 1)]
                        inc(nc.scalar.activation(EX[:, par], PS[:, 4, :], ACT.Exp, scale=r), "exp_done")
                        inc(nc.scalar.activation(RL[:, par], PS[:, 4, :], ACT.Relu, scale=r), "relu_done")
                        done(act, "score_taken", t + 1)
                        done(act, "attn_ready", t - 1)
                        met(act)
                        inc(nc.scalar.activation(V1[:, par, :, 0:DK], PS[:, 5, 0:D].rearrange("p (h v) -> p h v", h=H),
                                                 ACT.Copy, scale=r), "v_copied")
                    if n:
                        enter(s + 1, 1 - par)
                    if f:
                        done(act, "qkT_ready", t + 1)
                        done(act, "scores_ready", t - 1)
                        done(act, "attn_ready", t - 1)
                        inc(nc.scalar.copy(KT[:, par], PS[:, 1, :].rearrange("p (g t) -> p g t", g=G)), "kT_copied")
                        if k:
                            done(act, "attnT_ready", t)
                        inc(nc.scalar.copy(Q2[:, par], PS[:, 3, D:2 * D].rearrange("p (c t) -> p c t", c=2)), "q2_kept")
                    if k:
                        done(act, "attnT_ready", t)
                        done(act, "state1_kept", t)
                        done(act, "wo_ready", t - 2)
                        inc(nc.scalar.copy(ANT[:, 1 - par], PS[:, 3, 0:D].rearrange("p (c t) -> p c t", c=DC)),
                            "attnT_copied")
                        met(act)
                        inc(nc.scalar.copy(arena[:, ds((s - 1) * (2 * SW) + 4096, 2 * SW)],
                                           SX[:, 2 - 2 * par:4 - 2 * par].rearrange("p s c w -> p (s c w)")),
                            "states_stored")
                    if f:
                        done(act, "q2_kept", t + 1)
                        met(act)
                        inc(nc.scalar.copy(arena[:, ds(s * D, D)], Q2[:, par].rearrange("p c t -> p (c t)")),
                            "q_stored")

                act.wait_ge(biasd, 16)
                enter(0, 0)
                steps(act, step)
                done(act, "gate_arg", b + 1)
                inc(nc.scalar.activation(SC[:], SC[:], ACT.Exp), "gate_exp")

                def scaled(i, dst, src):
                    return nc.scalar.activation(dst, src, ACT.Identity, scale=RS2[:, i:i + 1], bias=NM[:, i:i + 1])

                for q in range(NQ):
                    n = b * NQ + q
                    tiles = range(QT4 * q, QT4 * q + QT4)
                    root(3 * n + 3, QT4)
                    done(act, "sum_asked", n + 1)
                    met(act)
                    for i in tiles:
                        inc(scaled(i, XO[:, i, :], XO[:, i, :]), "sum_normed")
                    root(3 * n + 4, QT4)
                    root(3 * n + 5, QT4)
                    done(act, "roots_ready", n + 1)
                    act.wait_ge(h_out, 16 * n + 16)
                    done(act, "xn_ready", b * NT + QT4 * q)
                    met(act)
                    for i in tiles:
                        inc(scaled(i, HN[:, i % QT4], X2[:, ds(b * NT + i, 1), :].rearrange("p o d -> p (o d)")), "h_ready")
                    for pair in range(2):
                        done(act, "xnT_ready", 2 * n + pair + 1)
                        done(act, "logit_ready", 2 * n)
                        inc(nc.scalar.copy(XNT[:, 2 * pair:2 * pair + 2].rearrange("p i c t -> p (i c t)"),
                                           PS[:, 6 + pair, :]), "xnT_copied")
                    done(act, "top_arg", n + 1)
                    inc(nc.scalar.activation(TV[:], TV[:], ACT.Exp), "top_exp")
                act.wait_ge(h_out, 16 * NQ * (b + 1) + 16)
                met(act)

            act.wait_ge(table_ready, 1)
            act.wait_ge(small_in, 64)
            store_fill(act, E // 2, E)


            def copy_rows(k, par):
                done(act, "xrT_ready", k + 1)
                done(act, "hid_ready", k - 1)
                inc(nc.scalar.copy(XRT[:, par], PS[:, par, 0:D].rearrange("p (c t) -> p c t", c=DC)), "xrT_copied")

            def sigmoid(k, par):
                done(act, "lin_ready", k + 1)
                done(act, "s_ready", k - 1)
                inc(nc.scalar.activation(hS[:, par], hA[:, par], ACT.Sigmoid, scale=ALPHA), "sig_ready")

            def scale_out(k, slot):
                par = slot % 2
                e = act.value_load(tabE[0:1, ds(k, 1)], min_val=0, max_val=E - 1)
                done(act, "y_ready", k + 1)
                done(act, "sum_added", k - 1)
                met(act)
                inc(nc.scalar.activation(YS[:, par], PS[:, 6 + par, 0:D], ACT.Copy,
                                         scale=XR[:, slot, ds(e + D, 1)]), "y_scaled")

            def block_step(k, j, inner=False):
                if inner or k + 1 < NBLK:
                    sigmoid(k + 1, (j + 1) % 2)
                if inner or k + 2 < NBLK:
                    copy_rows(k + 2, j % 2)
                if inner or k >= 1:
                    scale_out(k - 1, (j - 1) % RING)

            copy_rows(0, 0)
            copy_rows(1, 1)
            sigmoid(0, 0)
            for j in range(RING):
                block_step(j, j)
            with act.Fori(1, NBLK // RING - 1) as m:
                for j in range(RING):
                    block_step(RING * m + j, j, True)
            for j in range(RING):
                block_step(NBLK - RING + j, j)
            scale_out(NBLK - 1, RING - 1)
            for k in range(4):
                at = slice(8 * k, 8 * k + 8)
                act.wait_ge(sqrt_asked, 3 * B * NQ + 3 + k)
                nc.scalar.activation(sqS[:, at], tmpS[:, at], ACT.Sqrt).then_inc(sqrt_done, 1)
                act.wait_ge(final_asked, k + 1)
                for t in range(8 * k, 8 * k + 6):
                    nc.scalar.activation(FS[:, t], FS[:, t], ACT.Identity, scale=RS[:, t:t + 1],
                                         bias=NM[:, t:t + 1]).then_inc(final_normed, 1)

        @block.vector
        def _(v):
            order = [0]

            def own(ins):
                order[0] += 1
                ins.then_inc(dve, 1)
                v.wait_ge(dve, order[0])

            for n in ("raw_score_read", "xs0_ready", "mean_copied", "vm_copied", "xs_ready", "score_taken", "feat_ready", "qT_copied",
                      "state0_kept", "state1_kept", "masked", "attn_normed", "xo_done", "gate_arg", "gates_ready",
                      "z_used", "combined", "xn_ready", "sum_asked", "roots_ready", "logit_used", "top_arg", "mask_ready", "routed",
                      "lin_ready", "gate_lin_ready", "s_ready", "sT_copied", "result_ready", "score_stored"):
                v.sem_inc(S[n], CREDIT)
            v.sem_inc(h_out, 16)
            v.sem_inc(seeded, 1)
            v.memset(zeros[:], 0.0).then_inc(prep, 1)
            v.memset(PF[:], 0.0).then_inc(prep, 1)
            v.memset(V1[:], 1.0).then_inc(prep, 1)
            v.memset(CNT[:], 0.0).then_inc(prep, 1)
            v.memset(onesB[:], 1.0).then_inc(prep, 1)
            v.memset(onesE[:], 1.0).then_inc(prep, 1)
            v.wait_ge(prep, 7)
            v.sem_inc(seeded, 1)
            v.wait_ge(seeded, 5)
            v.wait_ge(const_in_s, 16)
            v.tensor_copy(beforeB[:], const[:, C_BEFORE:C_BEFORE + P]).then_inc(prep, 1)
            v.tensor_copy(TOKI[:], const[:, C_TOK:C_TOK + NTT]).then_inc(prep, 1)
            v.wait_ge(weights_in, 96)
            for k in range(5):
                v.wait_ge(wt_ready, k + 1)
                for c in range(DC):
                    src = PS[:, k, c * D:(c + 1) * D]
                    if k < 3:
                        ins = v.tensor_scalar(WT[:, c, k * D:(k + 1) * D], src, nw[:, c:c + 1], None, ALU.mult)
                    elif k == 3:
                        ins = v.tensor_copy(WoT[:, c, :], src)
                    else:
                        ins = v.tensor_copy(WT[:, c, 3 * D:4 * D], src)
                    ins.then_inc(wt_copied, 1)
            v.wait_ge(x_in_s, 16 * B)

            def aggregate(dst, n, q, count):
                v.wait_ge(q, count)
                met(v)
                for i in range(n):
                    last = v.bn_aggr(dst[:, i, :], ST[:, i, :])
                return last

            def tile(x, i):
                return x[:, ds(i, 1), :].rearrange("p o d -> p (o d)")

            with v.Fori(0, NTT // 8) as m:
                for k in range(8):
                    v.bn_stats(tile(ST, 8 * m + k), tile(X2, 8 * m + k)).then_inc(ord3, 1)
            own(aggregate(MV, NTT, ord3, NTT))

            asked = [0]

            def inverse_root(dst, n, arg, base=None):
                asked[0] += 1
                at = asked[0] if base is None else base
                arg.then_inc(sqrt_asked, 1)
                v.wait_ge(sqrt_done, at)
                own(v.reciprocal(dst, sqS[:, 0:n]))

            inverse_root(RS[:], NTT, v.tensor_scalar(tmpS[:], MV[:, :, 1], LN_EPS, None, ALU.add))
            own(v.tensor_tensor(tmpS[:], RS[:], RS[:], ALU.mult))
            own(v.tensor_tensor(tmpS[:], tmpS[:], MV[:, :, 1], ALU.mult))
            inverse_root(RR[:], NTT, v.tensor_scalar(tmpS[:], tmpS[:], ATT_RMS_EPS, None, ALU.add))
            v.wait_ge(bias_in, 32)
            b12 = [(b1s[:], slice(0, 2 * INNER)), (b2s[:], slice(2 * INNER, 3 * INNER))]
            for src, cols in b12:
                own(v.tensor_copy(bh[:, 0, cols], src))
                own(v.tensor_tensor(bres[:, 0, cols], src, bh[:, 0, cols], ALU.subtract))
                own(v.tensor_copy(bh[:, 1, cols], bres[:, 0, cols]))
                own(v.tensor_tensor(bres[:, 1, cols], bres[:, 0, cols], bh[:, 1, cols], ALU.subtract))
                own(v.tensor_copy(bh[:, 2, cols], bres[:, 1, cols]))
            v.sem_inc(biasq, 5)
            with v.Fori(0, B) as b:
                local = [0]

                def own_b(ins, wait=True):
                    local[0] += 1
                    ins.then_inc(ordB, 1)
                    if wait:
                        v.wait_ge(ordB, b * PER_BATCH + local[0])

                def root_b(dst, n, arg, k):
                    arg.then_inc(sqrt_asked, 1)
                    v.wait_ge(sqrt_done, 3 * NQ * b + 3 + k)
                    own_b(v.reciprocal(dst, sqS[:, 0:n]))

                for i in range(NT):
                    t = b * NT + i
                    inc(v.tensor_scalar(XO[:, i, :], tile(X2, t), MV[:, ds(t, 1), 0:1].rearrange("p o d -> p (o d)"),
                                        RS[:, ds(t, 1)], ALU.subtract, ALU.mult), "xs0_ready")
                done(v, "mean_ready", b + 1)
                inc(v.tensor_copy(MT[:], PS[:, 0:DC, 0:NSEG]), "mean_copied")
                done(v, "vm_ready", b + 1)
                inc(v.tensor_copy(VM[:], PS[:, 2, 0:DC * NSEG].rearrange("p (c n) -> p c n", c=DC)), "vm_copied")
                done(v, "attn_ready", b * NT)
                done(v, "states_stored", b * NT)
                own_b(v.memset(SX[:, 3], 0.0))

                def enter(s, par):
                    done(v, "front_T_ready", b * NT + s - 1)
                    inc(v.tensor_copy(XS[:, par], tile(XO, s)), "xs_ready")

                def step(s, par, inner=False):
                    n, f, k, w = parts(s, inner)
                    t = b * NT + s
                    q = 1 - par
                    heads = const[:, C_HEADS:C_HEADS + HG * HV].unsqueeze(1).broadcast_to([P, 2, HG * HV])
                    state = PS[:, 7, 0:SW].rearrange("p (c w) -> p c w", c=2)
                    if f:
                        done(v, "raw_score_ready", t + 1)
                        inc(v.tensor_copy(SCS[:, par, 0:NSEG], PS[:, 6, 272:272 + NSEG]), "raw_score_read")
                        done(v, "proj_ready", t + 1)
                        done(v, "mcur_copied", t + 1)
                        inc(v.tensor_tensor_reduce(MC[:, par], PS[:, 5, D:2 * D], MC[:, par], 1.0, 0.0, ALU.mult,
                                                   ALU.add, SCS[:, par, NSEG:NSEG + 1]), "score_taken")
                    if k:
                        done(v, "state0_ready", t)
                        done(v, "states_stored", t - 2)
                        done(v, "attn_ready", t - 1)
                        inc(v.tensor_tensor(SX[:, 2 * q], state, heads, ALU.mult), "state0_kept")
                    if n:
                        enter(s + 1, q)
                    if f:
                        done(v, "relu_done", t + 1)
                        done(v, "qkT_ready", t - 1)
                        done(v, "state1_ready", t - 1)
                        ex, rl = (x[:, par].rearrange("p (h w) -> p h w", w=DK) for x in (EX, RL))
                        v.scalar_tensor_tensor(F2[:, par].rearrange("p k w -> p (k w)"), EX[:, par], 1.0, RL[:, par],
                                               ALU.min, ALU.add)
                        inc(v.scalar_tensor_tensor(PF[:, par].rearrange("p k h w -> p (k h) w")[:, :, 0:DK], ex, 1.0,
                                                   rl, ALU.min, ALU.add), "feat_ready")
                    if k:
                        done(v, "scores_ready", t)
                        causal = const[:, C_CAUSAL:C_CAUSAL + SEG].unsqueeze(1).broadcast_to([P, G * G, SEG])
                        inc(v.tensor_tensor(AM[:, q], PS[:, 0:G, 0:G * SEG].rearrange("p j (g c) -> p j g c", g=G),
                                            causal.rearrange("p (j g) c -> p j g c", j=G), ALU.mult), "masked")
                        done(v, "state1_ready", t)
                        inc(v.tensor_tensor(SX[:, 2 * q + 1], state, heads, ALU.mult), "state1_kept")
                    if w:
                        done(v, "wo_ready", t - 1)
                        xo = tile(XO, s - 2)
                        inc(v.tensor_tensor(xo, PS[:, 4, 0:D], xo, ALU.add), "xo_done")
                    if k:
                        done(v, "attn_ready", t)
                        o = PS[:, 6, 0:H * HV].rearrange("p (h c) -> p h c", h=H)
                        v.tensor_scalar(rden[:, q], o[:, :, DK], DEN_EPS, None, ALU.add).then_inc(ordD, 1)
                        v.wait_ge(ordD, 2 * t - 1)
                        v.reciprocal(rden[:, q], rden[:, q]).then_inc(ordD, 1)
                        v.wait_ge(ordD, 2 * t)
                        done(v, "attnT_ready", t - 2)
                        inc(v.tensor_tensor(AN[:, q].rearrange("p (h v) -> p h v", h=H), o[:, :, 0:DK],
                                            rden[:, q].unsqueeze(2).broadcast_to([P, H, DK]), ALU.mult), "attn_normed")
                    if f:
                        done(v, "qkT_ready", t + 1)
                        inc(v.tensor_copy(QT[:, par], PS[:, 0, :].rearrange("p (g t) -> p g t", g=G)), "qT_copied")
                        done(v, "score_taken", t + 1)
                        inc(v.tensor_scalar(tile(SC, s), SCS[:, par], 1.0, None, ALU.mult), "score_stored")

                enter(0, 0)
                steps(v, step)

                done(v, "score_stored", (b + 1) * NT)
                flat = SC[:].rearrange("p i n -> p (i n)")
                own_b(v.scalar_tensor_tensor(flat, flat, 1.0 / 16.0, const[:, C_SCORE:C_BEFORE], ALU.mult, ALU.add))
                own_b(v.tensor_reduce(red[:], SC[:], AX_X, ALU.max))
                inc(v.tensor_tensor(SC[:], SC[:], red[:].unsqueeze(2).broadcast_to([P, NT, NSEG + 1]),
                                    ALU.subtract), "gate_arg")
                done(v, "gate_exp", b + 1)
                own_b(v.tensor_reduce(red[:], SC[:], AX_X, ALU.add))
                own_b(v.reciprocal(red[:], red[:]))
                inc(v.tensor_tensor(SC[:], SC[:], red[:].unsqueeze(2).broadcast_to([P, NT, NSEG + 1]),
                                    ALU.mult), "gates_ready")
                done(v, "gates_ready", b + 1)
                done(v, "xo_done", (b + 1) * NT)

                v.wait_ge(small_in, 64)
                stats = [0]

                def stat(i, src):
                    stats[0] += 1
                    met(v)
                    v.bn_stats(ST[:, i, :], src).then_inc(ord3, 1)

                def moments(q):
                    v.wait_ge(ord3, b * 2 * NT + NTT + stats[0])
                    met(v)
                    for i in range(QT4 * q, QT4 * q + QT4):
                        last = v.bn_aggr(MV2[:, i, :], ST[:, i, :])
                    own_b(last)

                def under(q, stage):
                    tiles = range(QT4 * q, QT4 * q + QT4)
                    cols = slice(QT4 * q, QT4 * q + QT4)
                    n = b * NQ + q
                    var, tmp = MV2[:, cols, 1], tmpS[:, 0:QT4]
                    if stage == 0:
                        moments(q)
                        v.tensor_scalar(tmp, var, LN_EPS, None, ALU.add).then_inc(sqrt_asked, 1)
                    elif stage == 1:
                        v.wait_ge(sqrt_done, 3 * n + 3)
                        own_b(v.reciprocal(RS2[:, cols], sqS[:, 0:QT4]))
                        inc(v.scalar_tensor_tensor(NM[:, cols], MV2[:, cols, 0], -1.0, RS2[:, cols], ALU.mult,
                                                   ALU.mult), "sum_asked")
                    elif stage == 2:
                        for i in tiles:
                            x2 = tile(X2, b * NT + i)
                            done(v, "sum_normed", b * NT + i + 1)
                            v.tensor_tensor(x2, x2, XO[:, i, :], ALU.add).then_inc(ord4, 1)
                        v.wait_ge(ord4, b * NT + QT4 * q + QT4)
                        for i in tiles:
                            stat(i, tile(X2, b * NT + i))
                        moments(q)
                        v.tensor_scalar(tmp, var, LN_EPS, None, ALU.add).then_inc(sqrt_asked, 1)
                    elif stage == 3:
                        v.wait_ge(sqrt_done, 3 * n + 4)
                        own_b(v.reciprocal(RS2[:, cols], sqS[:, 0:QT4]))
                        own_b(v.scalar_tensor_tensor(NM[:, cols], MV2[:, cols, 0], -1.0, RS2[:, cols], ALU.mult,
                                                     ALU.mult))
                        own_b(v.tensor_tensor(tmp, RS2[:, cols], RS2[:, cols], ALU.mult))
                        own_b(v.tensor_tensor(tmp, tmp, var, ALU.mult))
                        v.tensor_scalar(tmp, tmp, FFN_RMS_EPS, None, ALU.add).then_inc(sqrt_asked, 1)
                    elif stage == 4:
                        v.wait_ge(sqrt_done, 3 * n + 5)
                        own_b(v.reciprocal(RR2[:, cols], sqS[:, 0:QT4]))
                        v.sem_inc(S["roots_ready"], 1)
                    elif stage == 5:
                        done(v, "rows_sent", b)
                        for i in tiles:
                            done(v, "h_ready", b * NT + i + 1)
                            inc(v.scalar_tensor_tensor(RW[:, i, 0:D], HN[:, i % QT4], RR2[:, i:i + 1], nsB[:],
                                                       ALU.mult, ALU.mult), "xn_ready")
                    elif stage == 6:
                        for pair in range(2):
                            done(v, "logit_ready", 2 * n + pair + 1)
                            inc(v.tensor_tensor(LG[:, 2 * pair:2 * pair + 2],
                                                PS[:, 6 + pair, 0:2 * E].rearrange("p (i e) -> p i e", e=E),
                                                bgB[:].unsqueeze(1).broadcast_to([P, 2, E]), ALU.add), "logit_used")
                        done(v, "logit_used", 2 * n + 2)
                        met(v)
                        for k in range(QT4):
                            v.max(M8[:, k], LG[:, k]).then_inc(ord5, 1)
                        v.wait_ge(ord5, 2 * QT4 * n + QT4)
                        met(v)
                        for k in range(QT4):
                            v.max_index(I8[:, k], M8[:, k], LG[:, k]).then_inc(ord5, 1)
                        v.wait_ge(ord5, 2 * QT4 * n + 2 * QT4)
                        inc(v.tensor_tensor(TV[:], M8[:, :, 0:TOPK],
                                            M8[:, :, 0:1].broadcast_to([P, QT4, TOPK]), ALU.subtract), "top_arg")
                        own_b(v.tensor_copy(TI[:], I8[:, :, 0:TOPK]))
                        iota = const[:, C_IOTA:C_IOTA + E].unsqueeze(1).broadcast_to([P, QT4 * TOPK, E])
                        own_b(v.tensor_tensor(OH.rearrange("p i j e -> p (i j) e"),
                                              TI[:].rearrange("p i j -> p (i j)").unsqueeze(2).broadcast_to(
                                                  [P, QT4 * TOPK, E]), iota, ALU.is_equal))
                        own_b(v.tensor_reduce(MK[:], OH.rearrange("p i j e -> p i e j"), AX_X, ALU.add))
                        inc(v.tensor_copy(MKb[:], MK[:]), "mask_ready")
                    elif stage == 7:
                        red4 = red[:, 0:QT4]
                        done(v, "top_exp", n + 1)
                        own_b(v.tensor_reduce(red4, TV[:], AX_X, ALU.add))
                        own_b(v.reciprocal(red4, red4))
                        own_b(v.tensor_tensor(TV[:], TV[:], red4.unsqueeze(2).broadcast_to([P, QT4, TOPK]), ALU.mult))
                        tv = TV[:].rearrange("p i j -> p (i j)").unsqueeze(2).broadcast_to([P, QT4 * TOPK, E])
                        own_b(v.tensor_tensor(OT.rearrange("p i j e -> p (i j) e"), OH.rearrange("p i j e -> p (i j) e"),
                                              tv, ALU.mult))
                        own_b(v.tensor_reduce(RW[:, cols, D:D + E], OT.rearrange("p i j e -> p i e j"), AX_X, ALU.add))
                        own_b(v.tensor_scalar(RW[:, cols, IDCOL].bitcast(I32), TOKI[:, ds(b * NT + QT4 * q, QT4)], 1.0,
                                              None, ALU.mult), False)
                        done(v, "rank_ready", n + 1)
                        own_b(v.tensor_tensor(PR[:], PS[:, 6, 0:QT4 * E].rearrange("p (i e) -> p i e", e=E),
                                              CNT[:].unsqueeze(1).broadcast_to([P, QT4, E]), ALU.add))
                        own_b(v.tensor_tensor(PR[:], PR[:], const[:, C_BASE:C_BASE + E].unsqueeze(1).broadcast_to(
                            [P, QT4, E]), ALU.add), False)
                        own_b(v.tensor_tensor(CNT[:], CNT[:], PS[:, 7, 0:E], ALU.add))
                        own_b(v.tensor_tensor(OT, OH, PR[:].unsqueeze(2).broadcast_to([P, QT4, TOPK, E]), ALU.mult))
                        own_b(v.tensor_reduce(POSF[:], OT, AX_X, ALU.add))
                        inc(v.tensor_copy(POS[:, cols], POSF[:]), "routed")

                turn = 0
                for i in range(NT):
                    sums2 = [XO[:, i, :], AN[:, i % 2]]
                    last_in = [("order", local[0] + 1), ("order", local[0] + 2)]
                    own_b(v.tensor_scalar(sums2[0], sums2[0], SC[:, i, NSEG:NSEG + 1], None, ALU.mult), False)
                    own_b(v.memset(sums2[1], 0.0), False)
                    for k in range(TURNS[i]):
                        done(v, "z_ready", b * NTURN + turn + 1)
                        for n in range(SEGT * k, min(SEGT * (k + 1), 2 * i + 1)):
                            acc = sums2[n % 2].rearrange("p (c w) -> p c w", c=2)
                            what, count = last_in[n % 2]
                            if what == "order":
                                v.wait_ge(ordB, b * PER_BATCH + count)
                            else:
                                done(v, "z_used", b * NTURN + count)
                            z = PS[:, 2 * (turn % 3):2 * (turn % 3) + 2, (n % SEGT) * P:(n % SEGT + 1) * P]
                            ins = v.scalar_tensor_tensor(acc, z, SC[:, i, n:n + 1], acc, ALU.mult, ALU.add)
                            if n < min(SEGT * (k + 1) - 1, 2 * i):
                                own_b(ins, False)
                                last_in[n % 2] = ("order", local[0])
                            else:
                                inc(ins, "z_used")
                                last_in[n % 2] = ("turn", turn + 1)
                        turn += 1
                        if i >= QT4 and k == (TURNS[i] - 1) // 2:
                            under(i // QT4 - 1, 2 * (i % QT4))
                    done(v, "z_used", b * NTURN + turn)
                    v.wait_ge(ordB, b * PER_BATCH + local[0])
                    own_b(v.tensor_tensor(sums2[0], sums2[0], sums2[1], ALU.add))
                    stat(i, sums2[0])
                    if i >= QT4:
                        under(i // QT4 - 1, 2 * (i % QT4) + 1)
                v.sem_inc(S["combined"], 1)
                for stage in range(8):
                    under(NQ - 1, stage)
                assert local[0] == PER_BATCH, local[0]

            own(v.tensor_copy(ti32[:], CNT[:]))
            own(v.tensor_scalar(ti32[:], CNT[:], float(P - 1), None, ALU.add))
            own(v.tensor_scalar(ti32[:], ti32[:], 7, None, ALU.arith_shift_right))
            own(v.tensor_copy(nb[:], ti32[:]))
            own(v.tensor_tensor_scan(cum[:], onesE[:], nb[:], 0.0, ALU.mult, ALU.add))
            own(v.tensor_scalar(cum[:], cum[:], float(P), None, ALU.mult))
            blk = const[:, C_BLK:C_BLK + 2]
            cumB = cum[:].unsqueeze(1).broadcast_to([P, 2, E])
            own(v.tensor_tensor(cmp[:], cumB, blk.unsqueeze(2).broadcast_to([P, 2, E]), ALU.is_le))
            own(v.tensor_reduce(blkE[:], cmp[:], AX_X, ALU.add))
            own(v.tensor_tensor(cmq[:], cmp[:], cumB, ALU.mult))
            own(v.tensor_reduce(blkC[:], cmq[:], AX_X, ALU.max))
            own(v.scalar_tensor_tensor(blkR[:], blkE[:], float(CAP), blkC[:], ALU.mult, ALU.subtract))
            own(v.tensor_tensor(blkR[:], blkR[:], blk, ALU.add))
            v.sem_inc(blocks_ready, 1)
            v.wait_ge(blocks_T_ready, 1)
            own(v.tensor_scalar(tabR[:], PS[0:1, 0, 0:NBLK], float(E * CAP), None, ALU.min))
            own(v.tensor_scalar(tabE[:], PS[0:1, 0, 2 * P:2 * P + NBLK], float(E - 1), None, ALU.min))
            own(v.tensor_tensor(padF[:], CNT[0:1, :], const[0:1, C_BASE:C_BASE + E], ALU.add))
            own(v.tensor_copy(padR[:], padF[:]))
            v.sem_inc(table_ready, 1)

            v.wait_ge(h_out, 16 * (B * NQ + 1))
            def clip(k, par):
                done(v, "hid_ready", k + 1)
                done(v, "s_ready", k - 1)
                inc(v.tensor_scalar(hA[:, par], PS[:, 2 + par, 0:INNER], LIMIT, None, ALU.min), "lin_ready")
                inc(v.tensor_scalar(hB[:, par], PS[:, 2 + par, INNER:2 * INNER], LIMIT, -LIMIT, ALU.min, ALU.max),
                    "gate_lin_ready")

            def activate(k, par):
                done(v, "sT_ready", k - 1)
                done(v, "gate_lin_ready", k + 1)
                v.scalar_tensor_tensor(hB[:, par], hB[:, par], 1.0, hA[:, par], ALU.add, ALU.mult).then_inc(ordE, 1)
                v.wait_ge(ordE, k + 1)
                done(v, "sig_ready", k + 1)
                inc(v.tensor_tensor(sS[:, par], hB[:, par], hS[:, par], ALU.mult), "s_ready")

            def copy_s(k, par):
                done(v, "sT_ready", k + 1)
                done(v, "y_ready", k - 1)
                inc(v.tensor_copy(sT[:, par], PS[:, 4 + par, 0:D].rearrange("p (c t) -> p c t", c=2)), "sT_copied")

            clip(0, 0)
            activate(0, 0)

            def block_step(k, par):
                clip(k + 1, 1 - par)
                copy_s(k, par)
                activate(k + 1, 1 - par)

            with v.Fori(0, NBLK // 2 - 1) as m:
                block_step(2 * m, 0)
                block_step(2 * m + 1, 1)
            block_step(NBLK - 2, 0)
            copy_s(NBLK - 1, 1)

            def add_x2(k):
                v.wait_ge(final_normed, 8 * (k + 1))
                for t in range(8 * k, 8 * k + 8):
                    inc(v.tensor_tensor(FS[:, t], FS[:, t], X2[:, t], ALU.add), "result_ready")

            for k in range(4):
                at = slice(8 * k, 8 * k + 8)
                v.wait_ge(f_in[k], 16)
                for t in range(8 * k, 8 * k + 8):
                    v.bn_stats(ST[:, t], FS[:, t]).then_inc(ord3, 1)
                v.wait_ge(ord3, NTT + 2 * B * NT + 8 * (k + 1))
                for t in range(8 * k, 8 * k + 8):
                    last = v.bn_aggr(MV[:, t, :], ST[:, t, :])
                own(last)
                v.tensor_scalar(tmpS[:, at], MV[:, at, 1], LN_EPS, None, ALU.add).then_inc(sqrt_asked, 1)
                if k:
                    add_x2(k - 1)
                v.wait_ge(sqrt_done, 3 * B * NQ + 3 + k)
                own(v.reciprocal(RS[:, at], sqS[:, at]))
                own(v.scalar_tensor_tensor(NM[:, at], MV[:, at, 0], -1.0, RS[:, at], ALU.mult, ALU.mult))
                v.sem_inc(final_asked, 1)
                for t in range(8 * k + 6, 8 * k + 8):
                    v.tensor_scalar(FS[:, t], FS[:, t], MV[:, t, 0:1], RS[:, t:t + 1], ALU.subtract,
                                    ALU.mult).then_inc(final_normed, 1)
            add_x2(3)

        @block.gpsimd
        def _(pool):
            for n in ("rows_sent", "sum_added"):
                pool.sem_inc(S[n], CREDIT)
            pool.memset(RW[:], 0.0).then_inc(prep, 1)
            pool.sem_inc(seeded, 1)
            pool.wait_ge(seeded, 5)
            pool.wait_ge(prep, 9)
            with pool.Fori(0, B) as b:
                for i in range(NT):
                    if i % QT4 == 0:
                        done(pool, "routed", b * NQ + i // QT4 + 1)
                        met(pool)
                    for j in range(TOPK):
                        pool.indirect_dma_start(
                            out=lists, out_offset=bass.IndirectOffsetOnAxis(ap=POS[:, i, j:j + 1], axis=0),
                            in_=RW[:, i], in_offset=None).then_inc(sc_out, 16)
                pool.wait_ge(sc_out, 16 * TOPK * NT * (b + 1))
                pool.sem_inc(S["rows_sent"], 1)
            pool.wait_ge(h_out, 16 * (B * NQ + 1))
            pool.wait_ge(pad_out, 16 * (E + 2))
            with pool.Fori(0, NBLK // RING) as m:
                for slot in range(RING):
                    k = RING * m + slot
                    done(pool, "y_scaled", k + 1)
                    met(pool)
                    pool.indirect_dma_start(
                        out=sums,
                        out_offset=bass.IndirectOffsetOnAxis(ap=XR[:, slot, IDCOL:IDCOL + 1].bitcast(I32), axis=0),
                        in_=YS[:, slot % 2], in_offset=None, compute_op=ALU.add).then_inc(added, 16)
                    pool.wait_ge(added, 16 * k + 16)
                    pool.sem_inc(S["sum_added"], 1)


def kernel(**inputs):
    import concourse.bacc as _bacc
    from concourse.bass_utils import run_bass_kernel_spmd as _run

    nc = _bacc.Bacc("TRN2", target_bir_lowering=False, num_devices=1)
    order = ["L0_attn_x", "L0_attn_norm_w", "L0_attn_Wq", "L0_attn_Wk", "L0_attn_Wv", "L0_attn_Wo", "L0_attn_Wu",
             "L0_ffn_norm_scale", "L0_ffn_wg", "L0_ffn_bg", "L0_ffn_w1", "L0_ffn_b1", "L0_ffn_w2", "L0_ffn_b2"]
    arrays, args = {}, []
    c, fill = constants()
    for name, a in [(n, inputs[n]) for n in order] + [("consts", c), ("fill_rows", fill)]:
        a = np.ascontiguousarray(a)
        arrays[f"in_{name}"] = a
        args.append(nc.dram_tensor(f"in_{name}", a.shape, mybir.dt.from_np(a.dtype), kind="ExternalInput").ap())
    out = nc.dram_tensor("out", (B, T, D), F32, kind="ExternalOutput").ap()
    lists = nc.dram_tensor("lists", (E * CAP + P, ROW), F32, kind="Internal").ap()
    sums = nc.dram_tensor("sums", (B * T + P, D), F32, kind="Internal").ap()
    parts = nc.dram_tensor("bias_parts", (3, E, 3 * INNER), BF16, kind="Internal").ap()
    program(nc, *args, out, lists, sums, parts)
    return _run(nc, [arrays], core_ids=[0]).results[0]["out"]
```

```python
from contextlib import ExitStack

import numpy as np

import concourse.bass as bass
from concourse import mybir

P = 128
F32 = mybir.dt.float32
I32 = mybir.dt.int32
U32 = mybir.dt.uint32
F32R = mybir.dt.float32r
BF16 = mybir.dt.bfloat16
ALU = mybir.AluOpType
ACT = mybir.ActivationFunctionType
AX_X = mybir.AxisListType.X
ds = bass.ds

B, T, D = 2, 2048, 256
H, DK, SEG = 16, 16, 64
NT = T // P
NTT = B * NT
NSEG = T // SEG
DC = D // P
G = 4
HV = DK + 1
HG = H // 2
SW = 2 * HG * HV
RING = 8
E, TOPK, INNER = 16, 4, 256
CAP = B * T + P
WRING = 3
EW = 3 * 2 * 2 * INNER
WPIECES = 6
AREN = 15360
PASS = WRING * EW + 8 * D
NBLK = B * T * TOPK // P + E
IDCOL = D + E
ROW = 276
QT4 = 4
NQ = NT // QT4
SEGT = 4
TURNS = [-(-(2 * i + 1) // SEGT) for i in range(NT)]
NTURN = sum(TURNS)
PER_BATCH = 308
CREDIT = 2
LN_EPS, ATT_RMS_EPS, DEN_EPS, FFN_RMS_EPS = 1e-5, 1e-6, 1e-6, 1e-5
LIMIT, ALPHA = 7.0, 1.702

C_IDENT = 0
C_CAUSAL = C_IDENT + P
C_MEANS = C_CAUSAL + SEG
C_SEGMEAN = C_MEANS + P
C_HEADS = C_SEGMEAN + 2
C_SCORE = C_HEADS + HG * HV
C_BEFORE = C_SCORE + NT * (NSEG + 1)
C_IOTA = C_BEFORE + P
C_BASE = C_IOTA + E
C_TOK = C_BASE + E
C_BLK = C_TOK + NTT
C_SLOT = C_BLK + 2
C_ALL = C_SLOT + E


def constants():
    c = np.zeros((P, C_ALL), np.float32)
    p = np.arange(P)
    c[:, C_IDENT:C_IDENT + P] = np.eye(P)
    c[:, C_CAUSAL:C_CAUSAL + SEG] = np.arange(SEG)[None] >= (p % SEG)[:, None]
    same = (p[:, None] // SEG) == (p[None] // SEG)
    c[:, C_MEANS:C_MEANS + P] = same * (p[:, None] <= p[None]) / ((p % SEG)[None] + 1.0)
    c[:, C_SEGMEAN:C_SEGMEAN + 2] = (p[:, None] // SEG == np.arange(2)[None]) / float(SEG)
    c[:, C_HEADS:C_HEADS + HG * HV] = (p[:, None] // DK) == (np.arange(HG * HV)[None] // HV)
    score = np.zeros((P, NT, NSEG + 1), np.float32)
    for i in range(NT):
        seg = 2 * i + p // SEG
        score[:, i, :NSEG] = np.where(seg[:, None] > np.arange(NSEG)[None], 0.0, -1e30)
    c[:, C_SCORE:C_BEFORE] = score.reshape(P, -1)
    c[:, C_BEFORE:C_BEFORE + P] = p[:, None] < p[None]
    c[:, C_IOTA:C_IOTA + E] = np.arange(E)
    c[:, C_BASE:C_BASE + E] = np.arange(E) * CAP
    c[:, C_TOK:C_TOK + NTT] = p[:, None] * NTT + np.arange(NTT)[None]
    c[:, C_BLK:C_BLK + 2] = (np.arange(2)[None] * P + p[:, None]) * P
    place = np.arange(E) % WRING * EW
    c[:, C_SLOT:C_SLOT + E - 1] = np.diff(place)
    fill = np.zeros((P, ROW), np.int32)
    fill[:, IDCOL] = B * T + p
    return c, fill


def program(nc, x_in, norm_w, Wq, Wk, Wv, Wo, Wu, norm_scale, wg, bg, w1, b1, w2, b2,
            const_in, fill_in, out, lists, sums, parts_dram, split_dram):
    with ExitStack() as ctx:
        def sb(name, shape, dt=F32):
            return ctx.enter_context(nc.sbuf_tensor(name, shape, dt))

        def sem(name):
            return ctx.enter_context(nc.semaphore(name))

        PS = ctx.enter_context(nc.psum_tensor("PS", [P, 8, 512], F32))
        const = sb("const", [P, C_ALL])
        fill = sb("fill", [P, ROW], I32)
        ident = const[:, C_IDENT:C_IDENT + P]
        X2 = sb("X2", [P, NTT, D])
        XO = sb("XO", [P, NT, D])
        arena = sb("arena", [P, AREN])
        with nc.sbuf_tensor("passes", [P, PASS], F32) as passes:
            pass
        products = sb("products", [P, PASS], F32R)
        PQT = arena[:, 0:4096].rearrange("p (i c t) -> p i c t", i=NT, c=2)
        SB = arena[:, 4096:4096 + NSEG * SW].rearrange("p (n c w) -> p n c w", n=NSEG, c=2)
        FS = arena[:, 0:NTT * D].rearrange("p (t d) -> p t d", t=NTT)
        spare = {"arena": 4096 + NSEG * SW, "passes": 0}

        def early(shape, where="passes"):
            n = int(np.prod(shape))
            tensor, size = (arena, AREN) if where == "arena" else (passes, PASS)
            view = tensor[:, spare[where]:spare[where] + n]
            spare[where] += n
            assert spare[where] <= size, where
            names = " ".join("abcd"[:len(shape)])
            return view.rearrange(f"p ({names}) -> p {names}", **dict(zip("abcd", shape)))

        SC = early([NT, NSEG + 1], "arena")
        WT = early([DC, 4 * D])
        WoT = early([DC, D], "arena")
        Wun = early([DC, D], "arena")
        wraw = arena[:, 0:2048].rearrange("p (k c d) -> p k c d", k=4, c=DC)
        raw = early([2 * INNER], "arena")
        halves = early([2, 2 * INNER])
        nw = sb("nw", [P, DC])
        nsB = sb("nsB", [P, D])
        wgS = sb("wgS", [P, DC, E])
        bgB = sb("bgB", [P, E])
        zeros = early([SW], "arena")
        MV = sb("MV", [P, NTT, 2])
        RS = sb("RS", [P, NTT])
        RR = sb("RR", [P, NTT])
        tmpS = sb("tmpS", [P, NTT])
        sqS = sb("sqS", [P, NTT])
        XS = early([2, D])
        MT = early([DC, NSEG])
        VM = early([DC, NSEG])
        XT = early([2, DC, P])
        MC = early([2, D])
        EX = sb("EX", [P, 2, 2 * D])
        RL = sb("RL", [P, 2, 2 * D])
        PF = sb("PF", [P, 2, 2, H, 32])
        V1 = sb("V1", [P, 2, H, HV])
        QT = sb("QT", [P, 2, G, P])
        F2 = early([2, 2, D])
        Q2 = early([2, 2, P])
        KT = early([2, G, P])
        AM = early([2, G * G, SEG]).rearrange("p b (j g) c -> p b j g c", j=G)
        SX = early([4, 2, HG * HV])
        AN = sb("AN", [P, 2, D])
        rden = sb("rden", [P, 2, H])
        ANT = early([2, DC, P])
        SCS = early([2, NSEG + 1])
        red = sb("red", [P, NT])
        MV2 = sb("MV2", [P, NT, 2])
        RS2 = sb("RS2", [P, NT])
        RR2 = sb("RR2", [P, NT])
        NM = sb("NM", [P, NTT])
        LG = sb("LG", [P, QT4, E])
        M8 = sb("M8", [P, QT4, 8])
        I8 = sb("I8", [P, QT4, 8], U32)
        TV = sb("TV", [P, QT4, TOPK])
        TI = sb("TI", [P, QT4, TOPK])
        HN = EX[:].rearrange("p b (k d) -> p (b k) d", d=D)
        XNT = QT[:].rearrange("p b g t -> p (b g t)").rearrange("p (i c t) -> p i c t", i=QT4, c=DC)
        RLf = RL[:].rearrange("p b w -> p (b w)")
        OH = RLf[:, 0:QT4 * TOPK * E].rearrange("p (i j e) -> p i j e", j=TOPK, e=E)
        OT = RLf[:, 256:256 + QT4 * TOPK * E].rearrange("p (i j e) -> p i j e", j=TOPK, e=E)
        ST = RLf[:, 512:512 + 6 * NTT].rearrange("p (t s) -> p t s", t=NTT)
        MK = sb("MK", [P, QT4, E])
        MKb = sb("MKb", [P, QT4, E], BF16)
        beforeB = sb("beforeB", [P, P], BF16)
        onesB = sb("onesB", [P, P], BF16)
        PR = sb("PR", [P, QT4, E])
        CNT = sb("CNT", [P, E])
        POSF = sb("POSF", [P, QT4, TOPK])
        POS = sb("POS", [P, NT, TOPK], I32)
        TOKI = sb("TOKI", [P, NTT], I32)
        RW = sb("RW", [P, NT, ROW])
        XR = RW[:, 0:RING]
        ti32 = sb("ti32", [P, E], I32)
        nb = sb("nb", [P, E])
        cum = sb("cum", [P, E])
        onesE = sb("onesE", [P, E])
        cmp = sb("cmp", [P, 2, E])
        cmq = sb("cmq", [P, 2, E])
        blkE, blkC, blkR = sb("blkE", [P, 2]), sb("blkC", [P, 2]), sb("blkR", [P, 2])
        tabE = sb("tabE", [1, NBLK], I32)
        tabR = sb("tabR", [1, NBLK], I32)
        tabW = arena[0:1, NTT * D:NTT * D + NBLK].bitcast(I32)
        AHEAD = RING - 2
        tabA = arena[0:1, NTT * D + NBLK + E:NTT * D + 2 * NBLK + E].bitcast(I32)
        tabD = arena[0:1, NTT * D + NBLK:NTT * D + NBLK + E].bitcast(I32)
        blkW = sb("blkW", [P, 2])
        padF = sb("padF", [1, E])
        padR = sb("padR", [1, E], I32)
        b1s = arena[0:E, 6144:6144 + 2 * INNER]
        b2s = arena[0:E, 7168:7168 + D]
        bh = arena[0:E, 2048:2048 + 1152].bitcast(BF16).rearrange("e (k n) -> e k n", k=3)
        bres = arena[0:E, 4096:4096 + 1536].rearrange("e (k n) -> e k n", k=2)
        b1h = XO[0:3].rearrange("k i d -> k (i d)").bitcast(BF16).rearrange("k (e n) -> k e n", e=E)
        b2h = PF[0:3].rearrange("k a b h w -> k (a b h w)").bitcast(BF16).rearrange("k (e n) -> k e n", e=E)
        operands = products[:, WRING * EW:PASS]
        XRT = operands[:, 0:4 * D].rearrange("p (b h c t) -> p b h c t", b=2, h=2, c=DC)
        sTh, sTl = (operands[:, k * D:(k + 2) * D].rearrange("p (b c t) -> p b c t", b=2, c=DC)
                    for k in (4, 6))
        FO = products[:, 0:NTT * D].bitcast(F32).rearrange("p (t d) -> p t d", t=NTT)
        hA, hS = EX[:, :, 0:INNER], EX[:, :, INNER:2 * INNER]
        hB, sS = RL[:, :, 0:INNER], RL[:, :, INNER:2 * INNER]
        YS = AN

        (const_in_s, weights_in, x_in_s, bias_in, small_in) = map(
            sem, ("const_loaded", "weights_loaded", "x_loaded", "bias_loaded", "small_loaded"))
        wt_ready, wt_copied = sem("wt_ready"), sem("wt_copied")
        prep, sqrt_asked, sqrt_done = sem("prep_done"), sem("sqrt_asked"), sem("sqrt_done")
        dve = sem("dve_order")
        names = ("xs0_ready", "mean_ready", "mean_copied", "vm_ready", "vm_copied",
                 "xs_ready", "front_T_ready", "xT_copied", "mcur_copied", "proj_ready", "vu_ready", "exp_done",
                 "relu_done", "v_copied", "score_taken", "feat_ready", "qkT_ready", "qT_copied",
                 "kT_copied", "q_stored", "state0_ready", "state0_kept", "scores_ready", "masked",
                 "raw_score_ready", "raw_score_read", "state1_ready", "state1_kept", "states_stored", "attn_ready", "attn_normed",
                 "attnT_ready", "attnT_copied", "wo_ready", "xo_done", "score_stored",
                 "gate_arg", "gate_exp", "gates_ready", "z_ready", "z_used", "combined",
                 "xn_ready", "xnT_ready", "xnT_copied", "sum_asked", "sum_normed", "q2_kept", "roots_ready", "rows_sent", "logit_ready", "logit_used",
                 "h_ready", "top_arg", "top_exp", "mask_ready", "rank_ready", "routed")
        S = {n: sem(n) for n in names}
        h_out = sem("h_stored")
        sc_out = sem("scattered")
        pad_out, table_ready = sem("fill_stored"), sem("table_ready")
        blocks_ready, blocks_T_ready = sem("blocks_ready"), sem("blocks_T_ready")
        w_in = sem("expert_weights")
        raw_in, split_made, split_out = sem("raw_piece_loaded"), sem("piece_split"), sem("piece_stored")
        biasq = sem("bias_parts")
        biasd = sem("bias_moved")
        xr_in = [sem(f"rows_loaded_{k}") for k in range(RING)]
        enames = ("xrT_ready", "xrT_copied", "hid_ready", "lin_ready", "sig_ready", "gate_lin_ready",
                  "s_ready", "sT_ready", "sT_copied", "xrT_low", "sT_low", "y_ready", "y_scaled", "sum_added", "result_ready")
        S.update({n: sem(n) for n in enames})
        added = [sem("even_block_added"), sem("odd_block_added")]
        sums_joined = sem("sums_joined")
        f_in = [sem(f"sums_loaded_{k}") for k in range(4)]
        fout = sem("out_stored")
        seeded = sem("seeded")
        ordD, ordB = sem("order_den"), sem("order_batch")
        ord3, ord4, ord5 = sem("order_stats"), sem("order_sum"), sem("order_top")
        ordE, final_asked, final_normed = sem("order_expert"), sem("final_roots"), sem("final_normed")
        turns = sem("waits_met")

        def met(eng):
            eng.sem_inc(turns, 1)


        def done(eng, name, count):
            eng.wait_ge(S[name], count + CREDIT)

        def inc(ins, name):
            return ins.then_inc(S[name], 1)

        x_v = x_in.rearrange("b (i p) d -> p (b i) d", p=P)
        sums_v = [x[0:B * T, :].rearrange("(p t) d -> p t d", p=P) for x in sums]
        out_v = out.rearrange("b (i p) d -> (b i p) d", p=P)
        block = ctx.enter_context(nc.Block())

        def steps(eng, step):
            step(0, 0)
            step(1, 1)
            with eng.Fori(1, NT // 2 - 1) as m:
                for par in range(2):
                    step(2 * m + par, par, True)
            for s in range(NT - 2, NT + 2):
                step(s, s % 2)

        def parts(s, inner):
            if inner:
                return True, True, True, True
            return s + 1 < NT, s < NT, 1 <= s <= NT, 2 <= s

        def store_fill(eng, first, last):
            with eng.Fori(first // 4, last // 4) as m:
                for k in range(4):
                    row = eng.value_load(padR[0:1, ds(4 * m + k, 1)], min_val=0, max_val=E * CAP - P)
                    eng.dma_start(lists[ds(row, P), :], fill[:].bitcast(F32)).then_inc(pad_out, 16)

        def load_rows(eng, k, slot):
            row = eng.value_load(tabR[0:1, ds(k, 1)], min_val=0, max_val=E * CAP)
            eng.dma_start(XR[:, slot], lists[ds(row, P), :]).then_inc(xr_in[slot], 16)

        @block.sync
        def _(sp):
            sp.dma_start(const[:], const_in).then_inc(const_in_s, 16)
            for b in range(B):
                if b:
                    sp.wait_ge(x_in_s, 16 * b)
                sp.dma_start(X2[:, NT * b:NT * (b + 1), :], x_v[:, NT * b:NT * (b + 1), :]).then_inc(x_in_s, 16)
                if b == 0:
                    for k, w in enumerate((Wq, Wk, Wv, Wo)):
                        sp.dma_start(wraw[:, k], w.rearrange("(c p) d -> p c d", p=P)).then_inc(weights_in, 16)
                    sp.dma_start(Wun[:], Wu.rearrange("(c p) d -> p c d", p=P)).then_inc(weights_in, 16)
                    with nc.allow_non_contiguous_dma(reason="256 numbers, once"):
                        sp.dma_start(nw[:], norm_w.rearrange("(c p) -> p c", p=P)).then_inc(weights_in, 16)
            sp.dma_start(nsB[:], norm_scale.partition_broadcast(P)).then_inc(small_in, 16)
            sp.dma_start(bgB[:], bg.partition_broadcast(P)).then_inc(small_in, 16)
            sp.dma_start(wgS[:], wg.rearrange("(c p) e -> p c e", p=P)).then_inc(small_in, 16)
            sp.dma_start(fill[:], fill_in).then_inc(small_in, 16)
            sp.dma_start(b1s[:], b1).then_inc(bias_in, 16)
            sp.dma_start(b2s[:], b2).then_inc(bias_in, 16)
            sp.wait_ge(biasq, 5)
            sp.dma_start(parts_dram.rearrange("k e n -> e k n"), bh).then_inc(biasd, 16)
            sp.wait_ge(biasd, 16)
            sp.wait_ge(prep, 7)
            sp.dma_start(sums[0][B * T:B * T + P, :], nsB[:]).then_inc(pad_out, 16)
            for k in range(3):
                n = (B * T + P) // 3
                sp.dma_start(sums[1][k * n:(k + 1) * n, :].rearrange("(t p) d -> p t d", p=P),
                             zeros[:, 0:D].unsqueeze(1).broadcast_to([P, n // P, D])).then_inc(pad_out, 16)
            def split_experts(first, last):
                with sp.Fori(first, last) as e:
                    for j in range(3):
                        n = 3 * e + j
                        if j < DC:
                            src = w1[ds(e, 1), j * P:(j + 1) * P, :].rearrange("o p n -> p (o n)")
                        else:
                            src = w2[ds(e, 1)].rearrange("o (c p) n -> p (o c) n", p=P)
                        dst = raw if j < DC else raw.rearrange("p (c n) -> p c n", c=DC)
                        sp.dma_start(dst, src).then_inc(raw_in, 16)
                        sp.wait_ge(split_made, 2 * n + 4)
                        sp.dma_start(split_dram[ds(e, 1), :, j * 4 * INNER:(j + 1) * 4 * INNER].rearrange(
                            "o p n -> p (o n)"), halves[:].rearrange("p h n -> p (h n)")).then_inc(split_out, 16)

            def store_normed(n):
                t = n * QT4
                done(sp, "h_ready", t + QT4)
                sp.dma_start(sums_v[0][:, ds(t, QT4), :], HN).then_inc(h_out, 16)

            split_experts(0, E // B)
            with sp.Fori(0, (B - 1) * NQ) as n:
                store_normed(n)
            split_experts(E // B, E)
            def load_weights(e):
                for piece in range(WPIECES):
                    at, n = piece * EW // WPIECES, EW // WPIECES
                    sp.wait_ge(w_in, 16 * (e * WPIECES + piece) + 16)
                    sp.dma_start(products[:, e % WRING * EW + at:e % WRING * EW + at + n].bitcast(F32),
                                 split_dram[e, :, at:at + n]).then_inc(w_in, 16)

            done(sp, "gates_ready", B)
            done(sp, "xo_done", B * NT)
            done(sp, "states_stored", B * NT)
            done(sp, "q_stored", B * NT)
            sp.wait_ge(split_out, 16 * 3 * E + 16)
            for e in range(WRING):
                load_weights(e)
            with sp.Fori((B - 1) * NQ, B * NQ - 1) as n:
                store_normed(n)
            store_normed(B * NQ - 1)
            done(sp, "xnT_copied", B * NT // 2)
            sp.dma_start(b1h, parts_dram[:, :, 0:2 * INNER]).then_inc(biasd, 16)
            sp.dma_start(b2h, parts_dram[:, :, 2 * INNER:3 * INNER]).then_inc(biasd, 16)
            sp.wait_ge(table_ready, 1)
            sp.wait_ge(small_in, 64)
            sp.dma_start(lists[E * CAP:E * CAP + P, :], fill[:].bitcast(F32)).then_inc(pad_out, 16)
            store_fill(sp, 0, E // 2)
            sp.wait_ge(pad_out, 16 * (E + 5))
            sp.wait_ge(sc_out, 16 * TOPK * NTT)

            for k in range(RING):
                load_rows(sp, k, k)
            for e in range(WRING, E):
                blocks = sp.value_load(tabD[0:1, e - WRING:e - WRING + 1], min_val=0, max_val=NBLK)
                sp.wait_ge(S["y_ready"], blocks + CREDIT)
                load_weights(e)
            done(sp, "sum_added", NBLK)
            for k in range(4):
                for dst, src in zip((FS, FO), sums_v):
                    sp.dma_start(dst[:, 8 * k:8 * k + 8, :], src[:, 8 * k:8 * k + 8, :]).then_inc(f_in[k], 16)
            for m in range(NTT // 4):
                done(sp, "result_ready", 4 * m + 4)
                sp.dma_start(out_v[4 * m * P:4 * (m + 1) * P, :].rearrange("(t p) d -> p t d", p=P),
                             FS[:, 4 * m:4 * m + 4]).then_inc(fout, 16)
            sp.wait_ge(fout, 16 * (NTT // 4))

        @block.tensor
        def _(pe):
            for n in ("mean_ready", "vm_ready", "front_T_ready", "proj_ready", "vu_ready", "qkT_ready", "state0_ready",
                      "state1_ready", "raw_score_ready", "scores_ready", "attn_ready", "attnT_ready", "wo_ready", "z_ready",
                      "xnT_ready", "logit_ready", "rank_ready", "xrT_ready", "hid_ready", "sT_ready", "y_ready"):
                pe.sem_inc(S[n], CREDIT)
            pe.sem_inc(seeded, 1)
            pe.wait_ge(seeded, 5)
            pe.wait_ge(const_in_s, 16)
            pe.wait_ge(weights_in, 96)
            for k in range(5):
                for oc in range(DC):
                    for c in range(DC):
                        w = Wun[:, oc, c * P:(c + 1) * P] if k == 4 else wraw[:, k, oc, c * P:(c + 1) * P]
                        last = pe.transpose(PS[:, k, c * D + oc * P:c * D + (oc + 1) * P], w, ident)
                last.then_inc(wt_ready, 1)
            pe.wait_ge(wt_copied, 5 * DC)

            def pass0(b):
                for i in range(NT):
                    done(pe, "xs0_ready", b * NT + i + 1)
                    for c in range(DC):
                        last = pe.matmul(PS[:, c, 2 * i:2 * i + 2], lhsT=XO[:, i, c * P:(c + 1) * P],
                                         rhs=const[:, C_SEGMEAN:C_SEGMEAN + 2], start=True, stop=True)
                inc(last, "mean_ready")
                done(pe, "mean_copied", b + 1)
                for c in range(DC):
                    for oc in range(DC):
                        last = pe.matmul(PS[:, 2, c * NSEG:(c + 1) * NSEG], lhsT=Wun[:, oc, c * P:(c + 1) * P],
                                         rhs=MT[:, oc, :], start=(oc == 0), stop=(oc == DC - 1))
                inc(last, "vm_ready")
                done(pe, "vm_copied", b + 1)
                pe.matmul(PS[:, 7, 0:SW], lhsT=zeros[:, 0:P], rhs=zeros[:], start=True, stop=False,
                          skip_group_check=True)

            def front_T(b, s, p):
                done(pe, "xs_ready", b * NT + s + 1)
                done(pe, "mcur_copied", b * NT + s)
                done(pe, "masked", b * NT + s - 1)
                for c in range(DC):
                    pe.transpose(PS[:, 2, c * P:(c + 1) * P], XS[:, p, c * P:(c + 1) * P], ident)
                inc(pe.matmul(PS[:, 2, D:2 * D], lhsT=const[:, C_MEANS:C_MEANS + P], rhs=XS[:, p],
                              start=True, stop=True), "front_T_ready")

            def project(b, s, p):
                t = b * NT + s
                done(pe, "xT_copied", t + 1)
                done(pe, "exp_done", t)
                done(pe, "relu_done", t)
                if not isinstance(s, int) or s >= 3:
                    done(pe, "xo_done", t - 2)
                done(pe, "attn_normed", t - 1)
                for c in range(DC):
                    last = pe.matmul(PS[:, 6, 272:272 + NSEG], lhsT=XT[:, p, c, :], rhs=VM[:, c, :],
                                     start=(c == 0), stop=(c == DC - 1))
                inc(last, "raw_score_ready")
                for c in range(DC):
                    last = pe.matmul(PS[:, 4, :], lhsT=XT[:, p, c, :], rhs=WT[:, c, 0:512],
                                     start=(c == 0), stop=(c == DC - 1))
                inc(last, "proj_ready")

            def project_vu(b, s, p):
                t = b * NT + s
                done(pe, "v_copied", t)
                done(pe, "score_taken", t)
                for c in range(DC):
                    last = pe.matmul(PS[:, 5, :], lhsT=XT[:, p, c, :], rhs=WT[:, c, 512:1024],
                                     start=(c == 0), stop=(c == DC - 1))
                inc(last, "vu_ready")

            def features_T(b, s, p):
                t = b * NT + s
                done(pe, "feat_ready", t + 1)
                done(pe, "masked", t)
                for k in range(2):
                    for g in range(G):
                        pe.transpose(PS[:, k, g * P:(g + 1) * P],
                                     PF[:, p, k, 4 * g:4 * g + 4, :].rearrange("p h k -> p (h k)"), ident)
                for c in range(2):
                    last = pe.transpose(PS[:, 3, D + c * P:D + (c + 1) * P], F2[:, p, 0, c * P:(c + 1) * P], ident)
                inc(last, "qkT_ready")

            def state(b, s, p, seg):
                rows = slice(SEG * seg, SEG * seg + SEG)
                for c in range(2):
                    last = pe.matmul(PS[:, 7, c * HG * HV:(c + 1) * HG * HV],
                                     lhsT=F2[rows, p, 1, c * P:(c + 1) * P],
                                     rhs=V1[rows, p, HG * c:HG * (c + 1), :].rearrange("p h k -> p (h k)"),
                                     start=False, stop=False, skip_group_check=True)
                inc(last, f"state{seg}_ready")

            def scores(b, s, p):
                t = b * NT + s
                done(pe, "v_copied", t + 1)
                done(pe, "state1_kept", t)
                state(b, s, p, 0)
                done(pe, "qT_copied", t + 1)
                done(pe, "kT_copied", t + 1)
                done(pe, "q2_kept", t + 1)
                done(pe, "attnT_copied", t)
                for g in range(G):
                    for seg in range(2):
                        for j in range(G):
                            rows = slice(32 * j, 32 * j + 32)
                            toks = slice(SEG * seg, SEG * seg + SEG)
                            last = pe.matmul(PS[toks, j, g * SEG:(g + 1) * SEG], lhsT=KT[rows, p, g, toks],
                                             rhs=QT[rows, p, g, toks], start=True, stop=True,
                                             skip_group_check=True)
                inc(last, "scores_ready")
                done(pe, "state0_kept", t + 1)
                state(b, s, p, 1)

            def attend(b, s, p, front):
                t = b * NT + s
                done(pe, "attn_normed", t)
                done(pe, "masked", t + 1)
                done(pe, "raw_score_read", t + 2 if front else t + 1)
                for seg in range(2):
                    toks = slice(SEG * seg, SEG * seg + SEG)
                    slot = (2 * p + seg - 1) % 4
                    for c in range(2):
                        pe.matmul(PS[toks, 6, c * HG * HV:(c + 1) * HG * HV], lhsT=Q2[:, p, c, toks],
                                  rhs=SX[:, slot, c, :], start=(c == 0), stop=False, skip_group_check=True)
                    for h in range(H):
                        last = pe.matmul(PS[toks, 6, h * HV:(h + 1) * HV], lhsT=AM[toks, p, h % G, h // G, :],
                                         rhs=V1[toks, p, h, :], start=False, stop=True, skip_group_check=True)
                inc(last, "attn_ready")

            def attended_T(b, s, p):
                done(pe, "attn_normed", b * NT + s + 1)
                for c in range(DC):
                    last = pe.transpose(PS[:, 3, c * P:(c + 1) * P], AN[:, p, c * P:(c + 1) * P], ident)
                inc(last, "attnT_ready")

            def out_proj(b, s, p):
                done(pe, "attnT_copied", b * NT + s + 1)
                for c in range(DC):
                    last = pe.matmul(PS[:, 4, 0:D], lhsT=ANT[:, p, c, :], rhs=WoT[:, c, :],
                                     start=(c == 0), stop=(c == DC - 1))
                inc(last, "wo_ready")

            def normed_T(b, q):
                done(pe, "routed", b * NQ + q)
                for pair in range(2):
                    i = QT4 * q + 2 * pair
                    done(pe, "xn_ready", b * NT + i + 2)
                    for k in range(2):
                        for c in range(DC):
                            last = pe.transpose(PS[:, 6 + pair, k * D + c * P:k * D + (c + 1) * P],
                                                RW[:, i + k, c * P:(c + 1) * P], ident)
                    inc(last, "xnT_ready")

            def logits(b, q):
                for pair in range(2):
                    done(pe, "xnT_copied", (b * NQ + q) * 2 + pair + 1)
                    for k in range(2):
                        for c in range(DC):
                            last = pe.matmul(PS[:, 6 + pair, k * E:(k + 1) * E], lhsT=XNT[:, 2 * pair + k, c, :],
                                             rhs=wgS[:, c, :], start=(c == 0), stop=(c == DC - 1))
                    inc(last, "logit_ready")

            def ranks(b, q):
                done(pe, "mask_ready", b * NQ + q + 1)
                pe.matmul(PS[:, 6, 0:QT4 * E], lhsT=beforeB[:], rhs=MKb[:].rearrange("p i e -> p (i e)"),
                          start=True, stop=False, skip_group_check=True)
                for i in range(QT4 - 1):
                    pe.matmul(PS[:, 6, (i + 1) * E:QT4 * E].rearrange("p (i e) -> p i e", e=E), lhsT=onesB[:],
                              rhs=MKb[:, i:i + 1, :].broadcast_to([P, QT4 - 1 - i, E]),
                              start=False, stop=False, skip_group_check=True)
                for i in range(QT4):
                    last = pe.matmul(PS[:, 7, 0:E], lhsT=onesB[:], rhs=MKb[:, i, :], start=(i == 0),
                                     stop=(i == QT4 - 1))
                inc(last, "rank_ready")

            with pe.Fori(0, B) as b:
                pass0(b)

                def step(s, par, inner=False):
                    n, f, k, w = parts(s, inner)
                    if f:
                        project(b, s, par)
                    if k:
                        if f:
                            done(pe, "xT_copied", b * NT + s + 1)
                            done(pe, "mcur_copied", b * NT + s + 1)
                        scores(b, s - 1, 1 - par)
                    if f:
                        project_vu(b, s, par)
                    if w:
                        if f:
                            done(pe, "exp_done", b * NT + s + 1)
                            done(pe, "relu_done", b * NT + s + 1)
                        out_proj(b, s - 2, par)
                    if n:
                        front_T(b, s + 1, 1 - par)
                    if k:
                        attend(b, s - 1, 1 - par, f)
                    if f:
                        features_T(b, s, par)
                    if k:
                        attended_T(b, s - 1, 1 - par)

                front_T(b, 0, 0)
                steps(pe, step)
                done(pe, "gates_ready", b + 1)
                done(pe, "q_stored", (b + 1) * NT)
                done(pe, "states_stored", (b + 1) * NT)
                done(pe, "xo_done", (b + 1) * NT)
                turn = 0
                for i in range(NT):
                    q = i // QT4 - 1
                    routing = q >= 0 and i % QT4 == QT4 - 1
                    for k in range(TURNS[i]):
                        if turn >= 3:
                            done(pe, "z_used", b * NTURN + turn - 2)
                        for c in range(2):
                            last = pe.matmul(PS[:, 2 * (turn % 3) + c, :], lhsT=PQT[:, i, c, :],
                                             rhs=SB[:, SEGT * k:SEGT * (k + 1), c, :].rearrange(
                                                 "p n (h v) -> p n h v", h=HG)[:, :, :, 0:DK],
                                             start=True, stop=True)
                        inc(last, "z_ready")
                        turn += 1
                        if routing and k == 0:
                            normed_T(b, q)
                        if routing and k == 1:
                            logits(b, q)
                    if routing:
                        ranks(b, q)
                normed_T(b, NQ - 1)
                logits(b, NQ - 1)
                ranks(b, NQ - 1)
                done(pe, "z_used", (b + 1) * NTURN)
                done(pe, "routed", (b + 1) * NQ)

            pe.wait_ge(blocks_ready, 1)
            for k, column in enumerate((blkR[:, 0:1], blkR[:, 1:2], blkE[:, 0:1], blkE[:, 1:2])):
                last = pe.transpose(PS[0:1, 0, k * P:(k + 1) * P], column, ident)
            for k in range(2):
                last = pe.transpose(PS[0:1, 1, k * P:(k + 1) * P], blkW[:, k:k + 1], ident)
            last.then_inc(blocks_T_ready, 1)

            pe.wait_ge(biasd, 48)
            pe.wait_ge(table_ready, 1)

            def turn_rows(k, m, slot):
                par = slot % 2
                pe.wait_ge(xr_in[slot], 16 * m + 16)
                done(pe, "xrT_low", k - 1)
                for c in range(DC):
                    last = pe.transpose(PS[:, par, c * P:(c + 1) * P], XR[:, slot, c * P:(c + 1) * P], ident)
                inc(last, "xrT_ready")

            def product(out, xh, xl, w, at, step, n):
                for c in range(DC):
                    high, low = (w[:, at + c * step[0] + part * step[1]:at + c * step[0] + part * step[1] + n]
                                 for part in range(2))
                    for x, y in ((xh, high), (xh, low), (xl, high)):
                        pe.matmul(out, lhsT=x(c), rhs=y, start=(c == 0 and x is xh and y is high), stop=False)

            b1f, b2f = (x.rearrange("k e n -> k (e n)") for x in (b1h, b2h))

            def block_values(k):
                both = pe.value_load(tabW[0:1, ds(k, 1)], min_val=0, max_val=(WRING - 1) * EW * E + E - 1)
                return both & (E - 1), products[:, ds(both // E, EW)]

            def hidden(k, par, values):
                e, w = values
                pe.wait_ge(w_in, e * (16 * WPIECES) + (16 * WPIECES + 16))
                done(pe, "gate_lin_ready", k - 1)
                done(pe, "xrT_low", k + 1)
                product(PS[:, 2 + par, :], lambda c: XRT[:, par, 0, c, :], lambda c: XRT[:, par, 1, c, :],
                        w, 0, (4 * INNER, 2 * INNER), 2 * INNER)
                bias = b1f[:, ds(e * 512, 512)].rearrange("k (f two) -> k two f", two=2)
                inc(pe.matmul(PS[:, 2 + par, :], lhsT=onesB[0:3, :], rhs=bias, start=False, stop=True), "hid_ready")

            def turn_s(k, par):
                done(pe, "s_ready", k + 1)
                done(pe, "sT_low", k - 1)
                for c in range(2):
                    last = pe.transpose(PS[:, 4 + par, c * P:(c + 1) * P], sS[:, par, c * P:(c + 1) * P], ident)
                inc(last, "sT_ready")

            def expert_out(k, par, values):
                e, w = values
                done(pe, "sT_low", k + 1)
                done(pe, "y_scaled", k - 1)
                product(PS[:, 6 + par, 0:D], lambda c: sTh[:, par, c, :], lambda c: sTl[:, par, c, :],
                        w, 8 * INNER, (D, 2 * INNER), D)
                inc(pe.matmul(PS[:, 6 + par, 0:D], lhsT=onesB[0:3, :], rhs=b2f[:, ds(e * D, D)],
                              start=False, stop=True), "y_ready")

            def block_step(k, m, j, inner, values):
                if inner or k + 2 < NBLK:
                    turn_rows(k + 2, m + (j + 2) // RING, (j + 2) % RING)
                if inner or k + 1 < NBLK:
                    if j == 0:
                        values[1] = block_values(k + 1)
                    hidden(k + 1, (j + 1) % 2, values[j + 1])
                if j + 2 <= 2 * RING and (inner or k + 2 < NBLK):
                    values[j + 2] = block_values(k + 2)
                turn_s(k, j % 2)
                if j <= 1 and (inner or k >= 1):
                    values[j - 1] = block_values(k - 1)
                if inner or k >= 1:
                    expert_out(k - 1, (j + 1) % 2, values[j - 1])

            def round_of_blocks(k, m, inner):
                values = {}
                for j in range(2 * RING):
                    block_step(k + j, m, j, inner, values)

            turn_rows(0, 0, 0)
            turn_rows(1, 0, 1)
            hidden(0, 0, block_values(0))
            round_of_blocks(0, 0, False)
            with pe.Fori(1, NBLK // (2 * RING) - 1) as m:
                round_of_blocks(2 * RING * m, 2 * m, True)
            round_of_blocks(NBLK - 2 * RING, NBLK // RING - 2, False)
            expert_out(NBLK - 1, 1, block_values(NBLK - 1))

        @block.scalar
        def _(act):
            for n in ("xT_copied", "mcur_copied", "exp_done", "relu_done", "v_copied", "kT_copied", "attnT_copied",
                      "gate_exp", "xnT_copied", "h_ready", "sum_normed", "q2_kept", "states_stored", "q_stored", "top_exp", "xrT_copied", "sT_copied", "sig_ready", "y_scaled"):
                act.sem_inc(S[n], CREDIT)
            act.sem_inc(seeded, 1)
            act.wait_ge(seeded, 5)

            def root(asked, n):
                act.wait_ge(sqrt_asked, asked)
                nc.scalar.activation(sqS[:, 0:n], tmpS[:, 0:n], ACT.Sqrt).then_inc(sqrt_done, 1)

            root(1, NTT)
            root(2, NTT)

            with act.Fori(0, B) as b:
                def enter(s, par):
                    t = b * NT + s
                    done(act, "front_T_ready", t + 1)
                    done(act, "vu_ready", t - 1)
                    inc(nc.scalar.copy(XT[:, par], PS[:, 2, 0:D].rearrange("p (c t) -> p c t", c=DC)), "xT_copied")
                    done(act, "score_taken", t - 1)
                    inc(nc.scalar.copy(MC[:, par], PS[:, 2, D:2 * D]), "mcur_copied")

                def step(s, par, inner=False):
                    n, f, k, w = parts(s, inner)
                    t = b * NT + s
                    if f:
                        done(act, "proj_ready", t + 1)
                        done(act, "feat_ready", t - 1)
                        met(act)
                        r = RR[:, ds(t, 1)]
                        inc(nc.scalar.activation(EX[:, par], PS[:, 4, :], ACT.Exp, scale=r), "exp_done")
                        inc(nc.scalar.activation(RL[:, par], PS[:, 4, :], ACT.Relu, scale=r), "relu_done")
                        done(act, "vu_ready", t + 1)
                        done(act, "score_taken", t + 1)
                        done(act, "attn_ready", t - 1)
                        met(act)
                        inc(nc.scalar.activation(V1[:, par, :, 0:DK], PS[:, 5, 0:D].rearrange("p (h v) -> p h v", h=H),
                                                 ACT.Copy, scale=r), "v_copied")
                    if n:
                        enter(s + 1, 1 - par)
                    if f:
                        done(act, "qkT_ready", t + 1)
                        done(act, "scores_ready", t - 1)
                        done(act, "attn_ready", t - 1)
                        inc(nc.scalar.copy(KT[:, par], PS[:, 1, :].rearrange("p (g t) -> p g t", g=G)), "kT_copied")
                        if k:
                            done(act, "attnT_ready", t)
                        inc(nc.scalar.copy(Q2[:, par], PS[:, 3, D:2 * D].rearrange("p (c t) -> p c t", c=2)), "q2_kept")
                    if k:
                        done(act, "attnT_ready", t)
                        done(act, "state1_kept", t)
                        done(act, "wo_ready", t - 2)
                        inc(nc.scalar.copy(ANT[:, 1 - par], PS[:, 3, 0:D].rearrange("p (c t) -> p c t", c=DC)),
                            "attnT_copied")
                        met(act)
                        inc(nc.scalar.copy(arena[:, ds((s - 1) * (2 * SW) + 4096, 2 * SW)],
                                           SX[:, 2 - 2 * par:4 - 2 * par].rearrange("p s c w -> p (s c w)")),
                            "states_stored")
                    if f:
                        done(act, "q2_kept", t + 1)
                        met(act)
                        inc(nc.scalar.copy(arena[:, ds(s * D, D)], Q2[:, par].rearrange("p c t -> p (c t)")),
                            "q_stored")

                act.wait_ge(biasd, 16)
                enter(0, 0)
                steps(act, step)
                done(act, "gate_arg", b + 1)
                inc(nc.scalar.activation(SC[:], SC[:], ACT.Exp), "gate_exp")

                def scaled(i, dst, src):
                    return nc.scalar.activation(dst, src, ACT.Identity, scale=RS2[:, i:i + 1], bias=NM[:, i:i + 1])

                for q in range(NQ):
                    n = b * NQ + q
                    tiles = range(QT4 * q, QT4 * q + QT4)
                    root(3 * n + 3, QT4)
                    done(act, "sum_asked", n + 1)
                    met(act)
                    for i in tiles:
                        inc(scaled(i, XO[:, i, :], XO[:, i, :]), "sum_normed")
                    root(3 * n + 4, QT4)
                    root(3 * n + 5, QT4)
                    done(act, "roots_ready", n + 1)
                    act.wait_ge(h_out, 16 * n + 16)
                    done(act, "xn_ready", b * NT + QT4 * q)
                    met(act)
                    for i in tiles:
                        inc(scaled(i, HN[:, i % QT4], X2[:, ds(b * NT + i, 1), :].rearrange("p o d -> p (o d)")), "h_ready")
                    for pair in range(2):
                        done(act, "xnT_ready", 2 * n + pair + 1)
                        done(act, "logit_ready", 2 * n)
                        inc(nc.scalar.copy(XNT[:, 2 * pair:2 * pair + 2].rearrange("p i c t -> p (i c t)"),
                                           PS[:, 6 + pair, :]), "xnT_copied")
                    done(act, "top_arg", n + 1)
                    inc(nc.scalar.activation(TV[:], TV[:], ACT.Exp), "top_exp")
                act.wait_ge(h_out, 16 * NQ * (b + 1) + 16)
                met(act)

            act.wait_ge(table_ready, 1)
            act.wait_ge(small_in, 64)
            store_fill(act, E // 2, E)


            def copy_rows(k, par):
                done(act, "xrT_ready", k + 1)
                done(act, "hid_ready", k - 1)
                inc(nc.scalar.copy(XRT[:, par, 0], PS[:, par, 0:D].rearrange("p (c t) -> p c t", c=DC)), "xrT_copied")

            def copy_s(k, par):
                done(act, "sT_ready", k + 1)
                done(act, "y_ready", k - 1)
                inc(nc.scalar.copy(sTh[:, par], PS[:, 4 + par, 0:D].rearrange("p (c t) -> p c t", c=DC)), "sT_copied")

            def sigmoid(k, par):
                done(act, "lin_ready", k + 1)
                done(act, "s_ready", k - 1)
                inc(nc.scalar.activation(hS[:, par], hA[:, par], ACT.Sigmoid, scale=ALPHA), "sig_ready")

            def scale_out(k, slot):
                par = slot % 2
                both = act.value_load(tabA[0:1, ds(k, 1)], min_val=0, max_val=E * CAP * E + E - 1)
                e = both & (E - 1)
                done(act, "y_ready", k + 1)
                done(act, "sum_added", k - 1)
                met(act)
                inc(nc.scalar.activation(YS[:, par], PS[:, 6 + par, 0:D], ACT.Copy,
                                         scale=XR[:, slot, ds(e + D, 1)]), "y_scaled")
                return both // E

            def block_step(k, j, inner=False):
                if inner or k + 2 < NBLK:
                    copy_rows(k + 2, j % 2)
                if inner or k + 1 < NBLK:
                    sigmoid(k + 1, (j + 1) % 2)
                copy_s(k, j % 2)
                if inner or k >= 1:
                    row = scale_out(k - 1, (j - 1) % RING)
                if inner or 3 <= k < NBLK + 3 - RING:
                    done(act, "sum_added", k - 2)
                    slot = (j - 3) % RING
                    act.dma_start(XR[:, slot], lists[ds(row, P), :]).then_inc(xr_in[slot], 16)

            copy_rows(0, 0)
            copy_rows(1, 1)
            sigmoid(0, 0)
            for j in range(RING):
                block_step(j, j)
            with act.Fori(1, NBLK // RING - 1) as m:
                for j in range(RING):
                    block_step(RING * m + j, j, True)
            for j in range(RING):
                block_step(NBLK - RING + j, j)
            scale_out(NBLK - 1, RING - 1)
            for k in range(4):
                at = slice(8 * k, 8 * k + 8)
                act.wait_ge(sqrt_asked, 3 * B * NQ + 3 + k)
                nc.scalar.activation(sqS[:, at], tmpS[:, at], ACT.Sqrt).then_inc(sqrt_done, 1)
                act.wait_ge(final_asked, k + 1)
                for t in range(8 * k, 8 * k + 8):
                    nc.scalar.activation(FS[:, t], FS[:, t], ACT.Identity, scale=RS[:, t:t + 1],
                                         bias=NM[:, t:t + 1]).then_inc(final_normed, 1)

        @block.vector
        def _(v):
            order = [0]

            def own(ins):
                order[0] += 1
                ins.then_inc(dve, 1)
                v.wait_ge(dve, order[0])

            for n in ("raw_score_read", "xs0_ready", "mean_copied", "vm_copied", "xs_ready", "score_taken", "feat_ready", "qT_copied",
                      "state0_kept", "state1_kept", "masked", "attn_normed", "xo_done", "gate_arg", "gates_ready",
                      "z_used", "combined", "xn_ready", "sum_asked", "roots_ready", "logit_used", "top_arg", "mask_ready", "routed",
                      "lin_ready", "gate_lin_ready", "s_ready", "sT_low", "xrT_low", "result_ready", "score_stored"):
                v.sem_inc(S[n], CREDIT)
            v.sem_inc(h_out, 16)
            v.sem_inc(w_in, 16)
            v.sem_inc(split_out, 16)
            v.sem_inc(seeded, 1)
            v.memset(zeros[:], 0.0).then_inc(prep, 1)
            v.memset(PF[:], 0.0).then_inc(prep, 1)
            v.memset(V1[:], 1.0).then_inc(prep, 1)
            v.memset(CNT[:], 0.0).then_inc(prep, 1)
            v.memset(onesB[:], 1.0).then_inc(prep, 1)
            v.memset(onesE[:], 1.0).then_inc(prep, 1)
            v.wait_ge(prep, 7)
            v.sem_inc(seeded, 1)
            v.wait_ge(seeded, 5)
            v.wait_ge(const_in_s, 16)
            v.tensor_copy(beforeB[:], const[:, C_BEFORE:C_BEFORE + P]).then_inc(prep, 1)
            v.tensor_copy(TOKI[:], const[:, C_TOK:C_TOK + NTT]).then_inc(prep, 1)
            v.wait_ge(weights_in, 96)
            for k in range(5):
                v.wait_ge(wt_ready, k + 1)
                for c in range(DC):
                    src = PS[:, k, c * D:(c + 1) * D]
                    if k < 3:
                        ins = v.tensor_scalar(WT[:, c, k * D:(k + 1) * D], src, nw[:, c:c + 1], None, ALU.mult)
                    elif k == 3:
                        ins = v.tensor_copy(WoT[:, c, :], src)
                    else:
                        ins = v.tensor_copy(WT[:, c, 3 * D:4 * D], src)
                    ins.then_inc(wt_copied, 1)
            v.wait_ge(x_in_s, 16 * B)

            def aggregate(dst, n, q, count):
                v.wait_ge(q, count)
                met(v)
                for i in range(n):
                    last = v.bn_aggr(dst[:, i, :], ST[:, i, :])
                return last

            def tile(x, i):
                return x[:, ds(i, 1), :].rearrange("p o d -> p (o d)")

            with v.Fori(0, NTT // 8) as m:
                for k in range(8):
                    v.bn_stats(tile(ST, 8 * m + k), tile(X2, 8 * m + k)).then_inc(ord3, 1)
            own(aggregate(MV, NTT, ord3, NTT))

            asked = [0]

            def inverse_root(dst, n, arg, base=None):
                asked[0] += 1
                at = asked[0] if base is None else base
                arg.then_inc(sqrt_asked, 1)
                v.wait_ge(sqrt_done, at)
                own(v.reciprocal(dst, sqS[:, 0:n]))

            inverse_root(RS[:], NTT, v.tensor_scalar(tmpS[:], MV[:, :, 1], LN_EPS, None, ALU.add))
            own(v.tensor_tensor(tmpS[:], RS[:], RS[:], ALU.mult))
            own(v.tensor_tensor(tmpS[:], tmpS[:], MV[:, :, 1], ALU.mult))
            inverse_root(RR[:], NTT, v.tensor_scalar(tmpS[:], tmpS[:], ATT_RMS_EPS, None, ALU.add))
            v.wait_ge(bias_in, 32)
            b12 = [(b1s[:], slice(0, 2 * INNER)), (b2s[:], slice(2 * INNER, 3 * INNER))]
            for src, cols in b12:
                own(v.tensor_copy(bh[:, 0, cols], src))
                own(v.tensor_tensor(bres[:, 0, cols], src, bh[:, 0, cols], ALU.subtract))
                own(v.tensor_copy(bh[:, 1, cols], bres[:, 0, cols]))
                own(v.tensor_tensor(bres[:, 1, cols], bres[:, 0, cols], bh[:, 1, cols], ALU.subtract))
                own(v.tensor_copy(bh[:, 2, cols], bres[:, 1, cols]))
            v.sem_inc(biasq, 5)
            with v.Fori(0, B) as b:
                local = [0]

                def own_b(ins, wait=True):
                    local[0] += 1
                    ins.then_inc(ordB, 1)
                    if wait:
                        v.wait_ge(ordB, b * PER_BATCH + local[0])

                def root_b(dst, n, arg, k):
                    arg.then_inc(sqrt_asked, 1)
                    v.wait_ge(sqrt_done, 3 * NQ * b + 3 + k)
                    own_b(v.reciprocal(dst, sqS[:, 0:n]))

                for i in range(NT):
                    t = b * NT + i
                    inc(v.tensor_scalar(XO[:, i, :], tile(X2, t), MV[:, ds(t, 1), 0:1].rearrange("p o d -> p (o d)"),
                                        RS[:, ds(t, 1)], ALU.subtract, ALU.mult), "xs0_ready")
                done(v, "mean_ready", b + 1)
                inc(v.tensor_copy(MT[:], PS[:, 0:DC, 0:NSEG]), "mean_copied")
                done(v, "vm_ready", b + 1)
                inc(v.tensor_copy(VM[:], PS[:, 2, 0:DC * NSEG].rearrange("p (c n) -> p c n", c=DC)), "vm_copied")
                done(v, "attn_ready", b * NT)
                done(v, "states_stored", b * NT)
                own_b(v.memset(SX[:, 3], 0.0))

                def enter(s, par):
                    done(v, "front_T_ready", b * NT + s - 1)
                    inc(v.tensor_copy(XS[:, par], tile(XO, s)), "xs_ready")

                def step(s, par, inner=False):
                    n, f, k, w = parts(s, inner)
                    t = b * NT + s
                    q = 1 - par
                    heads = const[:, C_HEADS:C_HEADS + HG * HV].unsqueeze(1).broadcast_to([P, 2, HG * HV])
                    state = PS[:, 7, 0:SW].rearrange("p (c w) -> p c w", c=2)
                    if f:
                        done(v, "raw_score_ready", t + 1)
                        inc(v.tensor_copy(SCS[:, par, 0:NSEG], PS[:, 6, 272:272 + NSEG]), "raw_score_read")
                    if k:
                        done(v, "state0_ready", t)
                        done(v, "states_stored", t - 2)
                        done(v, "attn_ready", t - 1)
                        inc(v.tensor_tensor(SX[:, 2 * q], state, heads, ALU.mult), "state0_kept")
                    if n:
                        enter(s + 1, q)
                    if f:
                        done(v, "relu_done", t + 1)
                        done(v, "qkT_ready", t - 1)
                        done(v, "state1_ready", t - 1)
                        ex, rl = (x[:, par].rearrange("p (h w) -> p h w", w=DK) for x in (EX, RL))
                        v.scalar_tensor_tensor(F2[:, par].rearrange("p k w -> p (k w)"), EX[:, par], 1.0, RL[:, par],
                                               ALU.min, ALU.add)
                        inc(v.scalar_tensor_tensor(PF[:, par].rearrange("p k h w -> p (k h) w")[:, :, 0:DK], ex, 1.0,
                                                   rl, ALU.min, ALU.add), "feat_ready")
                    if k:
                        done(v, "scores_ready", t)
                        causal = const[:, C_CAUSAL:C_CAUSAL + SEG].unsqueeze(1).broadcast_to([P, G * G, SEG])
                        inc(v.tensor_tensor(AM[:, q], PS[:, 0:G, 0:G * SEG].rearrange("p j (g c) -> p j g c", g=G),
                                            causal.rearrange("p (j g) c -> p j g c", j=G), ALU.mult), "masked")
                        done(v, "state1_ready", t)
                        inc(v.tensor_tensor(SX[:, 2 * q + 1], state, heads, ALU.mult), "state1_kept")
                    if f:
                        done(v, "vu_ready", t + 1)
                        done(v, "mcur_copied", t + 1)
                        inc(v.tensor_tensor_reduce(MC[:, par], PS[:, 5, D:2 * D], MC[:, par], 1.0, 0.0, ALU.mult,
                                                   ALU.add, SCS[:, par, NSEG:NSEG + 1]), "score_taken")
                    if w:
                        done(v, "wo_ready", t - 1)
                        xo = tile(XO, s - 2)
                        inc(v.tensor_tensor(xo, PS[:, 4, 0:D], xo, ALU.add), "xo_done")
                    if k:
                        done(v, "attn_ready", t)
                        o = PS[:, 6, 0:H * HV].rearrange("p (h c) -> p h c", h=H)
                        v.tensor_scalar(rden[:, q], o[:, :, DK], DEN_EPS, None, ALU.add).then_inc(ordD, 1)
                        v.wait_ge(ordD, 2 * t - 1)
                        v.reciprocal(rden[:, q], rden[:, q]).then_inc(ordD, 1)
                        v.wait_ge(ordD, 2 * t)
                        done(v, "attnT_ready", t - 2)
                        inc(v.tensor_tensor(AN[:, q].rearrange("p (h v) -> p h v", h=H), o[:, :, 0:DK],
                                            rden[:, q].unsqueeze(2).broadcast_to([P, H, DK]), ALU.mult), "attn_normed")
                    if f:
                        done(v, "qkT_ready", t + 1)
                        inc(v.tensor_copy(QT[:, par], PS[:, 0, :].rearrange("p (g t) -> p g t", g=G)), "qT_copied")
                        done(v, "score_taken", t + 1)
                        inc(v.tensor_scalar(tile(SC, s), SCS[:, par], 1.0, None, ALU.mult), "score_stored")

                enter(0, 0)
                steps(v, step)

                done(v, "score_stored", (b + 1) * NT)
                flat = SC[:].rearrange("p i n -> p (i n)")
                own_b(v.scalar_tensor_tensor(flat, flat, 1.0 / 16.0, const[:, C_SCORE:C_BEFORE], ALU.mult, ALU.add))
                own_b(v.tensor_reduce(red[:], SC[:], AX_X, ALU.max))
                inc(v.tensor_tensor(SC[:], SC[:], red[:].unsqueeze(2).broadcast_to([P, NT, NSEG + 1]),
                                    ALU.subtract), "gate_arg")
                done(v, "gate_exp", b + 1)
                own_b(v.tensor_reduce(red[:], SC[:], AX_X, ALU.add))
                own_b(v.reciprocal(red[:], red[:]))
                inc(v.tensor_tensor(SC[:], SC[:], red[:].unsqueeze(2).broadcast_to([P, NT, NSEG + 1]),
                                    ALU.mult), "gates_ready")
                done(v, "gates_ready", b + 1)
                done(v, "xo_done", (b + 1) * NT)

                v.wait_ge(small_in, 64)
                stats = [0]

                def stat(i, src):
                    stats[0] += 1
                    met(v)
                    v.bn_stats(ST[:, i, :], src).then_inc(ord3, 1)

                def moments(q):
                    v.wait_ge(ord3, b * 2 * NT + NTT + stats[0])
                    met(v)
                    for i in range(QT4 * q, QT4 * q + QT4):
                        last = v.bn_aggr(MV2[:, i, :], ST[:, i, :])
                    own_b(last)

                def under(q, stage):
                    tiles = range(QT4 * q, QT4 * q + QT4)
                    cols = slice(QT4 * q, QT4 * q + QT4)
                    n = b * NQ + q
                    var, tmp = MV2[:, cols, 1], tmpS[:, 0:QT4]
                    if stage == 0:
                        moments(q)
                        v.tensor_scalar(tmp, var, LN_EPS, None, ALU.add).then_inc(sqrt_asked, 1)
                    elif stage == 1:
                        v.wait_ge(sqrt_done, 3 * n + 3)
                        own_b(v.reciprocal(RS2[:, cols], sqS[:, 0:QT4]))
                        inc(v.scalar_tensor_tensor(NM[:, cols], MV2[:, cols, 0], -1.0, RS2[:, cols], ALU.mult,
                                                   ALU.mult), "sum_asked")
                    elif stage == 2:
                        for i in tiles:
                            x2 = tile(X2, b * NT + i)
                            done(v, "sum_normed", b * NT + i + 1)
                            v.tensor_tensor(x2, x2, XO[:, i, :], ALU.add).then_inc(ord4, 1)
                        v.wait_ge(ord4, b * NT + QT4 * q + QT4)
                        for i in tiles:
                            stat(i, tile(X2, b * NT + i))
                        moments(q)
                        v.tensor_scalar(tmp, var, LN_EPS, None, ALU.add).then_inc(sqrt_asked, 1)
                    elif stage == 3:
                        v.wait_ge(sqrt_done, 3 * n + 4)
                        own_b(v.reciprocal(RS2[:, cols], sqS[:, 0:QT4]))
                        own_b(v.scalar_tensor_tensor(NM[:, cols], MV2[:, cols, 0], -1.0, RS2[:, cols], ALU.mult,
                                                     ALU.mult))
                        own_b(v.tensor_tensor(tmp, RS2[:, cols], RS2[:, cols], ALU.mult))
                        own_b(v.tensor_tensor(tmp, tmp, var, ALU.mult))
                        v.tensor_scalar(tmp, tmp, FFN_RMS_EPS, None, ALU.add).then_inc(sqrt_asked, 1)
                    elif stage == 4:
                        v.wait_ge(sqrt_done, 3 * n + 5)
                        own_b(v.reciprocal(RR2[:, cols], sqS[:, 0:QT4]))
                        v.sem_inc(S["roots_ready"], 1)
                    elif stage == 5:
                        done(v, "rows_sent", b)
                        for i in tiles:
                            done(v, "h_ready", b * NT + i + 1)
                            inc(v.scalar_tensor_tensor(RW[:, i, 0:D], HN[:, i % QT4], RR2[:, i:i + 1], nsB[:],
                                                       ALU.mult, ALU.mult), "xn_ready")
                    elif stage == 6:
                        for pair in range(2):
                            done(v, "logit_ready", 2 * n + pair + 1)
                            inc(v.tensor_tensor(LG[:, 2 * pair:2 * pair + 2],
                                                PS[:, 6 + pair, 0:2 * E].rearrange("p (i e) -> p i e", e=E),
                                                bgB[:].unsqueeze(1).broadcast_to([P, 2, E]), ALU.add), "logit_used")
                        done(v, "logit_used", 2 * n + 2)
                        met(v)
                        for k in range(QT4):
                            v.max(M8[:, k], LG[:, k]).then_inc(ord5, 1)
                        v.wait_ge(ord5, 2 * QT4 * n + QT4)
                        met(v)
                        for k in range(QT4):
                            v.max_index(I8[:, k], M8[:, k], LG[:, k]).then_inc(ord5, 1)
                        v.wait_ge(ord5, 2 * QT4 * n + 2 * QT4)
                        inc(v.tensor_tensor(TV[:], M8[:, :, 0:TOPK],
                                            M8[:, :, 0:1].broadcast_to([P, QT4, TOPK]), ALU.subtract), "top_arg")
                        own_b(v.tensor_copy(TI[:], I8[:, :, 0:TOPK]))
                        iota = const[:, C_IOTA:C_IOTA + E].unsqueeze(1).broadcast_to([P, QT4 * TOPK, E])
                        own_b(v.tensor_tensor(OH.rearrange("p i j e -> p (i j) e"),
                                              TI[:].rearrange("p i j -> p (i j)").unsqueeze(2).broadcast_to(
                                                  [P, QT4 * TOPK, E]), iota, ALU.is_equal))
                        own_b(v.tensor_reduce(MK[:], OH.rearrange("p i j e -> p i e j"), AX_X, ALU.add))
                        inc(v.tensor_copy(MKb[:], MK[:]), "mask_ready")
                    elif stage == 7:
                        red4 = red[:, 0:QT4]
                        done(v, "top_exp", n + 1)
                        own_b(v.tensor_reduce(red4, TV[:], AX_X, ALU.add))
                        own_b(v.reciprocal(red4, red4))
                        own_b(v.tensor_tensor(TV[:], TV[:], red4.unsqueeze(2).broadcast_to([P, QT4, TOPK]), ALU.mult))
                        tv = TV[:].rearrange("p i j -> p (i j)").unsqueeze(2).broadcast_to([P, QT4 * TOPK, E])
                        own_b(v.tensor_tensor(OT.rearrange("p i j e -> p (i j) e"), OH.rearrange("p i j e -> p (i j) e"),
                                              tv, ALU.mult))
                        own_b(v.tensor_reduce(RW[:, cols, D:D + E], OT.rearrange("p i j e -> p i e j"), AX_X, ALU.add))
                        own_b(v.tensor_scalar(RW[:, cols, IDCOL].bitcast(I32), TOKI[:, ds(b * NT + QT4 * q, QT4)], 1.0,
                                              None, ALU.mult), False)
                        done(v, "rank_ready", n + 1)
                        own_b(v.tensor_tensor(PR[:], PS[:, 6, 0:QT4 * E].rearrange("p (i e) -> p i e", e=E),
                                              CNT[:].unsqueeze(1).broadcast_to([P, QT4, E]), ALU.add))
                        own_b(v.tensor_tensor(PR[:], PR[:], const[:, C_BASE:C_BASE + E].unsqueeze(1).broadcast_to(
                            [P, QT4, E]), ALU.add), False)
                        own_b(v.tensor_tensor(CNT[:], CNT[:], PS[:, 7, 0:E], ALU.add))
                        own_b(v.tensor_tensor(OT, OH, PR[:].unsqueeze(2).broadcast_to([P, QT4, TOPK, E]), ALU.mult))
                        own_b(v.tensor_reduce(POSF[:], OT, AX_X, ALU.add))
                        inc(v.tensor_copy(POS[:, cols], POSF[:]), "routed")

                turn = 0
                for i in range(NT):
                    sums2 = [XO[:, i, :], AN[:, i % 2]]
                    last_in = [("order", local[0] + 1), None]
                    own_b(v.tensor_scalar(sums2[0], sums2[0], SC[:, i, NSEG:NSEG + 1], None, ALU.mult), False)
                    for k in range(TURNS[i]):
                        done(v, "z_ready", b * NTURN + turn + 1)
                        for n in range(SEGT * k, min(SEGT * (k + 1), 2 * i + 1)):
                            acc = sums2[n % 2].rearrange("p (c w) -> p c w", c=2)
                            if n != 1:
                                what, count = last_in[n % 2]
                                if what == "order":
                                    v.wait_ge(ordB, b * PER_BATCH + count)
                                else:
                                    done(v, "z_used", b * NTURN + count)
                            z = PS[:, 2 * (turn % 3):2 * (turn % 3) + 2, (n % SEGT) * P:(n % SEGT + 1) * P]
                            if n == 1:
                                ins = v.tensor_scalar(acc, z, SC[:, i, n:n + 1], None, ALU.mult)
                            else:
                                ins = v.scalar_tensor_tensor(acc, z, SC[:, i, n:n + 1], acc, ALU.mult, ALU.add)
                            if n < min(SEGT * (k + 1) - 1, 2 * i):
                                own_b(ins, False)
                                last_in[n % 2] = ("order", local[0])
                            else:
                                inc(ins, "z_used")
                                last_in[n % 2] = ("turn", turn + 1)
                        turn += 1
                        if i and k == 0:
                            v.wait_ge(ordB, b * PER_BATCH + complete)
                            stat(i - 1, XO[:, i - 1, :])
                        if i >= QT4 and k == (TURNS[i] - 1) // 2:
                            under(i // QT4 - 1, 2 * (i % QT4))
                    done(v, "z_used", b * NTURN + turn)
                    v.wait_ge(ordB, b * PER_BATCH + local[0])
                    if i:
                        own_b(v.tensor_tensor(sums2[0], sums2[0], sums2[1], ALU.add), False)
                    complete = local[0]
                    if i >= QT4:
                        under(i // QT4 - 1, 2 * (i % QT4) + 1)
                v.wait_ge(ordB, b * PER_BATCH + complete)
                stat(NT - 1, XO[:, NT - 1, :])
                v.sem_inc(S["combined"], 1)
                for stage in range(8):
                    under(NQ - 1, stage)
                assert local[0] == PER_BATCH, local[0]

            own(v.tensor_copy(ti32[:], CNT[:]))
            own(v.tensor_scalar(ti32[:], CNT[:], float(P - 1), None, ALU.add))
            own(v.tensor_scalar(ti32[:], ti32[:], 7, None, ALU.arith_shift_right))
            own(v.tensor_copy(nb[:], ti32[:]))
            own(v.tensor_scalar(nb[:], nb[:], 1.0, None, ALU.max))
            own(v.tensor_tensor_scan(cum[:], onesE[:], nb[:], 0.0, ALU.mult, ALU.add))
            own(v.tensor_copy(tabD[:], cum[0:1, :]))
            own(v.tensor_scalar(cum[:], cum[:], float(P), None, ALU.mult))
            blk = const[:, C_BLK:C_BLK + 2]
            cumB = cum[:].unsqueeze(1).broadcast_to([P, 2, E])
            own(v.tensor_tensor(cmp[:], cumB, blk.unsqueeze(2).broadcast_to([P, 2, E]), ALU.is_le))
            own(v.tensor_reduce(blkE[:], cmp[:], AX_X, ALU.add))
            own(v.tensor_tensor(cmq[:], cmp[:], const[:, C_SLOT:C_SLOT + E].unsqueeze(1).broadcast_to([P, 2, E]),
                                ALU.mult))
            own(v.tensor_reduce(blkW[:], cmq[:], AX_X, ALU.add))
            own(v.tensor_tensor(cmq[:], cmp[:], cumB, ALU.mult))
            own(v.tensor_reduce(blkC[:], cmq[:], AX_X, ALU.max))
            own(v.scalar_tensor_tensor(blkR[:], blkE[:], float(CAP), blkC[:], ALU.mult, ALU.subtract))
            own(v.tensor_tensor(blkR[:], blkR[:], blk, ALU.add))
            v.sem_inc(blocks_ready, 1)
            v.wait_ge(blocks_T_ready, 1)
            own(v.tensor_scalar(tabR[:], PS[0:1, 0, 0:NBLK], float(E * CAP), None, ALU.min))
            own(v.tensor_scalar(tabE[:], PS[0:1, 0, 2 * P:2 * P + NBLK], float(E - 1), None, ALU.min))
            own(v.tensor_copy(tabA, tabE[:]))
            own(v.scalar_tensor_tensor(tabA[:, 0:NBLK - AHEAD], tabR[:, AHEAD:], float(E), tabE[:, 0:NBLK - AHEAD],
                                       ALU.mult, ALU.add))
            own(v.scalar_tensor_tensor(tabW, PS[0:1, 1, 0:NBLK], float(E), tabE[:], ALU.mult, ALU.add))
            own(v.tensor_tensor(padF[:], CNT[0:1, :], const[0:1, C_BASE:C_BASE + E], ALU.add))
            own(v.tensor_copy(padR[:], padF[:]))
            v.sem_inc(table_ready, 1)

            v.wait_ge(h_out, 16 * (B * NQ + 1))
            def clip(k, par):
                done(v, "hid_ready", k + 1)
                done(v, "s_ready", k - 1)
                inc(v.tensor_scalar(hA[:, par], PS[:, 2 + par, 0:INNER], LIMIT, None, ALU.min), "lin_ready")
                inc(v.tensor_scalar(hB[:, par], PS[:, 2 + par, INNER:2 * INNER], LIMIT, -LIMIT, ALU.min, ALU.max),
                    "gate_lin_ready")

            def activate(k, par):
                done(v, "sT_ready", k - 1)
                done(v, "gate_lin_ready", k + 1)
                v.scalar_tensor_tensor(hB[:, par], hB[:, par], 1.0, hA[:, par], ALU.add, ALU.mult).then_inc(ordE, 1)
                v.wait_ge(ordE, k + 1)
                done(v, "sig_ready", k + 1)
                inc(v.tensor_tensor(sS[:, par], hB[:, par], hS[:, par], ALU.mult), "s_ready")

            def low_rows(k, par):
                done(v, "xrT_copied", k + 1)
                done(v, "hid_ready", k - 1)
                inc(v.tensor_tensor(XRT[:, par, 1], PS[:, par, 0:D].rearrange("p (c t) -> p c t", c=DC),
                                    XRT[:, par, 0].bitcast(F32), ALU.subtract), "xrT_low")

            def low_s(k, par):
                done(v, "sT_copied", k + 1)
                done(v, "y_ready", k - 1)
                inc(v.tensor_tensor(sTl[:, par], PS[:, 4 + par, 0:D].rearrange("p (c t) -> p c t", c=DC),
                                    sTh[:, par].bitcast(F32), ALU.subtract), "sT_low")

            low_rows(0, 0)
            low_rows(1, 1)
            clip(0, 0)
            activate(0, 0)

            def block_step(k, par):
                low_rows(k + 2, par)
                clip(k + 1, 1 - par)
                low_s(k, par)
                activate(k + 1, 1 - par)

            with v.Fori(0, NBLK // 8 - 1) as m:
                for j in range(8):
                    block_step(8 * m + j, j % 2)
            for k in range(NBLK - 8, NBLK - 2):
                block_step(k, k % 2)
            clip(NBLK - 1, 1)
            low_s(NBLK - 2, 0)
            activate(NBLK - 1, 1)
            low_s(NBLK - 1, 1)

            def add_x2(k):
                v.wait_ge(final_normed, 8 * (k + 1))
                for t in range(8 * k, 8 * k + 8):
                    inc(v.tensor_tensor(FS[:, t], FS[:, t], X2[:, t], ALU.add), "result_ready")

            for k in range(4):
                at = slice(8 * k, 8 * k + 8)
                v.wait_ge(sums_joined, k + 1)
                for t in range(8 * k, 8 * k + 8):
                    v.bn_stats(ST[:, t], FS[:, t]).then_inc(ord3, 1)
                v.wait_ge(ord3, NTT + 2 * B * NT + 8 * (k + 1))
                for t in range(8 * k, 8 * k + 8):
                    last = v.bn_aggr(MV[:, t, :], ST[:, t, :])
                own(last)
                v.tensor_scalar(tmpS[:, at], MV[:, at, 1], LN_EPS, None, ALU.add).then_inc(sqrt_asked, 1)
                if k:
                    add_x2(k - 1)
                v.wait_ge(sqrt_done, 3 * B * NQ + 3 + k)
                own(v.reciprocal(RS[:, at], sqS[:, at]))
                own(v.scalar_tensor_tensor(NM[:, at], MV[:, at, 0], -1.0, RS[:, at], ALU.mult, ALU.mult))
                v.sem_inc(final_asked, 1)
            add_x2(3)

        @block.gpsimd
        def _(pool):
            for n in ("rows_sent", "sum_added"):
                pool.sem_inc(S[n], CREDIT)
            pool.memset(RW[:], 0.0).then_inc(prep, 1)
            pool.sem_inc(split_made, 2)
            pool.sem_inc(seeded, 1)
            pool.wait_ge(seeded, 5)
            pool.wait_ge(prep, 9)
            with pool.Fori(0, B) as b:
                with pool.Fori(0, E // B) as e:
                    for j in range(3):
                        n = 3 * (b * (E // B) + e) + j
                        high, low = (halves[:, h].bitcast(F32R) for h in range(2))
                        piece = raw
                        if j < DC:
                            high, low = (x.rearrange("p (two f) -> p two f", two=2) for x in (high, low))
                            piece = raw.rearrange("p (f two) -> p two f", two=2)
                        pool.wait_ge(raw_in, 16 * n + 16)
                        pool.wait_ge(split_out, 16 * n + 16)
                        met(pool)
                        pool.tensor_copy(high, piece).then_inc(split_made, 1)
                        pool.wait_ge(split_made, 2 * n + 3)
                        met(pool)
                        pool.tensor_tensor(low, piece, high.bitcast(F32), ALU.subtract).then_inc(split_made, 1)
                for i in range(NT):
                    if i % QT4 == 0:
                        done(pool, "routed", b * NQ + i // QT4 + 1)
                        met(pool)
                    for j in range(TOPK):
                        pool.indirect_dma_start(
                            out=lists, out_offset=bass.IndirectOffsetOnAxis(ap=POS[:, i, j:j + 1], axis=0),
                            in_=RW[:, i], in_offset=None).then_inc(sc_out, 16)
                pool.wait_ge(sc_out, 16 * TOPK * NT * (b + 1))
                pool.sem_inc(S["rows_sent"], 1)
            pool.wait_ge(h_out, 16 * (B * NQ + 1))
            pool.wait_ge(pad_out, 16 * (E + 5))

            def add_block(m, slot, first=False):
                k = RING * m + slot
                done(pool, "y_scaled", k + 1)
                met(pool)
                pool.indirect_dma_start(
                    out=sums[slot % 2],
                    out_offset=bass.IndirectOffsetOnAxis(ap=XR[:, slot, IDCOL:IDCOL + 1].bitcast(I32), axis=0),
                    in_=YS[:, slot % 2], in_offset=None, compute_op=ALU.add).then_inc(added[slot % 2], 16)
                if not first:
                    pool.wait_ge(added[1 - slot % 2], 16 * (RING // 2) * m + 16 * ((slot + 1) // 2))
                    pool.sem_inc(S["sum_added"], 1)

            for slot in range(RING):
                add_block(0, slot, slot == 0)
            with pool.Fori(1, NBLK // RING) as m:
                for slot in range(RING):
                    add_block(m, slot)
            pool.wait_ge(added[1], 16 * (NBLK // 2))
            pool.sem_inc(S["sum_added"], 1)
            for k in range(4):
                pool.wait_ge(f_in[k], 32)
                at = slice(8 * k, 8 * k + 8)
                pool.tensor_tensor(FS[:, at], FS[:, at], FO[:, at], ALU.add).then_inc(sums_joined, 1)


def kernel(**inputs):
    import concourse.bacc as _bacc
    from concourse.bass_utils import run_bass_kernel_spmd as _run

    nc = _bacc.Bacc("TRN2", target_bir_lowering=False, num_devices=1)
    order = ["L0_attn_x", "L0_attn_norm_w", "L0_attn_Wq", "L0_attn_Wk", "L0_attn_Wv", "L0_attn_Wo", "L0_attn_Wu",
             "L0_ffn_norm_scale", "L0_ffn_wg", "L0_ffn_bg", "L0_ffn_w1", "L0_ffn_b1", "L0_ffn_w2", "L0_ffn_b2"]
    arrays, args = {}, []
    c, fill = constants()
    for name, a in [(n, inputs[n]) for n in order] + [("consts", c), ("fill_rows", fill)]:
        a = np.ascontiguousarray(a)
        arrays[f"in_{name}"] = a
        args.append(nc.dram_tensor(f"in_{name}", a.shape, mybir.dt.from_np(a.dtype), kind="ExternalInput").ap())
    out = nc.dram_tensor("out", (B, T, D), F32, kind="ExternalOutput").ap()
    lists = nc.dram_tensor("lists", (E * CAP + P, ROW), F32, kind="Internal").ap()
    sums = [nc.dram_tensor(f"sums_{which}", (B * T + P, D), F32, kind="Internal").ap() for which in ("even", "odd")]
    split = nc.dram_tensor("split_weights", (E, P, EW), F32, kind="Internal").ap()
    parts = nc.dram_tensor("bias_parts", (3, E, 3 * INNER), BF16, kind="Internal").ap()
    program(nc, *args, out, lists, sums, parts, split)
    return _run(nc, [arrays], core_ids=[0]).results[0]["out"]
```
